# Optimizing a Trainium2 kernel written in Bass

```python
import numpy as np
import jax
import jax.numpy as jnp

def _softmax(x, axis=-1):
    return jax.nn.softmax(x, axis=axis)

def _gelu(x):
    return jax.nn.gelu(x, approximate=True)

def _silu(x):
    return jax.nn.silu(x)

def _sigmoid(x):
    return jax.nn.sigmoid(x)

def _layernorm(x, axis=-1, eps=1e-05):
    m = jnp.mean(x, axis=axis, keepdims=True)
    v = jnp.var(x, axis=axis, keepdims=True)
    return (x - m) / jnp.sqrt(v + eps)

def _scatter_add(tgt, idx, src, axis=0):
    return tgt.at[idx].add(src)

def _segment_sum(src, seg, n):
    return jax.ops.segment_sum(src, seg, n)
kernel_name = 'mk_prb_d2_jaxref_r8_8cc7d2'

def setup_inputs(seed: int=0):
    np.random.seed(seed)
    _w = jnp.asarray

    def _L0_attn_setup():
        import jax, jax.numpy as jnp
        import numpy as np
        NUM_HEADS = 16
        key = jax.random.key(seed)
        k1, k2, k3 = jax.random.split(key, 3)
        B, D, N = (2, 256, 128)
        x = jax.random.normal(k1, (B, D, N), dtype=jnp.float32)
        W_qkv = jax.random.normal(k2, (N, 3 * N), dtype=jnp.float32) * (1.0 / np.sqrt(N))
        b_qkv = jax.random.normal(k3, (3 * N,), dtype=jnp.float32) * 0.01
        return {'x': x, 'W_qkv': W_qkv, 'b_qkv': b_qkv}
    _L0_attn_in = _L0_attn_setup()

    def _L0_ffn_setup():
        import jax, jax.numpy as jnp
        import numpy as np
        D_MODEL = 128
        D_FF = 512
        NUM_M = 2
        E_ROUTER = 8 * NUM_M - 1
        D_FF_R = D_FF // NUM_M
        TOP_K = NUM_M * 2 - 1
        B, T = (2, 256)

        def _expert_stack(x, W1, b1, W2, b2):
            h = jax.nn.gelu(jnp.einsum('btd,edf->ebtf', x, W1) + b1[:, None, None, :], approximate=False)
            return jnp.einsum('ebtf,efd->ebtd', h, W2) + b2[:, None, None, :]
        key = jax.random.key(seed)
        ks = jax.random.split(key, 12)
        s = lambda fan_in: 1.0 / np.sqrt(fan_in)
        x = jax.random.normal(ks[0], (B, T, D_MODEL), dtype=jnp.float32)
        sW1 = jax.random.uniform(ks[1], (1, D_MODEL, D_FF), jnp.float32, -s(D_MODEL), s(D_MODEL))
        sb1 = jax.random.uniform(ks[2], (1, D_FF), jnp.float32, -s(D_MODEL), s(D_MODEL))
        sW2 = jax.random.uniform(ks[3], (1, D_FF, D_MODEL), jnp.float32, -s(D_FF), s(D_FF))
        sb2 = jax.random.uniform(ks[4], (1, D_MODEL), jnp.float32, -s(D_FF), s(D_FF))
        rW1 = jax.random.uniform(ks[5], (E_ROUTER, D_MODEL, D_FF_R), jnp.float32, -s(D_MODEL), s(D_MODEL))
        rb1 = jax.random.uniform(ks[6], (E_ROUTER, D_FF_R), jnp.float32, -s(D_MODEL), s(D_MODEL))
        rW2 = jax.random.uniform(ks[7], (E_ROUTER, D_FF_R, D_MODEL), jnp.float32, -s(D_FF_R), s(D_FF_R))
        rb2 = jax.random.uniform(ks[8], (E_ROUTER, D_MODEL), jnp.float32, -s(D_FF_R), s(D_FF_R))
        gW = jax.random.uniform(ks[9], (D_MODEL, E_ROUTER), jnp.float32, -s(D_MODEL), s(D_MODEL))
        gb = jax.random.uniform(ks[10], (E_ROUTER,), jnp.float32, -s(D_MODEL), s(D_MODEL))
        return {'x': x, 'sW1': sW1, 'sb1': sb1, 'sW2': sW2, 'sb2': sb2, 'rW1': rW1, 'rb1': rb1, 'rW2': rW2, 'rb2': rb2, 'gW': gW, 'gb': gb}
    _L0_ffn_in = _L0_ffn_setup()

    def _L1_attn_setup():
        import jax, jax.numpy as jnp
        import numpy as np
        from jax import lax
        D_MODEL = 128
        D_INNER = 256
        D_STATE = 16
        DT_RANK = 128
        K = 4
        EPS = 1e-05

        def _layer_norm(x, w, b):
            mu = jnp.mean(x, axis=-1, keepdims=True)
            var = jnp.mean(jnp.square(x - mu), axis=-1, keepdims=True)
            return (x - mu) * lax.rsqrt(var + EPS) * w + b

        def _causal_depthwise_conv(x, w, b):
            L = x.shape[1]
            xp = jnp.pad(x, ((0, 0), (K - 1, 0), (0, 0)))
            out = b
            for k in range(K):
                out = out + w[:, k] * xp[:, k:k + L, :]
            return out

        def _selective_scan(u, delta, A, B, C, D):
            deltaA = jnp.exp(jnp.einsum('bld,dn->bldn', delta, A))
            deltaBu = jnp.einsum('bld,bln,bld->bldn', delta, B, u)
            bsz, _, d, n = deltaA.shape

            def step(h, inp):
                dA, dBu, Ct = inp
                h = dA * h + dBu
                y = jnp.einsum('bdn,bn->bd', h, Ct)
                return (h, y)
            h0 = jnp.zeros((bsz, d, n), u.dtype)
            _, ys = lax.scan(step, h0, (deltaA.transpose(1, 0, 2, 3), deltaBu.transpose(1, 0, 2, 3), C.transpose(1, 0, 2)))
            y = ys.transpose(1, 0, 2)
            return y + u * D
        key = jax.random.key(seed)
        ks = jax.random.split(key, 12)
        x = jax.random.normal(ks[0], (2, 128, D_MODEL), dtype=jnp.float32)
        norm_w = jnp.ones((D_MODEL,), jnp.float32)
        norm_b = jnp.zeros((D_MODEL,), jnp.float32)
        in_proj_w = jax.random.normal(ks[1], (D_MODEL, 2 * D_INNER), jnp.float32) * D_MODEL ** (-0.5)
        conv_w = jax.random.normal(ks[2], (D_INNER, K), jnp.float32) * K ** (-0.5)
        conv_b = jnp.zeros((D_INNER,), jnp.float32)
        x_proj_w = jax.random.normal(ks[3], (D_INNER, DT_RANK + 2 * D_STATE), jnp.float32) * D_INNER ** (-0.5)
        dt_init_std = DT_RANK ** (-0.5)
        dt_proj_w = jax.random.uniform(ks[4], (DT_RANK, D_INNER), jnp.float32, -dt_init_std, dt_init_std)
        dt = jnp.exp(jax.random.uniform(ks[5], (D_INNER,), jnp.float32) * (np.log(0.1) - np.log(0.001)) + np.log(0.001))
        dt_proj_b = dt + jnp.log(-jnp.expm1(-dt))
        A_log = jax.random.normal(ks[6], (D_INNER, D_STATE), jnp.float32)
        D_param = jax.random.normal(ks[7], (D_INNER,), jnp.float32)
        out_proj_w = jax.random.normal(ks[8], (D_INNER, D_MODEL), jnp.float32) * D_INNER ** (-0.5)
        return dict(x=x, norm_w=norm_w, norm_b=norm_b, in_proj_w=in_proj_w, conv_w=conv_w, conv_b=conv_b, x_proj_w=x_proj_w, dt_proj_w=dt_proj_w, dt_proj_b=dt_proj_b, A_log=A_log, D_param=D_param, out_proj_w=out_proj_w)
    _L1_attn_in = _L1_attn_setup()

    def _L1_ffn_setup():
        import jax, jax.numpy as jnp
        import numpy as np
        E = 16
        H = 128
        F = 256
        TOP_K = 1
        B, S = (2, 128)
        key = jax.random.key(seed)
        ks = jax.random.split(key, 7)
        s = 0.02
        return {'hidden_states': jax.random.normal(ks[0], (B, S, H), jnp.float32), 'w_router': jax.random.normal(ks[1], (E, H), jnp.float32) * s, 'gate_up_proj': jax.random.normal(ks[2], (E, H, 2 * F), jnp.float32) * s, 'down_proj': jax.random.normal(ks[3], (E, F, H), jnp.float32) * s, 'w_gate': jax.random.normal(ks[4], (F, H), jnp.float32) * s, 'w_up': jax.random.normal(ks[5], (F, H), jnp.float32) * s, 'w_down': jax.random.normal(ks[6], (H, F), jnp.float32) * s}
    _L1_ffn_in = _L1_ffn_setup()
    _d = {'L0_attn_x': _L0_attn_in['x'], 'L0_attn_W_qkv': _L0_attn_in['W_qkv'], 'L0_attn_b_qkv': _L0_attn_in['b_qkv'], 'L0_ffn_sW1': _L0_ffn_in['sW1'], 'L0_ffn_sb1': _L0_ffn_in['sb1'], 'L0_ffn_sW2': _L0_ffn_in['sW2'], 'L0_ffn_sb2': _L0_ffn_in['sb2'], 'L0_ffn_rW1': _L0_ffn_in['rW1'], 'L0_ffn_rb1': _L0_ffn_in['rb1'], 'L0_ffn_rW2': _L0_ffn_in['rW2'], 'L0_ffn_rb2': _L0_ffn_in['rb2'], 'L0_ffn_gW': _L0_ffn_in['gW'], 'L0_ffn_gb': _L0_ffn_in['gb'], 'L1_attn_norm_w': _L1_attn_in['norm_w'], 'L1_attn_norm_b': _L1_attn_in['norm_b'], 'L1_attn_in_proj_w': _L1_attn_in['in_proj_w'], 'L1_attn_conv_w': _L1_attn_in['conv_w'], 'L1_attn_conv_b': _L1_attn_in['conv_b'], 'L1_attn_x_proj_w': _L1_attn_in['x_proj_w'], 'L1_attn_dt_proj_w': _L1_attn_in['dt_proj_w'], 'L1_attn_dt_proj_b': _L1_attn_in['dt_proj_b'], 'L1_attn_A_log': _L1_attn_in['A_log'], 'L1_attn_D_param': _L1_attn_in['D_param'], 'L1_attn_out_proj_w': _L1_attn_in['out_proj_w'], 'L1_ffn_w_router': _L1_ffn_in['w_router'], 'L1_ffn_gate_up_proj': _L1_ffn_in['gate_up_proj'], 'L1_ffn_down_proj': _L1_ffn_in['down_proj'], 'L1_ffn_w_gate': _L1_ffn_in['w_gate'], 'L1_ffn_w_up': _L1_ffn_in['w_up'], 'L1_ffn_w_down': _L1_ffn_in['w_down']}
    _x0 = _d['L0_attn_x']
    _d['L0_attn_x'] = jax.random.normal(jax.random.fold_in(jax.random.key(seed), 1), (8, 512, 128), dtype=_x0.dtype)
    del _x0
    return _d

def reference(L0_attn_x, L0_attn_W_qkv, L0_attn_b_qkv, L0_ffn_sW1, L0_ffn_sb1, L0_ffn_sW2, L0_ffn_sb2, L0_ffn_rW1, L0_ffn_rb1, L0_ffn_rW2, L0_ffn_rb2, L0_ffn_gW, L0_ffn_gb, L1_attn_norm_w, L1_attn_norm_b, L1_attn_in_proj_w, L1_attn_conv_w, L1_attn_conv_b, L1_attn_x_proj_w, L1_attn_dt_proj_w, L1_attn_dt_proj_b, L1_attn_A_log, L1_attn_D_param, L1_attn_out_proj_w, L1_ffn_w_router, L1_ffn_gate_up_proj, L1_ffn_down_proj, L1_ffn_w_gate, L1_ffn_w_up, L1_ffn_w_down):

    def _L0_attn_ref(x, W_qkv, b_qkv):
        import jax, jax.numpy as jnp
        import numpy as np
        NUM_HEADS = 16
        B, D, N = x.shape
        H = NUM_HEADS
        p = N // H
        qkv = (x @ W_qkv + b_qkv).reshape(B, D, 3, H, p).transpose(2, 0, 3, 1, 4)
        q, k, v = (qkv[0], qkv[1], qkv[2])
        scores = jax.nn.softmax(jnp.einsum('bhip,bhjp->bhij', q, k), axis=-1)
        out = jnp.einsum('bhij,bhjp->bhip', scores, v)
        return out.reshape(B, D, N)

    def _L0_ffn_ref(x, sW1, sb1, sW2, sb2, rW1, rb1, rW2, rb2, gW, gb):
        import jax, jax.numpy as jnp
        import numpy as np
        D_MODEL = 128
        D_FF = 512
        NUM_M = 2
        E_ROUTER = 8 * NUM_M - 1
        D_FF_R = D_FF // NUM_M
        TOP_K = NUM_M * 2 - 1
        B, T = (2, 256)

        def _expert_stack(x, W1, b1, W2, b2):
            h = jax.nn.gelu(jnp.einsum('btd,edf->ebtf', x, W1) + b1[:, None, None, :], approximate=False)
            return jnp.einsum('ebtf,efd->ebtd', h, W2) + b2[:, None, None, :]
        shared_enc = _expert_stack(x, sW1, sb1, sW2, sb2).sum(0)
        weights = jax.nn.softmax(x @ gW + gb, axis=-1)
        topv, topi = jax.lax.top_k(weights, TOP_K)
        gated = (jax.nn.one_hot(topi, E_ROUTER, dtype=weights.dtype) * topv[..., None]).sum(axis=-2)
        router_out = _expert_stack(x, rW1, rb1, rW2, rb2)
        router_enc = jnp.einsum('ebtd,bte->btd', router_out, gated)
        return shared_enc + router_enc + x

    def _L1_attn_ref(x, norm_w, norm_b, in_proj_w, conv_w, conv_b, x_proj_w, dt_proj_w, dt_proj_b, A_log, D_param, out_proj_w):
        import jax, jax.numpy as jnp
        import numpy as np
        from jax import lax
        D_MODEL = 128
        D_INNER = 256
        D_STATE = 16
        DT_RANK = 128
        K = 4
        EPS = 1e-05

        def _layer_norm(x, w, b):
            mu = jnp.mean(x, axis=-1, keepdims=True)
            var = jnp.mean(jnp.square(x - mu), axis=-1, keepdims=True)
            return (x - mu) * lax.rsqrt(var + EPS) * w + b

        def _causal_depthwise_conv(x, w, b):
            L = x.shape[1]
            xp = jnp.pad(x, ((0, 0), (K - 1, 0), (0, 0)))
            out = b
            for k in range(K):
                out = out + w[:, k] * xp[:, k:k + L, :]
            return out

        def _selective_scan(u, delta, A, B, C, D):
            deltaA = jnp.exp(jnp.einsum('bld,dn->bldn', delta, A))
            deltaBu = jnp.einsum('bld,bln,bld->bldn', delta, B, u)
            bsz, _, d, n = deltaA.shape

            def step(h, inp):
                dA, dBu, Ct = inp
                h = dA * h + dBu
                y = jnp.einsum('bdn,bn->bd', h, Ct)
                return (h, y)
            h0 = jnp.zeros((bsz, d, n), u.dtype)
            _, ys = lax.scan(step, h0, (deltaA.transpose(1, 0, 2, 3), deltaBu.transpose(1, 0, 2, 3), C.transpose(1, 0, 2)))
            y = ys.transpose(1, 0, 2)
            return y + u * D
        residual = x
        h = _layer_norm(x, norm_w, norm_b)
        xr = h @ in_proj_w
        xs, res = (xr[..., :D_INNER], xr[..., D_INNER:])
        xs = _causal_depthwise_conv(xs, conv_w, conv_b)
        xs = jax.nn.silu(xs)
        A = -jnp.exp(A_log)
        xp = xs @ x_proj_w
        dr = xp[..., :DT_RANK]
        Bm = xp[..., DT_RANK:DT_RANK + D_STATE]
        Cm = xp[..., DT_RANK + D_STATE:]
        delta = jax.nn.softplus(dr @ dt_proj_w + dt_proj_b)
        y = _selective_scan(xs, delta, A, Bm, Cm, D_param)
        y = y * jax.nn.silu(res)
        return y @ out_proj_w + residual

    def _L1_ffn_ref(hidden_states, w_router, gate_up_proj, down_proj, w_gate, w_up, w_down):
        import jax, jax.numpy as jnp
        import numpy as np
        E = 16
        H = 128
        F = 256
        TOP_K = 1
        B, S = (2, 128)
        b, s, h = hidden_states.shape
        x = hidden_states.reshape(-1, h)
        logits = x @ w_router.T
        _, top_idx = jax.lax.top_k(logits, TOP_K)
        mask = jax.nn.one_hot(top_idx, E, dtype=logits.dtype).sum(axis=1)
        scores = jax.nn.sigmoid(logits) * mask
        masked_inputs = scores.T[:, :, None] * x[None, :, :]
        gate_up = jnp.einsum('eth,ehf->etf', masked_inputs, gate_up_proj)
        gate, up = jnp.split(gate_up, 2, axis=-1)
        expert_out = jnp.einsum('etf,efh->eth', up * jax.nn.silu(gate), down_proj)
        shared = jax.nn.silu(x @ w_gate.T) * (x @ w_up.T) @ w_down.T
        out = shared + expert_out.sum(axis=0)
        return out.reshape(b, s, h)
    x = L0_attn_x
    xn = _layernorm(x, axis=-1)
    x = x + _L0_attn_ref(xn, L0_attn_W_qkv, L0_attn_b_qkv) + _L0_ffn_ref(xn, L0_ffn_sW1, L0_ffn_sb1, L0_ffn_sW2, L0_ffn_sb2, L0_ffn_rW1, L0_ffn_rb1, L0_ffn_rW2, L0_ffn_rb2, L0_ffn_gW, L0_ffn_gb)
    xn = _layernorm(x, axis=-1)
    x = x + _L1_attn_ref(xn, L1_attn_norm_w, L1_attn_norm_b, L1_attn_in_proj_w, L1_attn_conv_w, L1_attn_conv_b, L1_attn_x_proj_w, L1_attn_dt_proj_w, L1_attn_dt_proj_b, L1_attn_A_log, L1_attn_D_param, L1_attn_out_proj_w) + _L1_ffn_ref(xn, L1_ffn_w_router, L1_ffn_gate_up_proj, L1_ffn_down_proj, L1_ffn_w_gate, L1_ffn_w_up, L1_ffn_w_down)
    return x

_drawn_inputs = setup_inputs


def setup_inputs(seed=0):
    import zlib

    import numpy as np

    out = dict(_drawn_inputs(seed))
    spreads = {'L1_attn_norm_w': (1.0, 0.2),
     'L1_attn_norm_b': (0.0, 0.347),
     'L1_attn_conv_b': (0.0, 0.436)}
    factors = {'L0_attn_b_qkv': 8.0,
     'L0_ffn_sb1': 6.423,
     'L0_ffn_sb2': 4.356,
     'L0_ffn_rW1': 2.668,
     'L0_ffn_rb1': 8.0,
     'L0_ffn_rb2': 8.0,
     'L0_ffn_gW': 2.731,
     'L0_ffn_gb': 8.0,
     'L1_attn_dt_proj_w': 3.913,
     'L1_ffn_w_router': 8.0,
     'L1_ffn_gate_up_proj': 8.0,
     'L1_ffn_down_proj': 8.0,
     'L1_ffn_w_gate': 8.0,
     'L1_ffn_w_up': 8.0,
     'L1_ffn_w_down': 8.0}
    for name, (base, spread) in spreads.items():
        noise = np.random.default_rng([zlib.crc32(name.encode()), seed]).standard_normal(out[name].shape)
        drawn = base * np.exp(spread * noise) if base else spread * noise
        out[name] = jnp.asarray(drawn.astype(out[name].dtype))
    for name, factor in factors.items():
        out[name] = (out[name] * factor).astype(out[name].dtype)
    return out
```

```python
import concourse.bass as bass
from concourse import mybir
from contextlib import ExitStack, contextmanager

F32 = mybir.dt.float32
BF16 = mybir.dt.bfloat16
I32 = mybir.dt.int32
ALU = mybir.AluOpType
ACT = mybir.ActivationFunctionType
AX = mybir.AxisListType

P = 128
B, L, D = 8, 512, 128
T = L // P
NT = B * T
H, HD = 16, 8
LN_EPS = 1e-5

Q_ROWS = [0, 0, 0, 1, 1, 2]
K_ROWS = [0, 1, 2, 0, 1, 0]
SR = 96
MR = SR + 3
HH = H // 2
VW = 32


class Chain:

    def __init__(self, eng, sem, base=0):
        self.eng, self.sem, self.base, self.n = eng, sem, base, 0

    def add(self, ins):
        ins.then_inc(self.sem, 1)
        self.n += 1

    def settle(self):
        self.eng.wait_ge(self.sem, self.base + self.n)


def norm_and_project(nc, ctx, A, R):
    with ExitStack() as own:
        def sb(name, shape, dt):
            return own.enter_context(nc.sbuf_tensor(name, shape, dt))

        def ps(name, shape, dt=F32):
            return own.enter_context(nc.psum_tensor(name, shape, dt))

        def sem(name):
            return nc.alloc_semaphore(name)

        E = A["gW"].shape[1]
        x_t = sb("x_t", [P, 2, T, D], F32)
        xc_t = sb("xc_t", [P, 2, T, D], F32)
        sq_t = sb("sq_t", [P, 2, T, D], F32)
        xn_t = sb("xn_t", [P, 2, T, D], F32)
        xT_t = sb("xT_t", [P, 2, L], F32)
        stat = sb("stat", [P, 2, 4, T], F32)
        minus_half = sb("minus_half", [P, T], F32)
        qk_f = sb("qk_f", [P, 2, 2, L], F32)
        qk_r = sb("qk_r", [P, 2, 2, L], F32)
        qk_p = sb("qk_p", [P, 2, 2, 3, L], BF16)
        wqkv = sb("wqkv", [P, 3 * D], F32)
        wqk = sb("wqk", [P, 2, D], F32)
        gw = sb("gw", [P, E], F32)
        bqk = sb("bqk", [P, 2], F32)
        bv = sb("bv", [P, D], F32)
        gb = sb("gb", [P, E], F32)
        p_T = ps("p_T", [P, L])
        p_q = ps("p_q", [P, L])
        p_k = ps("p_k", [P, L])
        p_v = ps("p_v", [P, T, D])
        p_g = ps("p_g", [P, T, E])

        ident_set = sem("ident_set")
        weights_in = sem("weights_in")
        x_in = [sem(f"x_in{u}") for u in range(2)]
        xc_done, sq_done, xn_done, a_dve = sem("xc_done"), sem("sq_done"), sem("xn_done"), sem("a_dve")
        T_done, T_kept, q_done, k_done, vg_done = sem("T_done"), sem("T_kept"), sem("q_done"), sem("k_done"), sem("vg_done")
        part1, rest1, part2, part3 = sem("part1"), sem("rest1"), sem("part2"), sem("part3")
        stacks_zero = sem("stacks_zero")
        half_set, w_turned = sem("half_set"), sem("w_turned")
        a_act, rstd_done = sem("a_act"), sem("rstd_done")
        kept = sem("kept")
        vg_kept = sem("vg_kept")
        qk_out = [sem(f"qk_out{u}") for u in range(2)]

        x_d = A["x"].rearrange("b (t p) d -> b p t d", p=P)
        block = own.enter_context(nc.Block())

        @block.sync
        def _(sp):
            sp.dma_start(wqkv[:], A["Wqkv"]).then_inc(weights_in, 16)
            sp.dma_start(gw[:], A["gW"]).then_inc(weights_in, 16)
            for n in range(2):
                for c in range(HD):
                    sp.dma_start(bqk[H * c:H * (c + 1), n:n + 1],
                                 A["bqkv"][n * D:(n + 1) * D].rearrange("(h c) -> c h", c=HD)[c].unsqueeze(1),
                                 allow_slow_non_contiguous=True).then_inc(weights_in, 16)
            sp.dma_start(bv[:], A["bqkv"][2 * D:3 * D].partition_broadcast(P)).then_inc(weights_in, 16)
            sp.dma_start(gb[:], A["gb"].partition_broadcast(P)).then_inc(weights_in, 16)

            def load_x(i, u, first):
                b = i * 2 + u
                if not first:
                    sp.wait_ge(kept, b * 3 - 3)
                sp.dma_start(x_t[:, u], x_d[bass.ds(b, 1)].rearrange("o p t d -> (o p) t d")).then_inc(x_in[u], 16)

            def store_qk(i, u):
                b = i * 2 + u
                sp.wait_ge(part3, b + 1)
                for n, dst in ((0, R["q_dram"]), (1, R["k_dram"])):
                    sp.dma_start(dst[bass.ds(b, 1)].rearrange("o c p t -> (o p) c t"), qk_p[:, u, n]).then_inc(qk_out[u], 16)

            load_x(0, 0, True)
            load_x(0, 1, True)
            with sp.Fori(1, B // 2) as i:
                for u in range(2):
                    load_x(i, u, False)
                    store_qk(i - 1, u)
            for u in range(2):
                store_qk(B // 2 - 1, u)
            for u in range(2):
                sp.wait_ge(qk_out[u], 32 * (B // 2))

        @block.gpsimd
        def _(pool):
            ident = R["ident"]
            nc.gpsimd.memset(minus_half[:], -0.5).then_inc(half_set, 1)
            pool.wait_ge(half_set, 1)
            nc.gpsimd.memset(ident[:], 0.0).then_inc(ident_set, 1)
            pool.wait_ge(ident_set, 1)
            nc.gpsimd.affine_select(out=ident[:], in_=ident[:], compare_op=ALU.not_equal, fill=1.0, base=0,
                                    pattern=[[-1, P]], channel_multiplier=1).then_inc(ident_set, 1)
            for n, stacks in enumerate((R["qs"], R["ks"])):
                nc.gpsimd.memset(stacks[:].bitcast(F32), 0.0).then_inc(stacks_zero, 1)
            pool.wait_ge(weights_in, 16 * (4 + 2 * HD))
            for n in range(2):
                nc.gpsimd.tensor_copy(wqk[:, n].rearrange("k (c h) -> k c h", c=HD),
                                      wqkv[:, n * D:(n + 1) * D].rearrange("k (h c) -> k c h", c=HD)).then_inc(w_turned, 1)
            with pool.Fori(0, B // 2) as i:
                for u in range(2):
                    b = i * 2 + u
                    rows = bass.ds(b * T, T)
                    pool.wait_ge(a_dve, b * 5 + 4)
                    nc.gpsimd.tensor_tensor(stat[:, u, 3], stat[:, u, 1], minus_half[:], ALU.pow).then_inc(rstd_done, 1)
                    pool.wait_ge(xn_done, b + 1)
                    nc.gpsimd.tensor_tensor(R["acc"][:, rows, :], x_t[:, u], xn_t[:, u], ALU.add).then_inc(kept, 1)
                    nc.gpsimd.tensor_copy(R["xn"][:, rows, :], xn_t[:, u]).then_inc(kept, 1)
                    pool.wait_ge(T_kept, b + 1)
                    nc.gpsimd.tensor_copy(R["xnT"][:, bass.ds(b * L, L)], xT_t[:, u]).then_inc(kept, 1)

        @block.vector
        def _(dve):
            dve.wait_ge(weights_in, 16 * (4 + 2 * HD))
            STEPS = 5

            def batch(i, u, first):
                b = i * 2 + u
                own_steps = Chain(dve, a_dve, b * STEPS)
                dve.wait_ge(x_in[u], i * 16 + 16)
                own_steps.add(nc.vector.tensor_reduce(stat[:, u, 1], x_t[:, u], AX.X, ALU.add))
                own_steps.settle()
                own_steps.add(nc.vector.tensor_scalar(stat[:, u, 0], stat[:, u, 1], 1.0 / D, None, ALU.mult))
                own_steps.settle()
                nc.vector.tensor_tensor(xc_t[:, u], x_t[:, u], stat[:, u, 0].unsqueeze(2).to_broadcast([P, T, D]),
                                        ALU.subtract).then_inc(xc_done, 1)
                dve.wait_ge(sq_done, b + 1)
                own_steps.add(nc.vector.tensor_reduce(stat[:, u, 2], sq_t[:, u], AX.X, ALU.add))
                own_steps.settle()
                own_steps.add(nc.vector.tensor_scalar(stat[:, u, 1], stat[:, u, 2], 1.0 / D, LN_EPS, ALU.mult, ALU.add))
                own_steps.settle()
                dve.wait_ge(rstd_done, b + 1)
                if not first:
                    dve.wait_ge(kept, b * 3 - 3)
                nc.vector.tensor_tensor(xn_t[:, u], xc_t[:, u], stat[:, u, 3].unsqueeze(2).to_broadcast([P, T, D]),
                                        ALU.mult).then_inc(xn_done, 1)
                dve.wait_ge(part1, b + 1)
                nc.vector.tensor_tensor(qk_r[:, u], qk_f[:, u], qk_p[:, u, :, 0], ALU.subtract).then_inc(rest1, 1)
                dve.wait_ge(vg_done, b + 1)
                own_steps.add(nc.vector.tensor_tensor(R["v"][:, bass.ds(b * T, T), :], p_v[:],
                                                      bv[:].unsqueeze(1).to_broadcast([P, T, D]), ALU.add))
                nc.vector.tensor_tensor(R["logits"][:, bass.ds(b * T, T), :], p_g[:],
                                        gb[:].unsqueeze(1).to_broadcast([P, T, E]), ALU.add).then_inc(vg_kept, 1)
                dve.wait_ge(part2, b + 1)
                nc.vector.tensor_tensor(qk_p[:, u, :, 2], qk_r[:, u], qk_p[:, u, :, 1], ALU.subtract).then_inc(part3, 1)
                assert own_steps.n == STEPS

            for u in range(2):
                batch(0, u, True)
            with dve.Fori(1, B // 2) as i:
                for u in range(2):
                    batch(i, u, False)

        @block.scalar
        def _(act):
            act.wait_ge(weights_in, 16 * (4 + 2 * HD))

            def batch(i, u, first):
                b = i * 2 + u
                act.wait_ge(xc_done, b + 1)
                nc.scalar.activation(sq_t[:, u], xc_t[:, u], ACT.Square).then_inc(sq_done, 1)
                act.wait_ge(T_done, b + 1)
                if not first:
                    act.wait_ge(kept, b * 3 - 3)
                nc.scalar.activation(xT_t[:, u], p_T[:], ACT.Copy).then_inc(T_kept, 1)
                act.wait_ge(q_done, b + 1)
                nc.scalar.activation(qk_f[:, u, 0], p_q[:], ACT.Identity, bias=bqk[:, 0:1]).then_inc(a_act, 1)
                act.wait_ge(k_done, b + 1)
                nc.scalar.activation(qk_f[:, u, 1], p_k[:], ACT.Identity, bias=bqk[:, 1:2]).then_inc(a_act, 1)
                act.wait_ge(a_act, b * 2 + 2)
                if not first:
                    act.wait_ge(qk_out[u], i * 32)
                nc.scalar.activation(qk_p[:, u, :, 0], qk_f[:, u], ACT.Copy).then_inc(part1, 1)
                act.wait_ge(rest1, b + 1)
                nc.scalar.activation(qk_p[:, u, :, 1], qk_r[:, u], ACT.Copy).then_inc(part2, 1)

            for u in range(2):
                batch(0, u, True)
            with act.Fori(1, B // 2) as i:
                for u in range(2):
                    batch(i, u, False)

        @block.tensor
        def _(pe):
            pe.wait_ge(ident_set, 2)
            pe.wait_ge(weights_in, 16 * (4 + 2 * HD))
            pe.wait_ge(w_turned, 2)
            with pe.Fori(0, B // 2) as i:
                for u in range(2):
                    b = i * 2 + u
                    pe.wait_ge(xn_done, b + 1)
                    for t in range(T):
                        last = nc.tensor.transpose(p_T[:, t * P:(t + 1) * P], xn_t[:, u, t], R["ident"][:])
                    last.then_inc(T_done, 1)
                    pe.wait_ge(T_kept, b + 1)
                    nc.tensor.matmul(p_q[:], wqk[:, 0], xT_t[:, u], start=True, stop=True).then_inc(q_done, 1)
                    nc.tensor.matmul(p_k[:], wqk[:, 1], xT_t[:, u], start=True, stop=True).then_inc(k_done, 1)
                    for t in range(T):
                        nc.tensor.matmul(p_v[:, t], xT_t[:, u, t * P:(t + 1) * P], wqkv[:, 2 * D:3 * D], start=True, stop=True)
                    for t in range(T):
                        last = nc.tensor.matmul(p_g[:, t], xT_t[:, u, t * P:(t + 1) * P], gw[:], start=True, stop=True)
                    last.then_inc(vg_done, 1)
                    pe.wait_ge(a_act, b * 2 + 2)
                    pe.wait_ge(vg_kept, b + 1)


def attention(nc, ctx, A, R):
    with ExitStack() as own:
        def sb(name, shape, dt):
            return own.enter_context(nc.sbuf_tensor(name, shape, dt))

        def ps(name, shape, dt=F32):
            return own.enter_context(nc.psum_tensor(name, shape, dt))

        def sem(name):
            return nc.alloc_semaphore(name)

        qs, ks = R["qs"], R["ks"]
        ones = sb("ones", [3, L], BF16)
        va = sb("va", [P, 2, T, H, VW], F32)
        pr = sb("pr", [P, 2, 4, L], F32)
        os_t = sb("os_t", [P, L], F32)
        rden = sb("rden", [P, T, 4], F32)
        at = sb("at", [P, 2, H, T, HD], F32)
        att = sb("att", [P, 2, T, D], F32)
        nmax = sb("nmax", [P, T, H], F32)
        nres = sb("nres", [P, T, HH], F32)
        nmp = sb("nmp", [P, T, 3, HH], BF16)
        nmT = sb("nmT", [3 * HH, L], BF16)
        p_st = ps("p_st", [P, 2, 2, L])
        p_s = ps("p_s", [P, 2, L])
        p_o = ps("p_o", [P, L])
        p_m = ps("p_m", [P, L])
        p_to = p_m[:].rearrange("p (t g c) -> p t g c", t=T, g=4)
        p_nm = p_m[0:3 * HH, 0:L // 2].bitcast(BF16)

        stacked = [[sem(f"stacked{u}{h}") for h in range(2)] for u in range(2)]
        ones_set, ones_in, va_zero, va_set = sem("ones_set"), sem("ones_in"), sem("va_zero"), sem("va_set")
        s_done, max_done = sem("s_done"), sem("max_done")
        st_done, exp_done, pv_done = sem("st_done"), sem("exp_done"), sem("pv_done")
        o_kept, to_done, at_done, added = sem("o_kept"), sem("to_done"), sem("at_done"), sem("added")
        at_out, at_in = sem("at_out"), sem("at_in")
        b_dve_r = sem("b_dve_r")
        b_dve, parts_done, nmT_done, nmT_kept, nm_out = (
            sem("b_dve"), sem("parts_done"), sem("nmT_done"), sem("nmT_kept"), sem("nm_out"))
        nm_in = [sem(f"nm_in{h}") for h in range(2)]
        identb_set = sem("identb_set")

        UNITS = 4 * T
        SCORES = H * T
        ROW_RUNS = [(0, 3), (3, 5), (5, 6)]
        LOADS = 2 * len(ROW_RUNS) * 16
        q_v = R["q_dram"].rearrange("b c (p h) t -> b c p (h t)", p=HD)
        k_v = R["k_dram"].rearrange("b c (p h) t -> b c p (h t)", p=HD)
        block = own.enter_context(nc.Block())

        @block.sync
        def _(sp):
            def stack(b, u, hf):
                hs, cols = slice(hf * HH, (hf + 1) * HH), slice(hf * HH * L, (hf + 1) * HH * L)
                for src, dst, rows in ((q_v, qs, Q_ROWS), (k_v, ks, K_ROWS)):
                    for lo, hi in ROW_RUNS:
                        c = rows[lo]
                        if rows[hi - 1] == c:
                            part = src[bass.ds(b, 1), c, :, cols].to_broadcast([hi - lo, HD, HH * L])
                        else:
                            part = src[bass.ds(b, 1), c:c + hi - lo, :, cols].rearrange("o c p t -> (o c) p t")
                        sp.dma_start(dst[HD * lo:HD * hi, u, hs].rearrange("p h t -> p (h t)"), part).then_inc(stacked[u][hf], 16)

            def place_max(b, u, h, n):
                sp.wait_ge(nmT_kept, n)
                sp.dma_start(R["nm_dram"][h], nmT[:]).then_inc(nm_out, 16)
                sp.wait_ge(nm_out, n * 16)
                sp.dma_start(qs[SR:MR, u, h * HH:(h + 1) * HH],
                             R["nm_dram"][h].rearrange("(c j) t -> c j t", c=3)).then_inc(nm_in[h], 16)

            for u in range(2):
                for hf in range(2):
                    stack(u, u, hf)
            sp.wait_ge(ones_set, 1)
            for u in range(2):
                sp.dma_start(ks[SR:MR, u], ones[:].unsqueeze(1).to_broadcast([3, H, L])).then_inc(ones_in, 16)
            for h in range(2):
                place_max(0, 0, h, 1 + h)

            def reshape_out(b, u, first):
                if not first:
                    sp.wait_ge(added, b - 1)
                sp.wait_ge(at_done, b * 4 + 4)
                sp.dma_start(R["at_dram"][u].rearrange("(h p c) -> p h c", h=H, p=P),
                             at[:, u].rearrange("p h t c -> p h (t c)")).then_inc(at_out, 16)
                sp.wait_ge(at_out, b * 16 + 16)
                sp.dma_start(att[:, u], R["at_dram"][u].rearrange("(t p d) -> p t d", t=T, p=P)).then_inc(at_in, 16)

            def batch(b, u, first=False, maxima=True, stacks=True):
                for hf in range(2):
                    if stacks:
                        sp.wait_ge(pv_done, b * UNITS + (hf + 1) * (UNITS // 2))
                        stack(b + 2, u, hf)
                    if maxima:
                        place_max(b + 1, 1 - u, hf, b * 2 + 3 + hf)
                reshape_out(b, u, first)

            for u in range(2):
                batch(u, u, first=True)
            with sp.Fori(1, B // 2 - 1) as i:
                for u in range(2):
                    batch(i * 2 + u, u)
            batch(B - 2, 0, stacks=False)
            batch(B - 1, 1, maxima=False, stacks=False)

        @block.gpsimd
        def _(pool):
            nc.gpsimd.memset(ones[:], 1.0).then_inc(ones_set, 1)
            nc.gpsimd.tensor_copy(R["identb"][:], R["ident"][:]).then_inc(identb_set, 1)
            nc.gpsimd.memset(va[:], 0.0).then_inc(va_zero, 1)
            pool.wait_ge(va_zero, 1)
            nc.gpsimd.memset(va[:, :, :, :, HD], 1.0).then_inc(va_zero, 1)

            def place_v(b, u):
                nc.gpsimd.tensor_copy(va[:, u, :, :, 0:HD],
                                      R["v"][:, bass.ds(b * T, T), :].rearrange("p t (h c) -> p t h c", c=HD)).then_inc(va_set, 1)

            def batch(b, u, more):
                rows = bass.ds(b * T, T)
                pool.wait_ge(at_in, b * 16 + 16)
                nc.gpsimd.tensor_tensor(R["acc"][:, rows, :], R["acc"][:, rows, :], att[:, u], ALU.add).then_inc(added, 1)
                if more:
                    place_v(b + 2, u)

            pool.wait_ge(va_zero, 2)
            place_v(0, 0)
            place_v(1, 1)
            with pool.Fori(0, B // 2 - 1) as i:
                for u in range(2):
                    batch(i * 2 + u, u, True)
            for u in range(2):
                batch(B - 2 + u, u, False)

        @block.tensor
        def _(pe):
            def max_scores(b, u, n, first=False):
                h, t = n // T, n % T
                if not (first and n < 2):
                    pe.wait_ge(max_done, b * SCORES + n - 1)
                q, k = qs[0:SR, u, h], ks[0:SR, u, h]
                nc.tensor.matmul(p_s[:, n % 2], q[:, t::T], k, start=True, stop=True).then_inc(s_done, 1)

            def turn_max(b, hf, turned):
                pe.wait_ge(parts_done, b * 2 + hf + 1)
                if turned is not None:
                    pe.wait_ge(at_done, turned)
                elif hf:
                    pe.wait_ge(nmT_kept, 1)
                for t in range(T):
                    last = nc.tensor.transpose(p_nm[:, t * P:(t + 1) * P], nmp[:, t].rearrange("p c h -> p (c h)"),
                                               R["identb"][:])
                last.then_inc(nmT_done, 1)

            def scores(b, u, w, n, first):
                g, t, x, y = w // T, w % T, n // 2, n % 2
                if y == 0 and not (first and w == 0):
                    pe.wait_ge(exp_done, b * (2 * UNITS) + 2 * w + x - 1)
                h = 4 * g + n
                q, k = qs[:, u, h], ks[:, u, h]
                last = nc.tensor.matmul(p_st[:, x, y], k[:, t * P:(t + 1) * P], q, start=True, stop=True)
                if y == 1:
                    last.then_inc(st_done, 1)

            def products(b, u, w, first):
                g, t = w // T, w % T
                if t == 0 and not (first and g == 0):
                    pe.wait_ge(o_kept, b * 4 + g)
                pe.wait_ge(exp_done, b * (2 * UNITS) + 2 * w + 2)
                for y in range(4):
                    last = nc.tensor.matmul(p_o[VW * y:VW * (y + 1)], va[:, u, t, 4 * g + y], pr[:, w % 2, y],
                                            start=t == 0, stop=t == T - 1, tile_position=(0, VW * y))
                last.then_inc(pv_done, 1)

            def turn_out(b, g, more):
                pe.wait_ge(o_kept, b * 4 + g + 1)
                if g == 0:
                    pe.wait_ge(nmT_kept, b * 2 + 2)
                if g > 1 and more:
                    pe.wait_ge(nmT_kept, b * 2 + g + 1)
                if not (g == 0 and isinstance(b, int) and b == 0):
                    pe.wait_ge(at_done, b * 4 + g)
                for t in range(T):
                    last = nc.tensor.transpose(p_m[:, t * P:(t + 1) * P], os_t[:, t::T], R["ident"][:])
                last.then_inc(to_done, 1)

            def batch(b, u, i, first, more):
                for w in range(UNITS):
                    if w == 0:
                        pe.wait_ge(nm_in[0], b * 16 + 16)
                        pe.wait_ge(va_set, b + 1)
                        if more:
                            pe.wait_ge(stacked[1 - u][0], (i + u) * LOADS + LOADS)
                    if w == UNITS // 2:
                        if more:
                            pe.wait_ge(stacked[1 - u][1], (i + u) * LOADS + LOADS)
                        pe.wait_ge(nm_in[1], b * 16 + 16)
                    for n in range(4):
                        scores(b, u, w, n, first)
                        if more and n > 0:
                            max_scores(b + 1, 1 - u, 4 * w + n - 1)
                    if w > 0:
                        products(b, u, w - 1, first)
                    if w % T == 1 and w > T:
                        turn_out(b, w // T - 1, more)
                    if more:
                        max_scores(b + 1, 1 - u, 4 * w + 3)
                        if w == UNITS // 2 + 3:
                            turn_max(b + 1, 0, b * 4 + 2)
                products(b, u, UNITS - 1, first)
                if more:
                    turn_max(b + 1, 1, b * 4 + 3)
                turn_out(b, 3, more)

            pe.wait_ge(identb_set, 1)
            pe.wait_ge(ones_in, 32)
            for hf in range(2):
                pe.wait_ge(stacked[0][hf], LOADS)
            for n in range(SCORES):
                max_scores(0, 0, n, first=True)
                if n == SCORES // 2 + 4:
                    turn_max(0, 0, None)
            turn_max(0, 1, None)
            batch(0, 0, 0, True, True)
            batch(1, 1, 0, False, True)
            with pe.Fori(1, B // 2 - 1) as i:
                for u in range(2):
                    batch(i * 2 + u, u, i, False, True)
            batch(B - 2, 0, B // 2 - 1, False, True)
            batch(B - 1, 1, B // 2 - 1, False, False)

        @block.scalar
        def _(act):
            def batch(b, first):
                for w in range(UNITS):
                    for x in range(2):
                        act.wait_ge(st_done, b * (2 * UNITS) + 2 * w + x + 1)
                        if x == 0 and not (first and w < 2):
                            act.wait_ge(pv_done, b * UNITS + w - 1)
                        nc.scalar.activation(pr[:, w % 2, 2 * x:2 * x + 2], p_st[:, x], ACT.Exp).then_inc(exp_done, 1)

            batch(0, True)
            with act.Fori(1, B) as b:
                batch(b, False)

        @block.vector
        def _(dve):
            STEPS = 8

            def maxima(b, n):
                h, t = n // T, n % T
                dve.wait_ge(s_done, b * SCORES + n + 1)
                nc.vector.tensor_reduce(nmax[:, t, h:h + 1], p_s[:, n % 2], AX.X, ALU.max,
                                        negate=True).then_inc(max_done, 1)

            def split_max(b, hf, steps):
                m, rest = nmax[:, :, hf * HH:(hf + 1) * HH], nres[:]
                part = [nmp[:, :, c] for c in range(3)]
                dve.wait_ge(max_done, b * SCORES + (hf + 1) * (SCORES // 2))
                steps.add(nc.vector.tensor_copy(part[0], m))
                steps.settle()
                steps.add(nc.vector.tensor_tensor(rest, m, part[0], ALU.subtract))
                steps.settle()
                steps.add(nc.vector.tensor_copy(part[1], rest))
                steps.settle()
                nc.vector.tensor_tensor(part[2], rest, part[1], ALU.subtract).then_inc(parts_done, 1)

            def keep_max(b, hf, first=False):
                dve.wait_ge(nmT_done, b * 2 + hf + 1)
                if not (first and hf == 0):
                    dve.wait_ge(nm_out, (b * 2 + hf) * 16)
                nc.vector.tensor_copy(nmT[:].rearrange("m (q t) -> m t q", t=T),
                                      p_nm.rearrange("m (t q) -> m t q", t=T)).then_inc(nmT_kept, 1)

            def keep_out(b, g):
                dve.wait_ge(pv_done, b * UNITS + (g + 1) * T)
                if isinstance(b, int) and b == 0 and g == 0:
                    pass
                else:
                    dve.wait_ge(to_done, b * 4 + g)
                nc.vector.tensor_copy(os_t[:], p_o[:]).then_inc(o_kept, 1)

            def normalize(b, u, g, first):
                dve.wait_ge(to_done, b * 4 + g + 1)
                if g == 0 and not first:
                    dve.wait_ge(at_out, b * 16 - 16)
                nc.vector.reciprocal(rden[:], p_to[:, :, :, HD]).then_inc(b_dve_r, 1)
                dve.wait_ge(b_dve_r, b * 4 + g + 1)
                nc.vector.tensor_tensor(at[:, u, 4 * g:4 * g + 4], p_to[:, :, :, 0:HD].rearrange("p t g c -> p g t c"),
                                        rden[:].rearrange("p t g -> p g t").unsqueeze(3).to_broadcast([P, 4, T, HD]),
                                        ALU.mult).then_inc(at_done, 1)

            def batch(b, u, first, more):
                steps = Chain(dve, b_dve, b * 6 + 6)
                for w in range(UNITS):
                    if more:
                        for n in range(3):
                            maxima(b + 1, 4 * w + n)
                    if w % T == 0 and w > 0:
                        keep_out(b, w // T - 1)
                    if more:
                        maxima(b + 1, 4 * w + 3)
                        if w == UNITS // 2:
                            split_max(b + 1, 0, steps)
                        if w == UNITS // 2 + 4:
                            keep_max(b + 1, 0)
                    if w % T == 1 and w > T:
                        normalize(b, u, w // T - 1, first)
                if more:
                    split_max(b + 1, 1, steps)
                    keep_out(b, 3)
                    keep_max(b + 1, 1)
                    assert steps.n == 6
                else:
                    keep_out(b, 3)
                normalize(b, u, 3, first)

            steps = Chain(dve, b_dve)
            for n in range(SCORES):
                maxima(0, n)
                if n == SCORES // 2 + 2:
                    split_max(0, 0, steps)
                if n == SCORES // 2 + 8:
                    keep_max(0, 0, first=True)
            split_max(0, 1, steps)
            keep_max(0, 1)
            batch(0, 0, True, True)
            batch(1, 1, True, True)
            with dve.Fori(1, B // 2 - 1) as i:
                for u in range(2):
                    batch(i * 2 + u, u, False, True)
            batch(B - 2, 0, False, True)
            batch(B - 1, 1, False, False)


def most_tiles(rows, experts):
    return rows // P - 1 + experts


def route(nc, ctx, R, tag, w, E, K, TILES):
    gate, slot, chosen, owner = R[tag + "gate"], R[tag + "slot"], R[tag + "chosen"], R[tag + "owner"]
    with ExitStack() as own:
        def sb(name, shape, dt=F32):
            return own.enter_context(nc.sbuf_tensor(tag + name, shape, dt))

        def sem(name):
            return nc.alloc_semaphore(tag + name)

        e_no = sb("e_no", [P, NT, E])
        t_rows = sb("t_rows", [P, E, NT])
        tile_no = sb("tile_no", [P, TILES, E])
        below = sb("below", [P, P])
        ones = sb("ones", [P, P])
        left = sb("left", [P, NT, E])
        is_max = sb("is_max", [P, NT, E])
        key = sb("key", [P, NT, E])
        first_key = sb("first_key", [P, NT])
        pick = sb("pick", [P, K, NT, E])
        picked = sb("picked", [P, E, NT])
        total = sb("total", [P, E, NT])
        reset = sb("reset", [P, E, NT])
        run = sb("run", [P, E, NT])
        over = sb("over", [P, E, NT])
        tiles = sb("tiles", [P, E])
        cum = sb("cum", [P, E])
        base = sb("base", [P, E])
        place = sb("place", [P, E, NT])
        prod = sb("prod", [P, NT, E])
        slot_f = sb("slot_f", [P, K, NT])
        passed = sb("passed", [P, TILES, E])
        owner_f = sb("owner_f", [P, TILES])
        p_rank = own.enter_context(nc.psum_tensor(tag + "p_rank", [P, E, NT], F32))
        p_total = own.enter_context(nc.psum_tensor(tag + "p_total", [P, E, NT], F32))
        tables, chain, picked_set, counted = sem("tables"), sem("chain"), sem("picked_set"), sem("counted")
        block = own.enter_context(nc.Block())

        @block.gpsimd
        def _(pool):
            exact = dict(allow_small_or_imprecise_dtypes=True)
            nc.gpsimd.iota(e_no[:], [[0, NT], [1, E]], base=0, channel_multiplier=0, **exact).then_inc(tables, 1)
            nc.gpsimd.memset(ones[:], 1.0).then_inc(tables, 1)
            nc.gpsimd.memset(reset[:], 1.0).then_inc(tables, 1)
            pool.wait_ge(tables, 3)
            nc.gpsimd.memset(reset[:, :, 0], 0.0).then_inc(tables, 1)
            nc.gpsimd.affine_select(out=below[:], in_=ones[:], compare_op=ALU.is_gt, fill=0.0, base=0,
                                    pattern=[[1, P]], channel_multiplier=-1).then_inc(tables, 1)
            nc.gpsimd.iota(t_rows[:], [[0, E], [P, NT]], base=0, channel_multiplier=0, **exact).then_inc(tables, 1)
            nc.gpsimd.iota(tile_no[:], [[1, TILES], [0, E]], base=0, channel_multiplier=0, **exact).then_inc(tables, 1)

        @block.tensor
        def _(pe):
            pe.wait_ge(tables, 7)
            pe.wait_ge(picked_set, 1)
            nc.tensor.matmul(p_rank[:], below[:], picked[:], start=True, stop=True)
            nc.tensor.matmul(p_total[:], ones[:], picked[:], start=True, stop=True).then_inc(counted, 1)

        @block.vector
        def _(dve):
            steps = Chain(dve, chain)

            def step(ins):
                steps.add(ins)
                steps.settle()

            def by_row(x):
                return x.unsqueeze(2).to_broadcast([P, NT, E])

            tt, stt = nc.vector.tensor_tensor, nc.vector.scalar_tensor_tensor
            dve.wait_ge(tables, 7)
            values = w
            for k in range(K):
                step(nc.vector.tensor_reduce(gate[:, k], values, AX.X, ALU.max))
                step(tt(is_max[:], values, by_row(gate[:, k]), ALU.is_equal))
                step(stt(out=key[:], in0=is_max[:], scalar=-2.0 * E, in1=e_no[:], op0=ALU.mult, op1=ALU.add))
                step(nc.vector.tensor_reduce(first_key[:], key[:], AX.X, ALU.min))
                step(tt(pick[:, k], key[:], by_row(first_key[:]), ALU.is_equal))
                if k < K - 1:
                    step(stt(out=left[:], in0=pick[:, k], scalar=-4.0, in1=values, op0=ALU.mult, op1=ALU.add))
                    values = left[:]
                step(nc.vector.tensor_copy(chosen[:], pick[:, 0]) if k == 0 else
                     tt(chosen[:], chosen[:], pick[:, k], ALU.add))
            nc.vector.tensor_copy(picked[:], chosen[:].rearrange("p t e -> p e t")).then_inc(picked_set, 1)
            dve.wait_ge(counted, 1)
            step(nc.vector.tensor_copy(total[:], p_total[:]))
            step(nc.vector.tensor_tensor_scan(run[:].rearrange("p e t -> p (e t)"), reset[:].rearrange("p e t -> p (e t)"),
                                              total[:].rearrange("p e t -> p (e t)"), 0.0, ALU.mult, ALU.add))
            step(tt(over[:], run[:, :, NT - 1:NT].to_broadcast([P, E, NT]), t_rows[:], ALU.is_gt))
            step(nc.vector.tensor_reduce(tiles[:], over[:], AX.X, ALU.add))
            step(nc.vector.tensor_tensor_scan(cum[:], ones[:, 0:E], tiles[:], 0.0, ALU.mult, ALU.add))
            step(tt(base[:], cum[:], tiles[:], ALU.subtract))
            step(tt(place[:], run[:], total[:], ALU.subtract))
            step(tt(place[:], place[:], p_rank[:], ALU.add))
            step(stt(out=place[:], in0=base[:].unsqueeze(2).to_broadcast([P, E, NT]), scalar=float(P), in1=place[:],
                     op0=ALU.mult, op1=ALU.add))
            for k in range(K):
                step(tt(prod[:], pick[:, k], place[:].rearrange("p e t -> p t e"), ALU.mult))
                step(nc.vector.tensor_reduce(slot_f[:, k], prod[:], AX.X, ALU.add))
            step(nc.vector.tensor_copy(slot[:], slot_f[:]))
            step(tt(passed[:], tile_no[:], cum[:].unsqueeze(1).to_broadcast([P, TILES, E]), ALU.is_ge))
            step(nc.vector.tensor_reduce(owner_f[:], passed[:], AX.X, ALU.add))
            step(nc.vector.tensor_scalar(owner[:], owner_f[:], float(E - 1), None, ALU.min))


def softmax_weights(nc, ctx, R, E):
    with ExitStack() as own:
        def sem(name):
            return nc.alloc_semaphore(name)

        top = own.enter_context(nc.sbuf_tensor("r_top", [P, 3, NT], F32))
        logits, weights = R["logits"], R["weights"]
        chain, shifted, expd = sem("r_chain"), sem("r_shifted"), sem("r_expd")
        block = own.enter_context(nc.Block())

        def by_row(x):
            return x.unsqueeze(2).to_broadcast([P, NT, E])

        @block.vector
        def _(dve):
            steps = Chain(dve, chain)
            steps.add(nc.vector.tensor_reduce(top[:, 0], logits[:], AX.X, ALU.max))
            steps.settle()
            nc.vector.tensor_tensor(weights[:], logits[:], by_row(top[:, 0]), ALU.subtract).then_inc(shifted, 1)
            dve.wait_ge(expd, 1)
            steps.add(nc.vector.tensor_reduce(top[:, 1], weights[:], AX.X, ALU.add))
            steps.settle()
            steps.add(nc.vector.reciprocal(top[:, 2], top[:, 1]))
            steps.settle()
            nc.vector.tensor_tensor(weights[:], weights[:], by_row(top[:, 2]), ALU.mult)

        @block.scalar
        def _(act):
            act.wait_ge(shifted, 1)
            nc.scalar.activation(weights[:], weights[:], ACT.Exp).then_inc(expd, 1)


def scatter_rows(nc, ctx, tag, slot, rows, K, table):
    with ExitStack() as own:
        sent = nc.alloc_semaphore(tag + "sent")
        block = own.enter_context(nc.Block())

        @block.gpsimd
        def _(pool):
            for t in range(NT):
                for k in range(K):
                    nc.gpsimd.indirect_dma_start(
                        out=table, out_offset=bass.IndirectOffsetOnAxis(ap=slot[:, k, t:t + 1], axis=0),
                        in_=rows[:, t], in_offset=None).then_inc(sent, 16)
            pool.wait_ge(sent, 16 * K * NT)


def gather_rows(nc, ctx, R, tag, slot, K, table):
    gate = R[tag + "gate"] if K > 1 else None
    DEPTH = 4
    with ExitStack() as own:
        got = own.enter_context(nc.sbuf_tensor(tag + "got", [P, DEPTH, K, D], F32))
        arrived = [nc.alloc_semaphore(tag + f"arrived{n}") for n in range(DEPTH)]
        taken = nc.alloc_semaphore(tag + "taken")
        block = own.enter_context(nc.Block())

        @block.gpsimd
        def _(pool):
            for t in range(NT):
                if t >= DEPTH:
                    pool.wait_ge(taken, K * (t - DEPTH + 1))
                for k in range(K):
                    nc.gpsimd.indirect_dma_start(
                        out=got[:, t % DEPTH, k], out_offset=None, in_=table,
                        in_offset=bass.IndirectOffsetOnAxis(ap=slot[:, k, t:t + 1], axis=0)).then_inc(arrived[t % DEPTH], 16)

        @block.vector
        def _(dve):
            for t in range(NT):
                dve.wait_ge(arrived[t % DEPTH], 16 * K * (t // DEPTH + 1))
                for k in range(K):
                    acc, row = R["acc"][:, t], got[:, t % DEPTH, k]
                    if k:
                        dve.wait_ge(taken, K * t + k)
                    if gate is None:
                        ins = nc.vector.tensor_tensor(acc, acc, row, ALU.add)
                    else:
                        ins = nc.vector.scalar_tensor_tensor(out=acc, in0=row, scalar=gate[:, k, t:t + 1], in1=acc,
                                                             op0=ALU.mult, op1=ALU.add)
                    ins.then_inc(taken, 1)


DEPTH = 4


def whole(tiles):
    return -(-tiles // DEPTH) * DEPTH


def expert_tiles(nc, ctx, R, tag, TILES, E, w1_d, w2_d, table_in, table_out, gated):
    N1 = w1_d.shape[2]
    C1 = N1 // P
    CF = w2_d.shape[1] // P
    owner = R[tag + "owner"]
    with ExitStack() as own:
        def sb(name, shape, dt=F32):
            return own.enter_context(nc.sbuf_tensor(tag + name, shape, dt))

        def sem(name):
            return nc.alloc_semaphore(tag + name)

        xs = sb("xs", [P, DEPTH, D])
        w1 = sb("w1", [P, DEPTH, N1])
        w2 = sb("w2", [P, DEPTH, CF, D])
        xT = sb("xT", [P, 2, P])
        hid = sb("hid", [P, 2, CF, P])
        sil = sb("sil", [P, 2, CF, P])
        y = sb("y", [P, DEPTH, D])
        p_x = [own.enter_context(nc.psum_tensor(tag + f"p_x{n}", [P, P], F32)) for n in range(2)]
        p_h = [own.enter_context(nc.psum_tensor(tag + f"p_h{n}", [P, C1, P], F32)) for n in range(2)]
        p_y = [own.enter_context(nc.psum_tensor(tag + f"p_y{n}", [P, D], F32)) for n in range(2)]
        tile_in = [sem(f"tile_in{n}") for n in range(DEPTH)]
        tile_out = [sem(f"tile_out{n}") for n in range(DEPTH)]
        x_turned, x_kept, h_done, sil_done, hid_done, y_done, y_kept = (
            sem("x_turned"), sem("x_kept"), sem("h_done"), sem("sil_done"), sem("hid_done"), sem("y_done"), sem("y_kept"))
        block = own.enter_context(nc.Block())

        def groups(eng, tile):
            for n in range(DEPTH):
                tile(n, n, True)
            with eng.Fori(1, TILES // DEPTH) as i:
                for n in range(DEPTH):
                    tile(i * DEPTH + n, n, False)

        @block.sync
        def _(sp):
            def store(j, n):
                sp.wait_ge(y_kept, j + 1)
                sp.dma_start(table_out[bass.ds(j * P, P), :], y[:, n]).then_inc(tile_out[n], 16)

            def tile(j, n, first):
                if not first:
                    store(j - DEPTH, n)
                    sp.wait_ge(y_done, j - DEPTH + 1)
                e = sp.value_load(owner[0:1, bass.ds(j, 1)], min_val=0, max_val=E - 1)
                sp.dma_start(xs[:, n], table_in[bass.ds(j * P, P), :]).then_inc(tile_in[n], 16)
                sp.dma_start(w1[:, n], w1_d[bass.ds(e, 1)].rearrange("o p f -> (o p) f")).then_inc(tile_in[n], 16)
                sp.dma_start(w2[:, n], w2_d[bass.ds(e, 1)].rearrange("o (c p) d -> (o p) c d", p=P)).then_inc(tile_in[n], 16)

            groups(sp, tile)
            for n in range(DEPTH):
                store(TILES - DEPTH + n, n)
            for n in range(DEPTH):
                sp.wait_ge(tile_out[n], 16 * (TILES // DEPTH))

        @block.tensor
        def _(pe):
            def turn(j, n, first, i):
                pe.wait_ge(tile_in[n], i * 48 + 48)
                if not (first and n < 2):
                    pe.wait_ge(x_kept, j - 1)
                nc.tensor.transpose(p_x[n % 2][:], xs[:, n], R["ident"][:]).then_inc(x_turned, 1)

            def hidden(j, n, first):
                pe.wait_ge(x_kept, j + 1)
                if not (first and n < 2):
                    pe.wait_ge(hid_done, j - 1)
                for c in range(C1):
                    last = nc.tensor.matmul(p_h[n % 2][:, c], w1[:, n, c * P:(c + 1) * P], xT[:, n % 2], start=True, stop=True)
                last.then_inc(h_done, 1)

            def product(j, n, first):
                pe.wait_ge(hid_done, j + 1)
                if not (first and n < 2):
                    pe.wait_ge(y_kept, j - 1)
                for c in range(CF):
                    last = nc.tensor.matmul(p_y[n % 2][:], hid[:, n % 2, c], w2[:, n, c], start=c == 0, stop=c == CF - 1)
                last.then_inc(y_done, 1)

            def step(j, n, first, i, last_group=False):
                if not (last_group and n == DEPTH - 1):
                    m = (n + 1) % DEPTH
                    turn(j + 1, m, first and m > 0, i + (1 if m == 0 else 0))
                hidden(j, n, first)
                if not (first and n == 0):
                    product(j - 1, (n - 1) % DEPTH, first)

            turn(0, 0, True, 0)
            for n in range(DEPTH):
                step(n, n, True, 0)
            with pe.Fori(1, TILES // DEPTH - 1) as i:
                for n in range(DEPTH):
                    step(i * DEPTH + n, n, False, i)
            for n in range(DEPTH):
                step(TILES - DEPTH + n, n, False, TILES // DEPTH - 1, last_group=True)
            product(TILES - 1, DEPTH - 1, False)

        @block.scalar
        def _(act):
            def tile(j, n, first):
                if gated:
                    act.wait_ge(h_done, j + 1)
                    if not (first and n < 2):
                        act.wait_ge(hid_done, j - 1)
                    nc.scalar.activation(sil[:, n % 2], p_h[n % 2][:, 0:CF], ACT.Silu).then_inc(sil_done, 1)
                    return
                e = act.value_load(owner[0:1, bass.ds(j, 1)], min_val=0, max_val=E - 1)
                act.wait_ge(h_done, j + 1)
                if not (first and n < 2):
                    act.wait_ge(y_done, j - 1)
                for c in range(CF):
                    last = nc.scalar.activation(hid[:, n % 2, c], p_h[n % 2][:, c], ACT.Gelu,
                                                bias=R["b1T"][:, bass.ds(e * CF + c, 1)])
                last.then_inc(hid_done, 1)

            groups(act, tile)

        @block.vector
        def _(dve):
            def keep_x(j, n, first):
                dve.wait_ge(x_turned, j + 1)
                if not (first and n < 2):
                    dve.wait_ge(h_done, j - 1)
                nc.vector.tensor_copy(xT[:, n % 2], p_x[n % 2][:]).then_inc(x_kept, 1)

            def keep_y(j, n, first):
                dve.wait_ge(y_done, j + 1)
                if not first:
                    dve.wait_ge(tile_out[n], (j // DEPTH) * 16 if isinstance(j, int) else j * (16 // DEPTH) - n * (16 // DEPTH))
                nc.vector.tensor_copy(y[:, n], p_y[n % 2][:]).then_inc(y_kept, 1)

            def hide(j, n, first):
                dve.wait_ge(sil_done, j + 1)
                if not (first and n < 2):
                    dve.wait_ge(y_done, j - 1)
                nc.vector.tensor_tensor(hid[:, n % 2], sil[:, n % 2], p_h[n % 2][:, CF:C1], ALU.mult).then_inc(hid_done, 1)

            def tile(j, n, first):
                keep_x(j, n, first)
                if not (first and n < 2):
                    m = (n - 2) % DEPTH
                    keep_y(j - 2, m, first or (n < 2 and isinstance(j, int) and j < 2 * DEPTH))
                if gated and not (first and n == 0):
                    hide(j - 1, (n - 1) % DEPTH, first)

            for n in range(DEPTH):
                tile(n, n, True)
            for n in range(2):
                tile(DEPTH + n, n, False)
            for n in range(2, DEPTH):
                tile(DEPTH + n, n, False)
            with dve.Fori(2, TILES // DEPTH) as i:
                for n in range(DEPTH):
                    tile(i * DEPTH + n, n, False)
            keep_y(TILES - 2, DEPTH - 2, False)
            if gated:
                hide(TILES - 1, DEPTH - 1, False)
            keep_y(TILES - 1, DEPTH - 1, False)


def expert_biases(nc, ctx, A, R, E):
    CF, CS = A["rb1"].shape[1] // P, A["sb1"].shape[1] // P
    with ExitStack() as own:
        rows = own.enter_context(nc.sbuf_tensor("b_rows", [E * CF + CS, P], F32))
        p_b = own.enter_context(nc.psum_tensor("p_b", [P, E * CF + CS], F32))
        b_in, b_turned, w_in = (nc.alloc_semaphore(n) for n in ("b_in", "b_turned", "sw_in"))
        g_set = nc.alloc_semaphore("g_set")
        block = own.enter_context(nc.Block())

        @block.sync
        def _(sp):
            sp.dma_start(rows[0:E * CF], A["rb1"].rearrange("e (c p) -> (e c) p", p=P)).then_inc(b_in, 16)
            sp.dma_start(rows[E * CF:], A["sb1"].rearrange("o (c p) -> (o c) p", p=P)).then_inc(b_in, 16)
            sp.dma_start(R["b2"][0:E], A["rb2"]).then_inc(w_in, 16)
            sp.dma_start(R["b2"][E:E + 1], A["sb2"]).then_inc(w_in, 16)
            sp.dma_start(R["sw1"][:], A["sW1"].rearrange("o p f -> (o p) f")).then_inc(w_in, 16)
            sp.dma_start(R["sw2"][:], A["sW2"].rearrange("o (c p) d -> (o p) c d", p=P)).then_inc(w_in, 16)
            sp.wait_ge(w_in, 64)

        @block.tensor
        def _(pe):
            pe.wait_ge(b_in, 32)
            n = E * CF + CS
            nc.tensor.transpose(p_b[:], rows[:], R["ident"][0:n, 0:n]).then_inc(b_turned, 1)

        @block.vector
        def _(dve):
            nc.vector.memset(R["gates"][:, :, E], 1.0).then_inc(g_set, 1)
            nc.vector.tensor_tensor(R["gates"][:, :, 0:E], R["achosen"][:], R["weights"][:], ALU.mult).then_inc(g_set, 1)
            dve.wait_ge(b_turned, 1)
            nc.vector.tensor_copy(R["b1T"][:], p_b[:])


def shared_expert(nc, ctx, R, E):
    CS = R["sw2"].shape[1]
    S0 = R["b1T"].shape[1] - CS
    with ExitStack() as own:
        def sb(name, shape, dt=F32):
            return own.enter_context(nc.sbuf_tensor("s_" + name, shape, dt))

        def sem(name):
            return nc.alloc_semaphore("s_" + name)

        hs = sb("hs", [P, 2, CS, L])
        gs = sb("gs", [P, T, E + 1])
        gT = sb("gT", [E + 1, L])
        p_h = own.enter_context(nc.psum_tensor("s_p_h", [P, 4, L], F32))
        p_g = own.enter_context(nc.psum_tensor("s_p_g", [E + 1, L], F32))
        p_o = own.enter_context(nc.psum_tensor("s_p_o", [P, 2, T, D], F32))
        h_done, hs_done, gs_done, g_turned, g_kept, o_done, o_added = (
            sem(n) for n in ("h_done", "hs_done", "gs_done", "g_turned", "g_kept", "o_done", "o_added"))
        block = own.enter_context(nc.Block())

        @block.tensor
        def _(pe):
            def hidden(b, first):
                for c in range(CS):
                    if not first:
                        pe.wait_ge(hs_done, b * CS + c + 1 - CS)
                    nc.tensor.matmul(p_h[:, c], R["sw1"][:, c * P:(c + 1) * P], R["xnT"][:, bass.ds(b * L, L)],
                                     start=True, stop=True).then_inc(h_done, 1)
                pe.wait_ge(gs_done, b + 1)
                for t in range(T):
                    last = nc.tensor.transpose(p_g[:, t * P:(t + 1) * P], gs[:, t], R["ident"][:])
                last.then_inc(g_turned, 1)

            def output(b, u, first):
                pe.wait_ge(hs_done, b * CS + CS)
                pe.wait_ge(g_kept, b + 1)
                if not first:
                    pe.wait_ge(o_added, b - 1)
                for t in range(T):
                    tok = slice(t * P, (t + 1) * P)
                    for c in range(CS):
                        nc.tensor.matmul(p_o[:, u, t], hs[:, u, c, tok], R["sw2"][:, c], start=c == 0, stop=False)
                    last = nc.tensor.matmul(p_o[:, u, t], gT[:, tok], R["b2"][:], start=False, stop=True)
                last.then_inc(o_done, 1)

            for u in range(2):
                hidden(u, u == 0)
                output(u, u, True)
            with pe.Fori(1, B // 2) as i:
                for u in range(2):
                    hidden(i * 2 + u, False)
                    output(i * 2 + u, u, False)

        @block.scalar
        def _(act):
            def batch(b, u, first):
                for c in range(CS):
                    act.wait_ge(h_done, b * CS + c + 1)
                    if c == 0 and not first:
                        act.wait_ge(o_done, b - 1)
                    nc.scalar.activation(hs[:, u, c], p_h[:, c], ACT.Gelu, bias=R["b1T"][:, S0 + c:S0 + c + 1]).then_inc(hs_done, 1)

            for u in range(2):
                batch(u, u, True)
            with act.Fori(1, B // 2) as i:
                for u in range(2):
                    batch(i * 2 + u, u, False)

        @block.vector
        def _(dve):
            def gates(b, first):
                if not first:
                    dve.wait_ge(g_turned, b)
                nc.vector.tensor_copy(gs[:], R["gates"][:, bass.ds(b * T, T), :]).then_inc(gs_done, 1)

            def batch(b, u, first, more=True):
                dve.wait_ge(g_turned, b + 1)
                if not first:
                    dve.wait_ge(o_done, b)
                nc.vector.tensor_copy(gT[:], p_g[:]).then_inc(g_kept, 1)
                if more:
                    gates(b + 1, False)
                dve.wait_ge(o_done, b + 1)
                rows = R["acc"][:, bass.ds(b * T, T), :]
                nc.vector.tensor_tensor(rows, rows, p_o[:, u], ALU.add).then_inc(o_added, 1)

            gates(0, True)
            batch(0, 0, True)
            batch(1, 1, False)
            with dve.Fori(1, B // 2 - 1) as i:
                for u in range(2):
                    batch(i * 2 + u, u, False)
            batch(B - 2, 0, False)
            batch(B - 1, 1, False, more=False)


def norm_chain(nc, dve, pool_wait, steps, src, xc, sq, stat, out, out_sem, rstd):
    def by_token(x):
        return x.unsqueeze(2).to_broadcast([P, T, D])

    steps.add(nc.vector.tensor_reduce(stat[:, 1], src, AX.X, ALU.add))
    steps.settle()
    steps.add(nc.vector.tensor_scalar(stat[:, 0], stat[:, 1], 1.0 / D, None, ALU.mult))
    steps.settle()
    steps.add(nc.vector.tensor_tensor(xc, src, by_token(stat[:, 0]), ALU.subtract))
    steps.settle()
    steps.add(nc.vector.tensor_tensor(sq, xc, xc, ALU.mult))
    steps.settle()
    steps.add(nc.vector.tensor_reduce(stat[:, 2], sq, AX.X, ALU.add))
    steps.settle()
    nc.vector.tensor_scalar(stat[:, 1], stat[:, 2], 1.0 / D, LN_EPS, ALU.mult, ALU.add).then_inc(pool_wait, 1)
    rstd()
    nc.vector.tensor_tensor(out, xc, by_token(stat[:, 3]), ALU.mult).then_inc(out_sem, 1)


TAPS = 4
DI = 256
NC = DI // P
NS = 16
DR = 128


def norm_and_mix(nc, ctx, A, R):
    E = A["w_router"].shape[0]
    with ExitStack() as own:
        def sb(name, shape, dt=F32):
            return own.enter_context(nc.sbuf_tensor("m_" + name, shape, dt))

        def sem(name):
            return nc.alloc_semaphore("m_" + name)

        inw = sb("inw", [P, 2 * DI])
        taps = sb("taps", [P, DI, TAPS])
        wtap = sb("wtap", [P, TAPS, DI])
        convb = sb("convb", [P, NC])
        rrows = sb("rrows", [E, D])
        rT = sb("rT", [P, E])
        nw = sb("nw", [P, 2, D])
        minus_half = sb("minus_half", [P, T])
        xc = sb("xc", [P, T, D])
        sq = sb("sq", [P, T, D])
        stat = sb("stat", [P, 2, 4, T])
        xs = sb("xs", [P, 2, T, D])
        xn_t = sb("xn_t", [P, 2, T, D])
        hn = sb("hn", [P, T, D])
        h_t = sb("h_t", [P, 2, T, D])
        xT_t = sb("xT_t", [P, 2, L])
        hT_t = sb("hT_t", [P, 2, TAPS - 1 + L])
        p_T = own.enter_context(nc.psum_tensor("m_p_T", [P, 2, L], F32))
        p_g = own.enter_context(nc.psum_tensor("m_p_g", [P, T, E], F32))
        p_c = own.enter_context(nc.psum_tensor("m_p_c", [P, 4, L], F32))
        w_in, r_turned, r_kept, wtap_set, set_up = sem("w_in"), sem("r_turned"), sem("r_kept"), sem("wtap_set"), sem("set_up")
        x_kept, chain, var_done, rstd_done, xn_done, hn_done, h_ready, added = (
            sem("x_kept"), sem("chain"), sem("var_done"), sem("rstd_done"), sem("xn_done"), sem("hn_done"), sem("h_ready"), sem("added"))
        x_turned, xT_kept, h_turned, hT_kept, g_done, g_kept, c_done, c_kept, copied = (
            sem("x_turned"), sem("xT_kept"), sem("h_turned"), sem("hT_kept"), sem("g_done"), sem("g_kept"), sem("c_done"), sem("c_kept"), sem("copied"))
        block = own.enter_context(nc.Block())
        LOADS = 16 * (6 + NC)

        @block.sync
        def _(sp):
            sp.dma_start(inw[:], A["in_proj_w"]).then_inc(w_in, 16)
            sp.dma_start(taps[:], A["conv_w"].partition_broadcast(P)).then_inc(w_in, 16)
            for c in range(NC):
                sp.dma_start(convb[:, c:c + 1], A["conv_b"][c * P:(c + 1) * P].unsqueeze(1)).then_inc(w_in, 16)
            sp.dma_start(rrows[:], A["w_router"]).then_inc(w_in, 16)
            sp.dma_start(nw[:, 0], A["norm_w"].partition_broadcast(P)).then_inc(w_in, 16)
            sp.dma_start(nw[:, 1], A["norm_b"].partition_broadcast(P)).then_inc(w_in, 16)
            sp.dma_start(R["A_log"][:], A["A_log"].rearrange("(c p) n -> p c n", p=P)).then_inc(w_in, 16)
            sp.wait_ge(w_in, LOADS)

        @block.gpsimd
        def _(pool):
            nc.gpsimd.memset(minus_half[:], -0.5).then_inc(set_up, 1)
            nc.gpsimd.memset(hT_t[:, :, 0:TAPS - 1], 0.0).then_inc(set_up, 1)
            pool.wait_ge(set_up, 2)
            with pool.Fori(0, B // 2) as i:
                for u in range(2):
                    b = i * 2 + u
                    rows = bass.ds(b * T, T)
                    pool.wait_ge(var_done, b * 2 + 1)
                    nc.gpsimd.tensor_tensor(stat[:, 0, 3], stat[:, 0, 1], minus_half[:], ALU.pow).then_inc(rstd_done, 1)
                    pool.wait_ge(xn_done, b + 1)
                    nc.gpsimd.tensor_copy(R["xn"][:, rows, :], xn_t[:, u]).then_inc(copied, 1)
                    pool.wait_ge(var_done, b * 2 + 2)
                    nc.gpsimd.tensor_tensor(stat[:, 1, 3], stat[:, 1, 1], minus_half[:], ALU.pow).then_inc(rstd_done, 1)
                    nc.gpsimd.tensor_tensor(R["acc"][:, rows, :], xs[:, u], xn_t[:, u], ALU.add).then_inc(copied, 1)
                    pool.wait_ge(xT_kept, b + 1)
                    nc.gpsimd.tensor_copy(R["xnT"][:, bass.ds(b * L, L)], xT_t[:, u]).then_inc(copied, 1)

        @block.vector
        def _(dve):
            dve.wait_ge(w_in, LOADS)
            for k in range(TAPS):
                nc.vector.tensor_tensor(wtap[:, k], inw[:, 0:DI], taps[:, :, k], ALU.mult).then_inc(wtap_set, 1)
            dve.wait_ge(r_turned, 1)
            nc.vector.tensor_copy(rT[:], p_g[:].rearrange("p t e -> p (t e)")[:, 0:E]).then_inc(r_kept, 1)
            STEPS = 12

            def batch(i, u, first):
                b = i * 2 + u
                steps = Chain(dve, chain, b * STEPS)

                def rstd(n):
                    return lambda: dve.wait_ge(rstd_done, b * 2 + n)

                if not first:
                    dve.wait_ge(copied, b * 3 - 3)
                steps.add(nc.vector.tensor_copy(xs[:, u], R["acc"][:, bass.ds(b * T, T), :]))
                steps.settle()
                norm_chain(nc, dve, var_done, steps, xs[:, u], xc[:], sq[:], stat[:, 0], xn_t[:, u], xn_done, rstd(1))
                dve.wait_ge(xn_done, b + 1)
                norm_chain(nc, dve, var_done, steps, xn_t[:, u], xc[:], sq[:], stat[:, 1], hn[:], hn_done, rstd(2))
                dve.wait_ge(hn_done, b + 1)
                steps.add(nc.vector.tensor_tensor(hn[:], hn[:], nw[:, 0].unsqueeze(1).to_broadcast([P, T, D]), ALU.mult))
                steps.settle()
                nc.vector.tensor_tensor(h_t[:, u], hn[:], nw[:, 1].unsqueeze(1).to_broadcast([P, T, D]), ALU.add).then_inc(h_ready, 1)
                dve.wait_ge(g_done, b + 1)
                nc.vector.tensor_copy(R["logits2"][:, bass.ds(b * T, T), :], p_g[:]).then_inc(g_kept, 1)
                assert steps.n == STEPS, steps.n

            for u in range(2):
                batch(0, u, True)
            with dve.Fori(1, B // 2) as i:
                for u in range(2):
                    batch(i, u, False)

        @block.tensor
        def _(pe):
            pe.wait_ge(w_in, LOADS)
            nc.tensor.transpose(p_g[:].rearrange("p t e -> p (t e)")[:, 0:E], rrows[:], R["ident"][0:E, 0:E]).then_inc(r_turned, 1)
            pe.wait_ge(r_kept, 1)
            pe.wait_ge(wtap_set, TAPS)
            pe.wait_ge(set_up, 2)

            def batch(b, u, first):
                pe.wait_ge(xn_done, b + 1)
                if not first:
                    pe.wait_ge(xT_kept, b)
                for t in range(T):
                    last = nc.tensor.transpose(p_T[:, 0, t * P:(t + 1) * P], xn_t[:, u, t], R["ident"][:])
                last.then_inc(x_turned, 1)
                pe.wait_ge(h_ready, b + 1)
                if not first:
                    pe.wait_ge(hT_kept, b)
                for t in range(T):
                    last = nc.tensor.transpose(p_T[:, 1, t * P:(t + 1) * P], h_t[:, u, t], R["ident"][:])
                last.then_inc(h_turned, 1)
                pe.wait_ge(xT_kept, b + 1)
                if not first:
                    pe.wait_ge(g_kept, b)
                for t in range(T):
                    last = nc.tensor.matmul(p_g[:, t], xT_t[:, u, t * P:(t + 1) * P], rT[:], start=True, stop=True)
                last.then_inc(g_done, 1)
                pe.wait_ge(hT_kept, b + 1)
                for c in range(4):
                    if not first:
                        pe.wait_ge(c_kept, b * 4 + c - 3)
                    if c < NC:
                        for k in range(TAPS):
                            last = nc.tensor.matmul(p_c[:, c], wtap[:, k, c * P:(c + 1) * P], hT_t[:, u, k:k + L],
                                                    start=k == 0, stop=k == TAPS - 1)
                    else:
                        last = nc.tensor.matmul(p_c[:, c], inw[:, c * P:(c + 1) * P], hT_t[:, u, TAPS - 1:],
                                                start=True, stop=True)
                    last.then_inc(c_done, 1)

            batch(0, 0, True)
            batch(1, 1, False)
            with pe.Fori(1, B // 2) as i:
                for u in range(2):
                    batch(i * 2 + u, u, False)

        @block.scalar
        def _(act):
            act.wait_ge(w_in, LOADS)

            def batch(b, u, first):
                act.wait_ge(x_turned, b + 1)
                if not first:
                    act.wait_ge(copied, b * 3 - 3)
                nc.scalar.activation(xT_t[:, u], p_T[:, 0], ACT.Copy).then_inc(xT_kept, 1)
                act.wait_ge(h_turned, b + 1)
                if not first:
                    act.wait_ge(c_done, b * 4 - 4)
                nc.scalar.activation(hT_t[:, u, TAPS - 1:], p_T[:, 1], ACT.Copy).then_inc(hT_kept, 1)
                for c in range(4):
                    act.wait_ge(c_done, b * 4 + c + 1)
                    if c < NC:
                        nc.scalar.activation(R["u"][:, c, bass.ds(b * L, L)], p_c[:, c], ACT.Silu, bias=convb[:, c:c + 1]).then_inc(c_kept, 1)
                    else:
                        nc.scalar.activation(R["g"][:, c - NC, bass.ds(b * L, L)], p_c[:, c], ACT.Silu).then_inc(c_kept, 1)

            for u in range(2):
                batch(u, u, True)
            with act.Fori(1, B // 2) as i:
                for u in range(2):
                    batch(i * 2 + u, u, False)


def step_sizes(nc, ctx, A, R):
    with ExitStack() as own:
        def sb(name, shape, dt=F32):
            return own.enter_context(nc.sbuf_tensor("d_" + name, shape, dt))

        def sem(name):
            return nc.alloc_semaphore("d_" + name)

        BC = 2 * NS
        xpw = sb("xpw", [P, NC, DR + BC])
        bcw = sb("bcw", [P, NC, 3, BC])
        dtw = sb("dtw", [P, DI])
        dtb = sb("dtb", [P, NC])
        dr = sb("dr", [P, L])
        first = sb("first", [3 * BC, L], BF16)
        rest = sb("rest", [3 * BC, L])
        z_abs = sb("z_abs", [P, NC, L])
        z_exp = sb("z_exp", [P, NC, L])
        z_pos = sb("z_pos", [P, NC, L])
        z_ln = sb("z_ln", [P, NC, L])
        p_dr = own.enter_context(nc.psum_tensor("d_p_dr", [P, L], F32))
        p_bc = own.enter_context(nc.psum_tensor("d_p_bc", [3 * BC, L], F32))
        p_z = own.enter_context(nc.psum_tensor("d_p_z", [P, NC, L], F32))
        w_in, bcw_set, a_exp, dr_done, dr_kept, bc_done, z_done, z_read, z_chain, ln_done, d_done = (
            sem(n) for n in ("w_in", "bcw_set", "a_exp", "dr_done", "dr_kept", "bc_done", "z_done", "z_read", "z_chain", "ln_done", "d_done"))
        split = sem("split")
        block = own.enter_context(nc.Block())
        LOADS = 16 * (2 + NC)

        @block.sync
        def _(sp):
            sp.dma_start(xpw[:], A["x_proj_w"].rearrange("(c p) n -> p c n", p=P)).then_inc(w_in, 16)
            sp.dma_start(dtw[:], A["dt_proj_w"]).then_inc(w_in, 16)
            for c in range(NC):
                sp.dma_start(dtb[:, c:c + 1], A["dt_proj_b"][c * P:(c + 1) * P].unsqueeze(1)).then_inc(w_in, 16)

        @block.gpsimd
        def _(pool):
            pool.wait_ge(w_in, LOADS)
            nc.gpsimd.tensor_copy(bcw[:], xpw[:, :, DR:].unsqueeze(2).to_broadcast([P, NC, 3, BC])).then_inc(bcw_set, 1)
            with pool.Fori(0, B) as b:
                pool.wait_ge(ln_done, b + 1)
                nc.gpsimd.tensor_tensor(R["delta"][:, :, bass.ds(b * L, L)], z_pos[:], z_ln[:], ALU.add).then_inc(d_done, 1)

        @block.tensor
        def _(pe):
            pe.wait_ge(w_in, LOADS)
            pe.wait_ge(bcw_set, 1)

            def batch(b, is_first):
                tok = bass.ds(b * L, L)
                if not is_first:
                    pe.wait_ge(dr_kept, b)
                for c in range(NC):
                    last = nc.tensor.matmul(p_dr[:], xpw[:, c, 0:DR], R["u"][:, c, tok], start=c == 0, stop=c == NC - 1)
                last.then_inc(dr_done, 1)
                if not is_first:
                    pe.wait_ge(split, b * 4)
                for c in range(NC):
                    last = nc.tensor.matmul(p_bc[:], bcw[:, c].rearrange("p r n -> p (r n)"), R["u"][:, c, tok],
                                            start=c == 0, stop=c == NC - 1)
                last.then_inc(bc_done, 1)
                pe.wait_ge(dr_kept, b + 1)
                if not is_first:
                    pe.wait_ge(z_read, b * 2)
                for c in range(NC):
                    last = nc.tensor.matmul(p_z[:, c], dtw[:, c * P:(c + 1) * P], dr[:], start=True, stop=True)
                last.then_inc(z_done, 1)

            batch(0, True)
            with pe.Fori(1, B) as b:
                batch(b, False)

        @block.scalar
        def _(act):
            act.wait_ge(w_in, LOADS)
            nc.scalar.activation(R["A_neg"][:], R["A_log"][:], ACT.Exp).then_inc(a_exp, 1)

            def batch(b, is_first):
                act.wait_ge(z_done, b + 1)
                if not is_first:
                    act.wait_ge(d_done, b)
                for c in range(NC):
                    last = nc.scalar.activation(z_abs[:, c], p_z[:, c], ACT.Abs, bias=dtb[:, c:c + 1])
                last.then_inc(z_read, 1)
                for c in range(NC):
                    last = nc.scalar.activation(z_pos[:, c], p_z[:, c], ACT.Relu, bias=dtb[:, c:c + 1])
                last.then_inc(z_read, 1)
                act.wait_ge(z_read, b * 2 + 2)
                nc.scalar.activation(z_exp[:], z_abs[:], ACT.Exp, scale=-1.0).then_inc(z_chain, 1)
                act.wait_ge(z_chain, b + 1)
                nc.scalar.activation(z_ln[:], z_exp[:], ACT.Ln, bias=1.0).then_inc(ln_done, 1)

            batch(0, True)
            with act.Fori(1, B) as b:
                batch(b, False)

        @block.vector
        def _(dve):
            dve.wait_ge(a_exp, 1)
            nc.vector.tensor_scalar(R["A_neg"][:], R["A_neg"][:], -1.0, None, ALU.mult)

            def batch(b, is_first):
                tok = bass.ds(b * L, L)
                dve.wait_ge(dr_done, b + 1)
                if not is_first:
                    dve.wait_ge(z_done, b)
                nc.vector.tensor_copy(dr[:], p_dr[:]).then_inc(dr_kept, 1)
                dve.wait_ge(bc_done, b + 1)
                nc.vector.tensor_copy(first[:], p_bc[:]).then_inc(split, 1)
                dve.wait_ge(split, b * 4 + 1)
                nc.vector.tensor_tensor(rest[:], p_bc[:], first[:], ALU.subtract).then_inc(split, 1)
                nc.vector.tensor_copy(R["bc"][0:BC, tok], first[0:BC])
                dve.wait_ge(split, b * 4 + 2)
                nc.vector.tensor_copy(first[BC:2 * BC], rest[BC:2 * BC])
                nc.vector.tensor_copy(first[2 * BC:], rest[2 * BC:]).then_inc(split, 1)
                dve.wait_ge(split, b * 4 + 3)
                nc.vector.tensor_copy(R["bc"][BC:2 * BC, tok], first[BC:2 * BC])
                nc.vector.tensor_tensor(R["bc"][2 * BC:, tok], rest[2 * BC:], first[2 * BC:], ALU.subtract).then_inc(split, 1)

            batch(0, True)
            with dve.Fori(1, B) as b:
                batch(b, False)


def state_space(nc, ctx, A, R):
    with ExitStack() as own:
        def sb(name, shape, dt=F32):
            return own.enter_context(nc.sbuf_tensor("y_" + name, shape, dt))

        def sem(name):
            return nc.alloc_semaphore("y_" + name)

        BC = 2 * NS
        pick = sb("pick", [3 * BC, BC, P], BF16)
        opw = sb("opw", [P, NC, D])
        dpar = sb("dpar", [P, NC])
        du = sb("du", [P, NC, L])
        bs = sb("bs", [P, 2, L])
        da = sb("da", [P, 2, NC, L])
        dbu = sb("dbu", [P, 2, NC, L])
        h = sb("h", [P, 2, NC, L])
        hc = sb("hc", [P, 2, NC, L])
        yz = sb("yz", [P, 2, NC, L])
        p_b = own.enter_context(nc.psum_tensor("y_p_b", [P, 2, L], F32))
        p_c = own.enter_context(nc.psum_tensor("y_p_c", [P, 2, L], F32))
        p_y = own.enter_context(nc.psum_tensor("y_p_y", [P, NC, L], F32))
        p_o = own.enter_context(nc.psum_tensor("y_p_o", [P, T, D], F32))
        (w_in, pick_set, du_done, b_done, c_done, b_kept, da_done, dbu_done, dbu_dve, h_done, hc_done, y_sum, yu, yz_done, o_done, o_added) = (
            sem(n) for n in ("w_in", "pick_set", "du_done", "b_done", "c_done", "b_kept", "da_done", "dbu_done", "dbu_dve", "h_done",
                             "hc_done", "y_sum", "yu", "yz_done", "o_done", "o_added"))
        block = own.enter_context(nc.Block())
        LOADS = 16 * (1 + NC)

        def on_pool(n, c):
            return c == 0 or n % 2 == 0

        N_POOL = sum(on_pool(n, c) for n in range(NS) for c in range(NC))
        N_DVE = NS * NC - N_POOL

        def pool_count(n, c):
            return sum(on_pool(m, d) for m in range(NS) for d in range(NC) if (m, d) <= (n, c))

        def pool_before(n):
            return pool_count(n, NC - 1) if n >= 0 else pool_count(NS + n, NC - 1) - N_POOL

        def dve_count(n, c):
            return n * NC + c + 1 - pool_count(n, c)

        @block.sync
        def _(sp):
            sp.dma_start(opw[:], A["out_proj_w"].rearrange("(c p) d -> p c d", p=P)).then_inc(w_in, 16)
            for c in range(NC):
                sp.dma_start(dpar[:, c:c + 1], A["D_param"][c * P:(c + 1) * P].unsqueeze(1)).then_inc(w_in, 16)

        @block.gpsimd
        def _(pool):
            nc.gpsimd.memset(pick[:], 1.0).then_inc(pick_set, 1)
            for r in range(3):
                pool.wait_ge(pick_set, r + 1)
                part = pick[r * BC:(r + 1) * BC]
                nc.gpsimd.affine_select(out=part, in_=part, compare_op=ALU.is_equal, fill=0.0, base=0,
                                        pattern=[[-1, BC], [0, P]], channel_multiplier=1).then_inc(pick_set, 1)

            def batch(b, first):
                pool.wait_ge(du_done, b + 1)
                for n in range(NS):
                    pool.wait_ge(b_kept, b * NS + n + 1)
                    for c in range(NC):
                        if on_pool(n, c):
                            if not (first and n < 2):
                                pool.wait_ge(h_done, b * NS * NC + (n - 2) * NC + c + 1)
                            nc.gpsimd.tensor_tensor(dbu[:, n % 2, c], du[:, c], bs[:, n % 2], ALU.mult).then_inc(dbu_done, 1)

            batch(0, True)
            with pool.Fori(1, B) as b:
                batch(b, False)

        @block.tensor
        def _(pe):
            pe.wait_ge(w_in, LOADS)
            pe.wait_ge(pick_set, 4)

            def spread(b, n, first):
                tok = bass.ds(b * L, L)
                if not (first and n < 2):
                    pe.wait_ge(b_kept, b * NS + n - 1)
                    if n % 2 == 1:
                        pe.wait_ge(dbu_dve, b * N_DVE + dve_count(n - 2, NC - 1) if n >= 2 else b * N_DVE)
                nc.tensor.matmul(p_b[:, n % 2], pick[:, n], R["bc"][:, tok], start=True, stop=True).then_inc(b_done, 1)
                if not (first and n < 2):
                    pe.wait_ge(hc_done, (b * NS + n - 1) * NC)
                nc.tensor.matmul(p_c[:, n % 2], pick[:, NS + n], R["bc"][:, tok], start=True, stop=True).then_inc(c_done, 1)

            def gather(b, n, first):
                for c in range(NC):
                    pe.wait_ge(hc_done, (b * NS + n) * NC + c + 1)
                    if n == 0 and not first:
                        pe.wait_ge(yu, (b - 1) * NC + c + 1)
                    nc.tensor.matmul(p_y[:, c], R["ident"][:], hc[:, n % 2, c], start=n == 0, stop=n == NS - 1).then_inc(y_sum, 1)

            def project(b, u, first):
                pe.wait_ge(yz_done, b * NC + NC)
                if not first:
                    pe.wait_ge(o_added, b)
                for t in range(T):
                    for c in range(NC):
                        last = nc.tensor.matmul(p_o[:, t], yz[:, u, c, t * P:(t + 1) * P], opw[:, c], start=c == 0, stop=c == NC - 1)
                last.then_inc(o_done, 1)

            def batch(b, u, first, before=True):
                for n in range(NS):
                    spread(b, n, first)
                    if n > 0:
                        gather(b, n - 1, first)
                    if n == 3 and before:
                        project(b - 1, 1 - u, isinstance(b, int) and b == 1)
                gather(b, NS - 1, first)

            batch(0, 0, True, before=False)
            batch(1, 1, False)
            with pe.Fori(1, B // 2) as i:
                for u in range(2):
                    batch(i * 2 + u, u, False)
            project(B - 1, 1, False)

        @block.scalar
        def _(act):
            def batch(b, first):
                tok = bass.ds(b * L, L)
                for n in range(NS):
                    act.wait_ge(b_done, b * NS + n + 1)
                    if not (first and n < 2):
                        act.wait_ge(dbu_done, b * N_POOL + pool_before(n - 2))
                        act.wait_ge(h_done, b * NS * NC + (n - 1) * NC)
                    nc.scalar.activation(bs[:, n % 2], p_b[:, n % 2], ACT.Copy).then_inc(b_kept, 1)
                    for c in range(NC):
                        nc.scalar.activation(da[:, n % 2, c], R["delta"][:, c, tok], ACT.Exp,
                                             scale=R["A_neg"][:, c, n:n + 1]).then_inc(da_done, 1)

            batch(0, True)
            with act.Fori(1, B) as b:
                batch(b, False)

        @block.vector
        def _(dve):
            dve.wait_ge(w_in, LOADS)

            def add_out(b):
                rows = R["acc"][:, bass.ds(b * T, T), :]
                dve.wait_ge(o_done, b + 1)
                nc.vector.tensor_tensor(rows, rows, p_o[:], ALU.add).then_inc(o_added, 1)

            def batch(b, u, first, before=True):
                tok = bass.ds(b * L, L)
                if not first:
                    dve.wait_ge(dbu_done, b * N_POOL)
                nc.vector.tensor_tensor(du[:], R["delta"][:, :, tok], R["u"][:, :, tok], ALU.mult).then_inc(du_done, 1)
                dve.wait_ge(du_done, b + 1)

                def times_c(n):
                    for c in range(NC):
                        at = (b * NS + n) * NC + c
                        dve.wait_ge(c_done, b * NS + n + 1)
                        dve.wait_ge(h_done, at + 1)
                        if not (first and n < 2):
                            dve.wait_ge(y_sum, at - 2 * NC + 1)
                        nc.vector.tensor_tensor(hc[:, n % 2, c], h[:, n % 2, c], p_c[:, n % 2], ALU.mult).then_inc(hc_done, 1)

                for n in range(NS):
                    for c in range(NC):
                        at = (b * NS + n) * NC + c
                        if on_pool(n, c):
                            dve.wait_ge(dbu_done, b * N_POOL + pool_count(n, c))
                        else:
                            dve.wait_ge(b_done, b * NS + n + 1)
                            nc.vector.tensor_tensor(dbu[:, n % 2, c], du[:, c], p_b[:, n % 2], ALU.mult).then_inc(dbu_dve, 1)
                            dve.wait_ge(dbu_dve, b * N_DVE + dve_count(n, c))
                        dve.wait_ge(da_done, at + 1)
                        nc.vector.tensor_tensor_scan(h[:, n % 2, c], da[:, n % 2, c], dbu[:, n % 2, c], 0.0,
                                                     ALU.mult, ALU.add).then_inc(h_done, 1)
                    if n > 0:
                        times_c(n - 1)
                    if n == 5 and before:
                        add_out(b - 1)
                times_c(NS - 1)
                for c in range(NC):
                    dve.wait_ge(y_sum, (b * NS + NS - 1) * NC + c + 1)
                    nc.vector.scalar_tensor_tensor(out=yz[:, u, c], in0=R["u"][:, c, tok], scalar=dpar[:, c:c + 1],
                                                   in1=p_y[:, c], op0=ALU.mult, op1=ALU.add).then_inc(yu, 1)
                for c in range(NC):
                    dve.wait_ge(yu, b * NC + c + 1)
                    nc.vector.tensor_tensor(yz[:, u, c], yz[:, u, c], R["g"][:, c, tok], ALU.mult).then_inc(yz_done, 1)

            batch(0, 0, True, before=False)
            batch(1, 1, False)
            with dve.Fori(1, B // 2) as i:
                for u in range(2):
                    batch(i * 2 + u, u, False)
            add_out(B - 1)


def scale_rows(nc, ctx, R):
    with ExitStack() as own:
        score = own.enter_context(nc.sbuf_tensor("z_score", [P, NT], F32))
        scored = nc.alloc_semaphore("z_scored")
        block = own.enter_context(nc.Block())

        @block.scalar
        def _(act):
            nc.scalar.activation(score[:], R["bgate"][:, 0], ACT.Sigmoid).then_inc(scored, 1)

        @block.vector
        def _(dve):
            dve.wait_ge(scored, 1)
            nc.vector.tensor_tensor(R["xn"][:], R["xn"][:], score[:].unsqueeze(2).to_broadcast([P, NT, D]), ALU.mult)


def shared_gated(nc, ctx, A, R):
    F = A["w_gate"].shape[0]
    CF = F // P
    with ExitStack() as own:
        def sb(name, shape, dt=F32):
            return own.enter_context(nc.sbuf_tensor("v_" + name, shape, dt))

        def sem(name):
            return nc.alloc_semaphore("v_" + name)

        raw = sb("raw", [P, 3, CF, P])
        wT = sb("wT", [P, 3, CF, P])
        sil = sb("sil", [P, CF, L])
        hid = sb("hid", [P, 2, CF, L])
        p_w = own.enter_context(nc.psum_tensor("v_p_w", [P, 2, CF, P], F32))
        p_h = own.enter_context(nc.psum_tensor("v_p_h", [P, 2, CF, L], F32))
        p_o = own.enter_context(nc.psum_tensor("v_p_o", [P, 2, T, D], F32))
        w_in, w_turned, w_kept, gate_done, up_done, sil_done, hid_done, o_done, o_added = (
            sem(n) for n in ("w_in", "w_turned", "w_kept", "gate_done", "up_done", "sil_done", "hid_done", "o_done", "o_added"))
        block = own.enter_context(nc.Block())

        @block.sync
        def _(sp):
            sp.dma_start(raw[:, 0], A["w_gate"].rearrange("(c p) d -> p c d", p=P)).then_inc(w_in, 16)
            sp.dma_start(raw[:, 1], A["w_up"].rearrange("(c p) d -> p c d", p=P)).then_inc(w_in, 16)
            sp.dma_start(raw[:, 2], A["w_down"].rearrange("d (c p) -> d c p", p=P)).then_inc(w_in, 16)

        @block.tensor
        def _(pe):
            pe.wait_ge(w_in, 48)
            for m in range(3):
                if m > 0:
                    pe.wait_ge(w_kept, m)
                for c in range(CF):
                    last = nc.tensor.transpose(p_w[:, 0, c], raw[:, m, c], R["ident"][:])
                last.then_inc(w_turned, 1)
            pe.wait_ge(w_kept, 3)

            def hidden(b, first):
                tok = bass.ds(b * L, L)
                for m, done in ((0, gate_done), (1, up_done)):
                    if not first:
                        pe.wait_ge(hid_done, b)
                    for c in range(CF):
                        last = nc.tensor.matmul(p_h[:, m, c], wT[:, m, c], R["xnT"][:, tok], start=True, stop=True)
                    last.then_inc(done, 1)

            def output(b, u, first):
                pe.wait_ge(hid_done, b + 1)
                if not first:
                    pe.wait_ge(o_added, b - 1)
                for t in range(T):
                    for c in range(CF):
                        last = nc.tensor.matmul(p_o[:, u, t], hid[:, u, c, t * P:(t + 1) * P], wT[:, 2, c],
                                                start=c == 0, stop=c == CF - 1)
                last.then_inc(o_done, 1)

            for u in range(2):
                hidden(u, u == 0)
                output(u, u, True)
            with pe.Fori(1, B // 2) as i:
                for u in range(2):
                    hidden(i * 2 + u, False)
                    output(i * 2 + u, u, False)

        @block.scalar
        def _(act):
            def batch(b, first):
                act.wait_ge(gate_done, b + 1)
                if not first:
                    act.wait_ge(hid_done, b)
                nc.scalar.activation(sil[:], p_h[:, 0], ACT.Silu).then_inc(sil_done, 1)

            batch(0, True)
            with act.Fori(1, B) as b:
                batch(b, False)

        @block.vector
        def _(dve):
            for m in range(3):
                dve.wait_ge(w_turned, m + 1)
                nc.vector.tensor_copy(wT[:, m], p_w[:, 0]).then_inc(w_kept, 1)

            def batch(b, u, first):
                dve.wait_ge(up_done, b + 1)
                dve.wait_ge(sil_done, b + 1)
                if not first:
                    dve.wait_ge(o_done, b - 1)
                nc.vector.tensor_tensor(hid[:, u], sil[:], p_h[:, 1], ALU.mult).then_inc(hid_done, 1)
                dve.wait_ge(o_done, b + 1)
                rows = R["acc"][:, bass.ds(b * T, T), :]
                nc.vector.tensor_tensor(rows, rows, p_o[:, u], ALU.add).then_inc(o_added, 1)

            for u in range(2):
                batch(u, u, True)
            with dve.Fori(1, B // 2) as i:
                for u in range(2):
                    batch(i * 2 + u, u, False)


def clear_tables(nc, ctx, R):
    with ExitStack() as own:
        zeros = own.enter_context(nc.sbuf_tensor("t_zeros", [P, D], F32))
        zeros_set, cleared = (nc.alloc_semaphore("t_" + n) for n in ("zeros_set", "cleared"))
        block = own.enter_context(nc.Block())

        @block.vector
        def _(dve):
            nc.vector.memset(zeros[:], 0.0).then_inc(zeros_set, 1)

        @block.sync
        def _(sp):
            sp.wait_ge(zeros_set, 1)
            for table in (R["atable"], R["btable"]):
                n = table.shape[0] // P
                sp.dma_start(table.rearrange("(p a) d -> p a d", p=P), zeros[:].unsqueeze(1).to_broadcast([P, n, D])).then_inc(cleared, 16)
            sp.wait_ge(cleared, 32)


def store_acc(nc, ctx, R, out):
    with ExitStack() as own:
        stored = nc.alloc_semaphore("stored")
        block = own.enter_context(nc.Block())

        @block.sync
        def _(sp):
            sp.dma_start(out.rearrange("b (t p) d -> p (b t) d", p=P), R["acc"][:]).then_inc(stored, 16)
            sp.wait_ge(stored, 16)


@contextmanager
def signals_of_a_part(nc):
    before = nc.snapshot_sems()
    yield
    nc.clear_and_free_semaphores(nc.allocated_since(before))
    nc.all_engine_barrier()


def two_layers(nc, A, out):
    E0, K0, E1 = A["gW"].shape[1], 3, A["w_router"].shape[0]
    tiles0, tiles1 = whole(most_tiles(K0 * B * L, E0)), whole(most_tiles(B * L, E1))
    CF0, CS = A["rb1"].shape[1] // P, A["sb1"].shape[1] // P

    def dram(name, shape, dt=F32):
        return nc.dram_tensor(name, shape, dt).ap()

    with ExitStack() as ctx:
        R = {}

        def keep(scope, name, shape, dt=F32, tag="sb"):
            R[name] = scope.enter_context(nc.sbuf_tensor(name + "_" + tag, shape, dt))

        keep(ctx, "ident", [P, P])
        keep(ctx, "identb", [P, P], BF16)
        keep(ctx, "acc", [P, NT, D])
        for tag, E, K, tiles in (("a", E0, K0, tiles0), ("b", E1, 1, tiles1)):
            keep(ctx, tag + "gate", [P, K, NT])
            keep(ctx, tag + "slot", [P, K, NT], I32)
            keep(ctx, tag + "chosen", [P, NT, E])
            keep(ctx, tag + "owner", [P, tiles], I32)
            R[tag + "table"] = dram(tag + "_table", [tiles * P, D])
            R[tag + "answers"] = dram(tag + "_answers", [tiles * P, D])
        R["q_dram"], R["k_dram"] = dram("q_parts", [B, 3, P, L], BF16), dram("k_parts", [B, 3, P, L], BF16)
        R["at_dram"], R["nm_dram"] = dram("heads_out", [2, L * D]), dram("max_rows", [2, 3 * HH, L], BF16)

        clear_tables(nc, ctx, R)
        with ExitStack() as first, signals_of_a_part(nc):
            keep(first, "xn", [P, NT, D])
            keep(first, "xnT", [P, B * L])
            keep(first, "logits", [P, NT, E0])
            keep(first, "weights", [P, NT, E0])
            with ExitStack() as heads:
                keep(heads, "v", [P, NT, D])
                keep(heads, "qs", [P, 2, H, L], BF16)
                keep(heads, "ks", [P, 2, H, L], BF16)
                norm_and_project(nc, ctx, A, R)
                attention(nc, ctx, A, R)
            keep(first, "gates", [P, NT, E0 + 1])
            keep(first, "b1T", [P, E0 * CF0 + CS])
            keep(first, "b2", [E0 + 1, D])
            keep(first, "sw1", [P, CS * P])
            keep(first, "sw2", [P, CS, D])
            softmax_weights(nc, ctx, R, E0)
            route(nc, ctx, R, "a", R["weights"][:], E0, K0, tiles0)
            scatter_rows(nc, ctx, "a", R["aslot"], R["xn"], K0, R["atable"])
            expert_biases(nc, ctx, A, R, E0)
            shared_expert(nc, ctx, R, E0)
            expert_tiles(nc, ctx, R, "a", tiles0, E0, A["rW1"], A["rW2"], R["atable"], R["aanswers"], False)
            gather_rows(nc, ctx, R, "a", R["aslot"], K0, R["aanswers"])
        with ExitStack() as states:
            keep(states, "u", [P, NC, B * L])
            keep(states, "g", [P, NC, B * L])
            keep(states, "A_log", [P, NC, NS])
            keep(states, "A_neg", [P, NC, NS])
            with ExitStack() as rows:
                keep(rows, "xn", [P, NT, D], tag="second")
                keep(rows, "xnT", [P, B * L], tag="second")
                keep(rows, "logits2", [P, NT, E1])
                norm_and_mix(nc, ctx, A, R)
                route(nc, ctx, R, "b", R["logits2"][:], E1, 1, tiles1)
                scale_rows(nc, ctx, R)
                scatter_rows(nc, ctx, "b", R["bslot"], R["xn"], 1, R["btable"])
                shared_gated(nc, ctx, A, R)
            keep(states, "delta", [P, NC, B * L])
            keep(states, "bc", [3 * 2 * NS, B * L], BF16)
            step_sizes(nc, ctx, A, R)
            state_space(nc, ctx, A, R)
        expert_tiles(nc, ctx, R, "b", tiles1, E1, A["gate_up"], A["down"], R["btable"], R["banswers"], True)
        gather_rows(nc, ctx, R, "b", R["bslot"], 1, R["banswers"])
        store_acc(nc, ctx, R, out)


_INS = {
    "x": "L0_attn_x", "Wqkv": "L0_attn_W_qkv", "bqkv": "L0_attn_b_qkv",
    "sW1": "L0_ffn_sW1", "sb1": "L0_ffn_sb1", "sW2": "L0_ffn_sW2", "sb2": "L0_ffn_sb2",
    "rW1": "L0_ffn_rW1", "rb1": "L0_ffn_rb1", "rW2": "L0_ffn_rW2", "rb2": "L0_ffn_rb2",
    "gW": "L0_ffn_gW", "gb": "L0_ffn_gb",
    "norm_w": "L1_attn_norm_w", "norm_b": "L1_attn_norm_b", "in_proj_w": "L1_attn_in_proj_w",
    "conv_w": "L1_attn_conv_w", "conv_b": "L1_attn_conv_b", "x_proj_w": "L1_attn_x_proj_w",
    "dt_proj_w": "L1_attn_dt_proj_w", "dt_proj_b": "L1_attn_dt_proj_b", "A_log": "L1_attn_A_log",
    "D_param": "L1_attn_D_param", "out_proj_w": "L1_attn_out_proj_w",
    "w_router": "L1_ffn_w_router", "gate_up": "L1_ffn_gate_up_proj", "down": "L1_ffn_down_proj",
    "w_gate": "L1_ffn_w_gate", "w_up": "L1_ffn_w_up", "w_down": "L1_ffn_w_down",
}


def kernel(**inputs):
    import numpy as _np
    import concourse.bacc as _bacc
    from concourse import mybir as _mybir
    from concourse.bass_utils import run_bass_kernel_spmd as _run

    nc = _bacc.Bacc("TRN2", target_bir_lowering=False, num_devices=1)
    arrays, args = {}, {}
    for short, name in _INS.items():
        a = _np.ascontiguousarray(inputs[name])
        arrays[f"in_{name}"] = a
        args[short] = nc.dram_tensor(f"in_{name}", a.shape, _mybir.dt.from_np(a.dtype), kind="ExternalInput").ap()
    out = nc.dram_tensor("out_x", [B, L, D], F32, kind="ExternalOutput").ap()
    two_layers(nc, args, out)
    r = _run(nc, [arrays], core_ids=[0])
    return r.results[0]["out_x"]
```

```python
import concourse.bass as bass
from concourse import mybir
from contextlib import ExitStack, contextmanager

F32 = mybir.dt.float32
BF16 = mybir.dt.bfloat16
I32 = mybir.dt.int32
ALU = mybir.AluOpType
ACT = mybir.ActivationFunctionType
AX = mybir.AxisListType

P = 128
B, L, D = 8, 512, 128
T = L // P
NT = B * T
H, HD = 16, 8
LN_EPS = 1e-5

Q_ROWS = [0, 0, 0, 1, 1, 2]
K_ROWS = [0, 1, 2, 0, 1, 0]
SR = 96
MR = SR + 3
HH = H // 2
VW = 32


class Chain:

    def __init__(self, eng, sem, base=0):
        self.eng, self.sem, self.base, self.n = eng, sem, base, 0

    def add(self, ins):
        ins.then_inc(self.sem, 1)
        self.n += 1

    def settle(self):
        self.eng.wait_ge(self.sem, self.base + self.n)


def scatter_rows(nc, R, tag, slot, tiles, sent):
    for t in tiles:
        for k in range(slot.shape[1]):
            nc.gpsimd.indirect_dma_start(
                out=R[tag + "table"], out_offset=bass.IndirectOffsetOnAxis(ap=slot[:, k, t:t + 1], axis=0),
                in_=R["xn"][:, t], in_offset=None).then_inc(sent, 16)


def gather_rows(nc, R, tag, slot, b, got, arrived):
    K = slot.shape[1]
    for t in range(T):
        for k in range(K):
            nc.gpsimd.indirect_dma_start(
                out=got[:, t * K + k], out_offset=None, in_=R[tag + "answers"],
                in_offset=bass.IndirectOffsetOnAxis(ap=slot[:, k, b * T + t:b * T + t + 1], axis=0)).then_inc(arrived, 16)


def norm_and_project(nc, ctx, A, R):
    with ExitStack() as own:
        def sb(name, shape, dt):
            return own.enter_context(nc.sbuf_tensor(name, shape, dt))

        def ps(name, shape, dt=F32):
            return own.enter_context(nc.psum_tensor(name, shape, dt))

        def sem(name):
            return nc.alloc_semaphore(name)

        E = A["gW"].shape[1]
        x_t = sb("x_t", [P, 2, T, D], F32)
        xc_t = sb("xc_t", [P, 2, T, D], F32)
        sq_t = sb("sq_t", [P, 2, T, D], F32)
        xn_t = sb("xn_t", [P, 2, T, D], F32)
        xT_t = sb("xT_t", [P, 2, L], F32)
        stat = sb("stat", [P, 2, 4, T], F32)
        minus_half = sb("minus_half", [P, T], F32)
        zeros = sb("zeros", [P, D], F32)
        qk_f = R["aw1"][:].rearrange("p e f -> p (e f)")[:, 0:4 * L].rearrange("p (u n t) -> p u n t", u=2, n=2)
        qk_r = sb("qk_r", [P, 2, 2, L], F32)
        qk_p = sb("qk_p", [P, 2, 2, 3, L], BF16)
        wqkv = sb("wqkv", [P, 3 * D], F32)
        wqk = sb("wqk", [P, 2, D], F32)
        gw = sb("gw", [P, E], F32)
        bqk = sb("bqk", [P, 2], F32)
        bv = sb("bv", [P, D], F32)
        gb = sb("gb", [P, E], F32)
        p_T = ps("p_T", [P, L])
        p_q = ps("p_q", [P, L])
        p_k = ps("p_k", [P, L])
        p_v = ps("p_v", [P, T, D])
        p_g = ps("p_g", [P, T, E])

        ident_set = sem("ident_set")
        weights_in = sem("weights_in")
        x_in = [sem(f"x_in{u}") for u in range(2)]
        xc_done, sq_done, xn_done, a_dve = sem("xc_done"), sem("sq_done"), sem("xn_done"), sem("a_dve")
        T_done, T_kept, q_done, k_done, vg_done = sem("T_done"), sem("T_kept"), sem("q_done"), sem("k_done"), sem("vg_done")
        part1, rest1, part2, part3 = sem("part1"), sem("rest1"), sem("part2"), sem("part3")
        stacks_zero, zeros_set = sem("stacks_zero"), sem("zeros_set")
        half_set, w_turned = sem("half_set"), sem("w_turned")
        a_act, rstd_done = sem("a_act"), sem("rstd_done")
        kept = sem("kept")
        vg_kept = sem("vg_kept")
        qk_out = [sem(f"qk_out{u}") for u in range(2)]

        x_d = A["x"].rearrange("b (t p) d -> b p t d", p=P)
        block = own.enter_context(nc.Block())

        @block.sync
        def _(sp):
            sp.dma_start(wqkv[:], A["Wqkv"]).then_inc(weights_in, 16)
            sp.dma_start(gw[:], A["gW"]).then_inc(weights_in, 16)
            for n in range(2):
                for c in range(HD):
                    sp.dma_start(bqk[H * c:H * (c + 1), n:n + 1],
                                 A["bqkv"][n * D:(n + 1) * D].rearrange("(h c) -> c h", c=HD)[c].unsqueeze(1),
                                 allow_slow_non_contiguous=True).then_inc(weights_in, 16)
            sp.dma_start(bv[:], A["bqkv"][2 * D:3 * D].partition_broadcast(P)).then_inc(weights_in, 16)
            sp.dma_start(gb[:], A["gb"].partition_broadcast(P)).then_inc(weights_in, 16)

            def load_x(i, u, first):
                b = i * 2 + u
                if not first:
                    sp.wait_ge(kept, b * 3 - 3)
                sp.dma_start(x_t[:, u], x_d[bass.ds(b, 1)].rearrange("o p t d -> (o p) t d")).then_inc(x_in[u], 16)

            def store_qk(i, u):
                b = i * 2 + u
                sp.wait_ge(part3, b + 1)
                for n, dst in ((0, R["q_dram"]), (1, R["k_dram"])):
                    sp.dma_start(dst[bass.ds(b, 1)].rearrange("o c p t -> (o p) c t"), qk_p[:, u, n]).then_inc(qk_out[u], 16)

            load_x(0, 0, True)
            load_x(0, 1, True)
            with sp.Fori(1, B // 2) as i:
                for u in range(2):
                    load_x(i, u, False)
                    store_qk(i - 1, u)
            sp.wait_ge(zeros_set, 1)
            for table in (R["atable"], R["btable"]):
                n = table.shape[0] // P
                sp.dma_start(table.rearrange("(p a) d -> p a d", p=P),
                             zeros[:].unsqueeze(1).to_broadcast([P, n, D])).then_inc(R["cleared"], 16)
            for u in range(2):
                store_qk(B // 2 - 1, u)
            for u in range(2):
                sp.wait_ge(qk_out[u], 32 * (B // 2))
            sp.wait_ge(R["cleared"], 32)

        @block.gpsimd
        def _(pool):
            ident = R["ident"]
            nc.gpsimd.memset(minus_half[:], -0.5).then_inc(half_set, 1)
            nc.gpsimd.memset(zeros[:], 0.0).then_inc(zeros_set, 1)
            pool.wait_ge(half_set, 1)
            nc.gpsimd.memset(ident[:], 0.0).then_inc(ident_set, 1)
            pool.wait_ge(ident_set, 1)
            nc.gpsimd.affine_select(out=ident[:], in_=ident[:], compare_op=ALU.not_equal, fill=1.0, base=0,
                                    pattern=[[-1, P]], channel_multiplier=1).then_inc(ident_set, 1)
            for n, stacks in enumerate((R["qs"], R["ks"])):
                nc.gpsimd.memset(stacks[:].bitcast(F32), 0.0).then_inc(stacks_zero, 1)
            pool.wait_ge(weights_in, 16 * (4 + 2 * HD))
            for n in range(2):
                nc.gpsimd.tensor_copy(wqk[:, n].rearrange("k (c h) -> k c h", c=HD),
                                      wqkv[:, n * D:(n + 1) * D].rearrange("k (h c) -> k c h", c=HD)).then_inc(w_turned, 1)
            with pool.Fori(0, B // 2) as i:
                for u in range(2):
                    b = i * 2 + u
                    rows = bass.ds(b * T, T)
                    pool.wait_ge(a_dve, b * 5 + 4)
                    nc.gpsimd.tensor_tensor(stat[:, u, 3], stat[:, u, 1], minus_half[:], ALU.pow).then_inc(rstd_done, 1)
                    pool.wait_ge(xn_done, b + 1)
                    nc.gpsimd.tensor_tensor(R["acc"][:, rows, :], x_t[:, u], xn_t[:, u], ALU.add).then_inc(kept, 1)
                    nc.gpsimd.tensor_copy(R["xn"][:, rows, :], xn_t[:, u]).then_inc(kept, 1)
                    pool.wait_ge(T_kept, b + 1)
                    nc.gpsimd.tensor_copy(R["xnT"][:, bass.ds(b * L, L)], xT_t[:, u]).then_inc(kept, 1)

        @block.vector
        def _(dve):
            dve.wait_ge(weights_in, 16 * (4 + 2 * HD))
            STEPS = 5

            def batch(i, u, first):
                b = i * 2 + u
                own_steps = Chain(dve, a_dve, b * STEPS)
                dve.wait_ge(x_in[u], i * 16 + 16)
                own_steps.add(nc.vector.tensor_reduce(stat[:, u, 1], x_t[:, u], AX.X, ALU.add))
                own_steps.settle()
                own_steps.add(nc.vector.tensor_scalar(stat[:, u, 0], stat[:, u, 1], 1.0 / D, None, ALU.mult))
                own_steps.settle()
                nc.vector.tensor_tensor(xc_t[:, u], x_t[:, u], stat[:, u, 0].unsqueeze(2).to_broadcast([P, T, D]),
                                        ALU.subtract).then_inc(xc_done, 1)
                dve.wait_ge(sq_done, b + 1)
                own_steps.add(nc.vector.tensor_reduce(stat[:, u, 2], sq_t[:, u], AX.X, ALU.add))
                own_steps.settle()
                own_steps.add(nc.vector.tensor_scalar(stat[:, u, 1], stat[:, u, 2], 1.0 / D, LN_EPS, ALU.mult, ALU.add))
                own_steps.settle()
                dve.wait_ge(rstd_done, b + 1)
                if not first:
                    dve.wait_ge(kept, b * 3 - 3)
                nc.vector.tensor_tensor(xn_t[:, u], xc_t[:, u], stat[:, u, 3].unsqueeze(2).to_broadcast([P, T, D]),
                                        ALU.mult).then_inc(xn_done, 1)
                dve.wait_ge(part1, b + 1)
                nc.vector.tensor_tensor(qk_r[:, u], qk_f[:, u], qk_p[:, u, :, 0], ALU.subtract).then_inc(rest1, 1)
                dve.wait_ge(vg_done, b + 1)
                own_steps.add(nc.vector.tensor_tensor(R["v"][:, bass.ds(b * T, T), :], p_v[:],
                                                      bv[:].unsqueeze(1).to_broadcast([P, T, D]), ALU.add))
                nc.vector.tensor_tensor(R["logits"][:, bass.ds(b * T, T), :], p_g[:],
                                        gb[:].unsqueeze(1).to_broadcast([P, T, E]), ALU.add).then_inc(vg_kept, 1)
                dve.wait_ge(part2, b + 1)
                nc.vector.tensor_tensor(qk_p[:, u, :, 2], qk_r[:, u], qk_p[:, u, :, 1], ALU.subtract).then_inc(part3, 1)
                assert own_steps.n == STEPS

            for u in range(2):
                batch(0, u, True)
            with dve.Fori(1, B // 2) as i:
                for u in range(2):
                    batch(i, u, False)

        @block.scalar
        def _(act):
            act.wait_ge(weights_in, 16 * (4 + 2 * HD))

            def batch(i, u, first):
                b = i * 2 + u
                act.wait_ge(xc_done, b + 1)
                nc.scalar.activation(sq_t[:, u], xc_t[:, u], ACT.Square).then_inc(sq_done, 1)
                act.wait_ge(T_done, b + 1)
                if not first:
                    act.wait_ge(kept, b * 3 - 3)
                nc.scalar.activation(xT_t[:, u], p_T[:], ACT.Copy).then_inc(T_kept, 1)
                act.wait_ge(q_done, b + 1)
                nc.scalar.activation(qk_f[:, u, 0], p_q[:], ACT.Identity, bias=bqk[:, 0:1]).then_inc(a_act, 1)
                act.wait_ge(k_done, b + 1)
                nc.scalar.activation(qk_f[:, u, 1], p_k[:], ACT.Identity, bias=bqk[:, 1:2]).then_inc(a_act, 1)
                act.wait_ge(a_act, b * 2 + 2)
                if not first:
                    act.wait_ge(qk_out[u], i * 32)
                nc.scalar.activation(qk_p[:, u, :, 0], qk_f[:, u], ACT.Copy).then_inc(part1, 1)
                act.wait_ge(rest1, b + 1)
                nc.scalar.activation(qk_p[:, u, :, 1], qk_r[:, u], ACT.Copy).then_inc(part2, 1)

            for u in range(2):
                batch(0, u, True)
            with act.Fori(1, B // 2) as i:
                for u in range(2):
                    batch(i, u, False)

        @block.tensor
        def _(pe):
            pe.wait_ge(ident_set, 2)
            pe.wait_ge(weights_in, 16 * (4 + 2 * HD))
            pe.wait_ge(w_turned, 2)
            with pe.Fori(0, B // 2) as i:
                for u in range(2):
                    b = i * 2 + u
                    pe.wait_ge(xn_done, b + 1)
                    for t in range(T):
                        last = nc.tensor.transpose(p_T[:, t * P:(t + 1) * P], xn_t[:, u, t], R["ident"][:])
                    last.then_inc(T_done, 1)
                    pe.wait_ge(T_kept, b + 1)
                    nc.tensor.matmul(p_q[:], wqk[:, 0], xT_t[:, u], start=True, stop=True).then_inc(q_done, 1)
                    nc.tensor.matmul(p_k[:], wqk[:, 1], xT_t[:, u], start=True, stop=True).then_inc(k_done, 1)
                    for t in range(T):
                        nc.tensor.matmul(p_v[:, t], xT_t[:, u, t * P:(t + 1) * P], wqkv[:, 2 * D:3 * D], start=True, stop=True)
                    for t in range(T):
                        last = nc.tensor.matmul(p_g[:, t], xT_t[:, u, t * P:(t + 1) * P], gw[:], start=True, stop=True)
                    last.then_inc(vg_done, 1)
                    pe.wait_ge(a_act, b * 2 + 2)
                    pe.wait_ge(vg_kept, b + 1)


def attention(nc, ctx, A, R):
    with ExitStack() as own:
        def sb(name, shape, dt):
            return own.enter_context(nc.sbuf_tensor(name, shape, dt))

        def ps(name, shape, dt=F32):
            return own.enter_context(nc.psum_tensor(name, shape, dt))

        def sem(name):
            return nc.alloc_semaphore(name)

        qs, ks = R["qs"], R["ks"]
        ones = sb("ones", [3, L], BF16)
        va = sb("va", [P, 2, T, H, VW], F32)
        pr = sb("pr", [P, 2, 4, L], F32)
        os_t = sb("os_t", [P, L], F32)
        rden = sb("rden", [P, T, 4], F32)
        at = sb("at", [P, 2, H, T, HD], F32)
        att = sb("att", [P, 2, T, D], F32)
        nmax = sb("nmax", [P, T, H], F32)
        nres = sb("nres", [P, T, HH], F32)
        nmp = sb("nmp", [P, T, 3, HH], BF16)
        nmT = sb("nmT", [3 * HH, L], BF16)
        p_st = ps("p_st", [P, 2, 2, L])
        p_s = ps("p_s", [P, 2, L])
        p_o = ps("p_o", [P, L])
        p_m = ps("p_m", [P, L])
        p_to = p_m[:].rearrange("p (t g c) -> p t g c", t=T, g=4)
        p_nm = p_m[0:3 * HH, 0:L // 2].bitcast(BF16)

        stacked = [[sem(f"stacked{u}{h}") for h in range(2)] for u in range(2)]
        ones_set, ones_in, va_zero, va_set = sem("ones_set"), sem("ones_in"), sem("va_zero"), sem("va_set")
        s_done, max_done = sem("s_done"), sem("max_done")
        st_done, exp_done, pv_done = sem("st_done"), sem("exp_done"), sem("pv_done")
        o_kept, to_done, at_done, added = sem("o_kept"), sem("to_done"), sem("at_done"), sem("added")
        at_out, at_in = sem("at_out"), sem("at_in")
        b_dve_r = sem("b_dve_r")
        b_dve, parts_done, nmT_done, nmT_kept, nm_out = (
            sem("b_dve"), sem("parts_done"), sem("nmT_done"), sem("nmT_kept"), sem("nm_out"))
        nm_in = [sem(f"nm_in{h}") for h in range(2)]
        identb_set, scattered, loaded = sem("identb_set"), sem("scattered"), sem("aloaded")

        UNITS = 4 * T
        SCORES = H * T
        ROW_RUNS = [(0, 3), (3, 5), (5, 6)]
        LOADS = 2 * len(ROW_RUNS) * 16
        q_v = R["q_dram"].rearrange("b c (p h) t -> b c p (h t)", p=HD)
        k_v = R["k_dram"].rearrange("b c (p h) t -> b c p (h t)", p=HD)
        block = own.enter_context(nc.Block())

        @block.sync
        def _(sp):
            def stack(b, u, hf):
                hs, cols = slice(hf * HH, (hf + 1) * HH), slice(hf * HH * L, (hf + 1) * HH * L)
                for src, dst, rows in ((q_v, qs, Q_ROWS), (k_v, ks, K_ROWS)):
                    for lo, hi in ROW_RUNS:
                        c = rows[lo]
                        if rows[hi - 1] == c:
                            part = src[bass.ds(b, 1), c, :, cols].to_broadcast([hi - lo, HD, HH * L])
                        else:
                            part = src[bass.ds(b, 1), c:c + hi - lo, :, cols].rearrange("o c p t -> (o c) p t")
                        sp.dma_start(dst[HD * lo:HD * hi, u, hs].rearrange("p h t -> p (h t)"), part).then_inc(stacked[u][hf], 16)

            def place_max(b, u, h, n):
                sp.wait_ge(nmT_kept, n)
                sp.dma_start(R["nm_dram"][h], nmT[:]).then_inc(nm_out, 16)
                sp.wait_ge(nm_out, n * 16)
                sp.dma_start(qs[SR:MR, u, h * HH:(h + 1) * HH],
                             R["nm_dram"][h].rearrange("(c j) t -> c j t", c=3)).then_inc(nm_in[h], 16)

            for u in range(2):
                for hf in range(2):
                    stack(u, u, hf)
            sp.wait_ge(ones_set, 1)
            for u in range(2):
                sp.dma_start(ks[SR:MR, u], ones[:].unsqueeze(1).to_broadcast([3, H, L])).then_inc(ones_in, 16)
            for h in range(2):
                place_max(0, 0, h, 1 + h)
            load_first(sp, R, "a", A["rW1"], loaded)

            def reshape_out(b, u, first):
                if not first:
                    sp.wait_ge(added, b - 1)
                sp.wait_ge(at_done, b * 4 + 4)
                sp.dma_start(R["at_dram"][u].rearrange("(h p c) -> p h c", h=H, p=P),
                             at[:, u].rearrange("p h t c -> p h (t c)")).then_inc(at_out, 16)
                sp.wait_ge(at_out, b * 16 + 16)
                sp.dma_start(att[:, u], R["at_dram"][u].rearrange("(t p d) -> p t d", t=T, p=P)).then_inc(at_in, 16)

            def batch(b, u, first=False, maxima=True, stacks=True):
                for hf in range(2):
                    if stacks:
                        sp.wait_ge(pv_done, b * UNITS + (hf + 1) * (UNITS // 2))
                        stack(b + 2, u, hf)
                    if maxima:
                        place_max(b + 1, 1 - u, hf, b * 2 + 3 + hf)
                reshape_out(b, u, first)

            for u in range(2):
                batch(u, u, first=True)
            with sp.Fori(1, B // 2 - 1) as i:
                for u in range(2):
                    batch(i * 2 + u, u)
            batch(B - 2, 0, stacks=False)
            batch(B - 1, 1, maxima=False, stacks=False)
            sp.wait_ge(loaded, 16)

        @block.gpsimd
        def _(pool):
            nc.gpsimd.memset(ones[:], 1.0).then_inc(ones_set, 1)
            nc.gpsimd.tensor_copy(R["identb"][:], R["ident"][:]).then_inc(identb_set, 1)
            nc.gpsimd.memset(va[:], 0.0).then_inc(va_zero, 1)
            pool.wait_ge(va_zero, 1)
            nc.gpsimd.memset(va[:, :, :, :, HD], 1.0).then_inc(va_zero, 1)

            def place_v(b, u):
                nc.gpsimd.tensor_copy(va[:, u, :, :, 0:HD],
                                      R["v"][:, bass.ds(b * T, T), :].rearrange("p t (h c) -> p t h c", c=HD)).then_inc(va_set, 1)

            def batch(b, u, more):
                rows = bass.ds(b * T, T)
                pool.wait_ge(at_in, b * 16 + 16)
                nc.gpsimd.tensor_tensor(R["acc"][:, rows, :], R["acc"][:, rows, :], att[:, u], ALU.add).then_inc(added, 1)
                if more:
                    place_v(b + 2, u)

            pool.wait_ge(va_zero, 2)
            place_v(0, 0)
            place_v(1, 1)
            cuts = [0, NT // 2, 3 * NT // 4, NT]
            scatter_rows(nc, R, "a", R["aslot"], range(cuts[0], cuts[1]), scattered)
            for u in range(2):
                batch(u, u, True)
                scatter_rows(nc, R, "a", R["aslot"], range(cuts[u + 1], cuts[u + 2]), scattered)
            with pool.Fori(1, B // 2 - 1) as i:
                for u in range(2):
                    batch(i * 2 + u, u, True)
            for u in range(2):
                batch(B - 2 + u, u, False)
            pool.wait_ge(scattered, 16 * R["aslot"].shape[1] * NT)

        @block.tensor
        def _(pe):
            def max_scores(b, u, n, first=False):
                h, t = n // T, n % T
                if not (first and n < 2):
                    pe.wait_ge(max_done, b * SCORES + n - 1)
                q, k = qs[0:SR, u, h], ks[0:SR, u, h]
                nc.tensor.matmul(p_s[:, n % 2], q[:, t::T], k, start=True, stop=True).then_inc(s_done, 1)

            def turn_max(b, hf, turned):
                pe.wait_ge(parts_done, b * 2 + hf + 1)
                if turned is not None:
                    pe.wait_ge(at_done, turned)
                elif hf:
                    pe.wait_ge(nmT_kept, 1)
                for t in range(T):
                    last = nc.tensor.transpose(p_nm[:, t * P:(t + 1) * P], nmp[:, t].rearrange("p c h -> p (c h)"),
                                               R["identb"][:])
                last.then_inc(nmT_done, 1)

            def scores(b, u, w, n, first):
                g, t, x, y = w // T, w % T, n // 2, n % 2
                if y == 0 and not (first and w == 0):
                    pe.wait_ge(exp_done, b * (2 * UNITS) + 2 * w + x - 1)
                h = 4 * g + n
                q, k = qs[:, u, h], ks[:, u, h]
                last = nc.tensor.matmul(p_st[:, x, y], k[:, t * P:(t + 1) * P], q, start=True, stop=True)
                if y == 1:
                    last.then_inc(st_done, 1)

            def products(b, u, w, first):
                g, t = w // T, w % T
                if t == 0 and not (first and g == 0):
                    pe.wait_ge(o_kept, b * 4 + g)
                pe.wait_ge(exp_done, b * (2 * UNITS) + 2 * w + 2)
                for y in range(4):
                    last = nc.tensor.matmul(p_o[VW * y:VW * (y + 1)], va[:, u, t, 4 * g + y], pr[:, w % 2, y],
                                            start=t == 0, stop=t == T - 1, tile_position=(0, VW * y))
                last.then_inc(pv_done, 1)

            def turn_out(b, g, more):
                pe.wait_ge(o_kept, b * 4 + g + 1)
                if g == 0:
                    pe.wait_ge(nmT_kept, b * 2 + 2)
                if g > 1 and more:
                    pe.wait_ge(nmT_kept, b * 2 + g + 1)
                if not (g == 0 and isinstance(b, int) and b == 0):
                    pe.wait_ge(at_done, b * 4 + g)
                for t in range(T):
                    last = nc.tensor.transpose(p_m[:, t * P:(t + 1) * P], os_t[:, t::T], R["ident"][:])
                last.then_inc(to_done, 1)

            def batch(b, u, i, first, more):
                for w in range(UNITS):
                    if w == 0:
                        pe.wait_ge(nm_in[0], b * 16 + 16)
                        pe.wait_ge(va_set, b + 1)
                        if more:
                            pe.wait_ge(stacked[1 - u][0], (i + u) * LOADS + LOADS)
                    if w == UNITS // 2:
                        if more:
                            pe.wait_ge(stacked[1 - u][1], (i + u) * LOADS + LOADS)
                        pe.wait_ge(nm_in[1], b * 16 + 16)
                    for n in range(4):
                        scores(b, u, w, n, first)
                        if more and n > 0:
                            max_scores(b + 1, 1 - u, 4 * w + n - 1)
                    if w > 0:
                        products(b, u, w - 1, first)
                    if w % T == 1 and w > T:
                        turn_out(b, w // T - 1, more)
                    if more:
                        max_scores(b + 1, 1 - u, 4 * w + 3)
                        if w == UNITS // 2 + 3:
                            turn_max(b + 1, 0, b * 4 + 2)
                products(b, u, UNITS - 1, first)
                if more:
                    turn_max(b + 1, 1, b * 4 + 3)
                turn_out(b, 3, more)

            pe.wait_ge(identb_set, 1)
            pe.wait_ge(ones_in, 32)
            for hf in range(2):
                pe.wait_ge(stacked[0][hf], LOADS)
            for n in range(SCORES):
                max_scores(0, 0, n, first=True)
                if n == SCORES // 2 + 4:
                    turn_max(0, 0, None)
            turn_max(0, 1, None)
            batch(0, 0, 0, True, True)
            batch(1, 1, 0, False, True)
            with pe.Fori(1, B // 2 - 1) as i:
                for u in range(2):
                    batch(i * 2 + u, u, i, False, True)
            batch(B - 2, 0, B // 2 - 1, False, True)
            batch(B - 1, 1, B // 2 - 1, False, False)

        @block.scalar
        def _(act):
            def batch(b, first):
                for w in range(UNITS):
                    for x in range(2):
                        act.wait_ge(st_done, b * (2 * UNITS) + 2 * w + x + 1)
                        if x == 0 and not (first and w < 2):
                            act.wait_ge(pv_done, b * UNITS + w - 1)
                        nc.scalar.activation(pr[:, w % 2, 2 * x:2 * x + 2], p_st[:, x], ACT.Exp).then_inc(exp_done, 1)

            batch(0, True)
            with act.Fori(1, B) as b:
                batch(b, False)

        @block.vector
        def _(dve):
            STEPS = 8

            def maxima(b, n):
                h, t = n // T, n % T
                dve.wait_ge(s_done, b * SCORES + n + 1)
                nc.vector.tensor_reduce(nmax[:, t, h:h + 1], p_s[:, n % 2], AX.X, ALU.max,
                                        negate=True).then_inc(max_done, 1)

            def split_max(b, hf, steps):
                m, rest = nmax[:, :, hf * HH:(hf + 1) * HH], nres[:]
                part = [nmp[:, :, c] for c in range(3)]
                dve.wait_ge(max_done, b * SCORES + (hf + 1) * (SCORES // 2))
                steps.add(nc.vector.tensor_copy(part[0], m))
                steps.settle()
                steps.add(nc.vector.tensor_tensor(rest, m, part[0], ALU.subtract))
                steps.settle()
                steps.add(nc.vector.tensor_copy(part[1], rest))
                steps.settle()
                nc.vector.tensor_tensor(part[2], rest, part[1], ALU.subtract).then_inc(parts_done, 1)

            def keep_max(b, hf, first=False):
                dve.wait_ge(nmT_done, b * 2 + hf + 1)
                if not (first and hf == 0):
                    dve.wait_ge(nm_out, (b * 2 + hf) * 16)
                nc.vector.tensor_copy(nmT[:].rearrange("m (q t) -> m t q", t=T),
                                      p_nm.rearrange("m (t q) -> m t q", t=T)).then_inc(nmT_kept, 1)

            def keep_out(b, g):
                dve.wait_ge(pv_done, b * UNITS + (g + 1) * T)
                if isinstance(b, int) and b == 0 and g == 0:
                    pass
                else:
                    dve.wait_ge(to_done, b * 4 + g)
                nc.vector.tensor_copy(os_t[:], p_o[:]).then_inc(o_kept, 1)

            def normalize(b, u, g, first):
                dve.wait_ge(to_done, b * 4 + g + 1)
                if g == 0 and not first:
                    dve.wait_ge(at_out, b * 16 - 16)
                nc.vector.reciprocal(rden[:], p_to[:, :, :, HD]).then_inc(b_dve_r, 1)
                dve.wait_ge(b_dve_r, b * 4 + g + 1)
                nc.vector.tensor_tensor(at[:, u, 4 * g:4 * g + 4], p_to[:, :, :, 0:HD].rearrange("p t g c -> p g t c"),
                                        rden[:].rearrange("p t g -> p g t").unsqueeze(3).to_broadcast([P, 4, T, HD]),
                                        ALU.mult).then_inc(at_done, 1)

            def batch(b, u, first, more):
                steps = Chain(dve, b_dve, b * 6 + 6)
                for w in range(UNITS):
                    if more:
                        for n in range(3):
                            maxima(b + 1, 4 * w + n)
                    if w % T == 0 and w > 0:
                        keep_out(b, w // T - 1)
                    if more:
                        maxima(b + 1, 4 * w + 3)
                        if w == UNITS // 2:
                            split_max(b + 1, 0, steps)
                        if w == UNITS // 2 + 4:
                            keep_max(b + 1, 0)
                    if w % T == 1 and w > T:
                        normalize(b, u, w // T - 1, first)
                if more:
                    split_max(b + 1, 1, steps)
                    keep_out(b, 3)
                    keep_max(b + 1, 1)
                    assert steps.n == 6
                else:
                    keep_out(b, 3)
                normalize(b, u, 3, first)

            steps = Chain(dve, b_dve)
            for n in range(SCORES):
                maxima(0, n)
                if n == SCORES // 2 + 2:
                    split_max(0, 0, steps)
                if n == SCORES // 2 + 8:
                    keep_max(0, 0, first=True)
            split_max(0, 1, steps)
            keep_max(0, 1)
            batch(0, 0, True, True)
            batch(1, 1, True, True)
            with dve.Fori(1, B // 2 - 1) as i:
                for u in range(2):
                    batch(i * 2 + u, u, False, True)
            batch(B - 2, 0, False, True)
            batch(B - 1, 1, False, False)


def most_tiles(rows, experts):
    return rows // P - 1 + experts


def route(nc, ctx, R, tag, w, E, K, TILES):
    gate, slot, chosen, owner = R[tag + "gate"], R[tag + "slot"], R[tag + "chosen"], R[tag + "owner"]
    with ExitStack() as own:
        def sb(name, shape, dt=F32):
            return own.enter_context(nc.sbuf_tensor(tag + name, shape, dt))

        def sem(name):
            return nc.alloc_semaphore(tag + name)

        e_no = sb("e_no", [P, NT, E])
        t_rows = sb("t_rows", [P, E, NT])
        tile_no = sb("tile_no", [P, TILES, E])
        below = sb("below", [P, P])
        ones = sb("ones", [P, P])
        left = sb("left", [P, NT, E])
        is_max = sb("is_max", [P, NT, E])
        key = sb("key", [P, NT, E])
        first_key = sb("first_key", [P, NT])
        pick = sb("pick", [P, K, NT, E])
        picked = sb("picked", [P, E, NT])
        total = sb("total", [P, E, NT])
        reset = sb("reset", [P, E, NT])
        run = sb("run", [P, E, NT])
        over = sb("over", [P, E, NT])
        tiles = sb("tiles", [P, E])
        cum = sb("cum", [P, E])
        base = sb("base", [P, E])
        place = sb("place", [P, E, NT])
        prod = sb("prod", [P, NT, E])
        slot_f = sb("slot_f", [P, K, NT])
        owner_f = sb("owner_f", [P, TILES])
        p_rank = own.enter_context(nc.psum_tensor(tag + "p_rank", [P, E, NT], F32))
        p_total = own.enter_context(nc.psum_tensor(tag + "p_total", [P, E, NT], F32))
        tables, chain, picked_set, counted = sem("tables"), sem("chain"), sem("picked_set"), sem("counted")
        block = own.enter_context(nc.Block())

        @block.gpsimd
        def _(pool):
            exact = dict(allow_small_or_imprecise_dtypes=True)
            nc.gpsimd.iota(e_no[:], [[0, NT], [1, E]], base=0, channel_multiplier=0, **exact).then_inc(tables, 1)
            nc.gpsimd.memset(ones[:], 1.0).then_inc(tables, 1)
            nc.gpsimd.memset(reset[:], 1.0).then_inc(tables, 1)
            pool.wait_ge(tables, 3)
            nc.gpsimd.memset(reset[:, :, 0], 0.0).then_inc(tables, 1)
            nc.gpsimd.affine_select(out=below[:], in_=ones[:], compare_op=ALU.is_gt, fill=0.0, base=0,
                                    pattern=[[1, P]], channel_multiplier=-1).then_inc(tables, 1)
            nc.gpsimd.iota(t_rows[:], [[0, E], [P, NT]], base=0, channel_multiplier=0, **exact).then_inc(tables, 1)
            nc.gpsimd.iota(tile_no[:], [[1, TILES], [0, E]], base=0, channel_multiplier=0, **exact).then_inc(tables, 1)

        @block.tensor
        def _(pe):
            pe.wait_ge(tables, 7)
            pe.wait_ge(picked_set, 1)
            nc.tensor.matmul(p_rank[:], below[:], picked[:], start=True, stop=True)
            nc.tensor.matmul(p_total[:], ones[:], picked[:], start=True, stop=True).then_inc(counted, 1)

        @block.vector
        def _(dve):
            steps = Chain(dve, chain)

            def step(ins):
                steps.add(ins)
                steps.settle()

            def by_row(x):
                return x.unsqueeze(2).to_broadcast([P, NT, E])

            tt, stt = nc.vector.tensor_tensor, nc.vector.scalar_tensor_tensor
            dve.wait_ge(tables, 7)
            values = w
            for k in range(K):
                step(nc.vector.tensor_reduce(gate[:, k], values, AX.X, ALU.max))
                step(tt(is_max[:], values, by_row(gate[:, k]), ALU.is_equal))
                step(stt(out=key[:], in0=is_max[:], scalar=-2.0 * E, in1=e_no[:], op0=ALU.mult, op1=ALU.add))
                step(nc.vector.tensor_reduce(first_key[:], key[:], AX.X, ALU.min))
                step(tt(pick[:, k], key[:], by_row(first_key[:]), ALU.is_equal))
                if k < K - 1:
                    step(stt(out=left[:], in0=pick[:, k], scalar=-4.0, in1=values, op0=ALU.mult, op1=ALU.add))
                    values = left[:]
                step(nc.vector.tensor_copy(chosen[:], pick[:, 0]) if k == 0 else
                     tt(chosen[:], chosen[:], pick[:, k], ALU.add))
            nc.vector.tensor_copy(picked[:], chosen[:].rearrange("p t e -> p e t")).then_inc(picked_set, 1)
            dve.wait_ge(counted, 1)
            step(nc.vector.tensor_copy(total[:], p_total[:]))
            step(nc.vector.tensor_tensor_scan(run[:].rearrange("p e t -> p (e t)"), reset[:].rearrange("p e t -> p (e t)"),
                                              total[:].rearrange("p e t -> p (e t)"), 0.0, ALU.mult, ALU.add))
            step(tt(over[:], run[:, :, NT - 1:NT].to_broadcast([P, E, NT]), t_rows[:], ALU.is_gt))
            step(nc.vector.tensor_reduce(tiles[:], over[:], AX.X, ALU.add))
            step(nc.vector.tensor_tensor_scan(cum[:], ones[:, 0:E], tiles[:], 0.0, ALU.mult, ALU.add))
            step(tt(base[:], cum[:], tiles[:], ALU.subtract))
            step(tt(place[:], run[:], total[:], ALU.subtract))
            step(tt(place[:], place[:], p_rank[:], ALU.add))
            step(stt(out=place[:], in0=base[:].unsqueeze(2).to_broadcast([P, E, NT]), scalar=float(P), in1=place[:],
                     op0=ALU.mult, op1=ALU.add))
            for k in range(K):
                step(tt(prod[:], pick[:, k], place[:].rearrange("p e t -> p t e"), ALU.mult))
                step(nc.vector.tensor_reduce(slot_f[:, k], prod[:], AX.X, ALU.add))
            step(nc.vector.tensor_copy(slot[:], slot_f[:]))
            step(tt(tile_no[:], tile_no[:], cum[:].unsqueeze(1).to_broadcast([P, TILES, E]), ALU.is_ge))
            step(nc.vector.tensor_reduce(owner_f[:], tile_no[:], AX.X, ALU.add))
            step(nc.vector.tensor_scalar(owner[:], owner_f[:], float(E - 1), None, ALU.min))


def softmax_weights(nc, ctx, R, E):
    with ExitStack() as own:
        def sem(name):
            return nc.alloc_semaphore(name)

        top = own.enter_context(nc.sbuf_tensor("r_top", [P, 3, NT], F32))
        logits, weights = R["logits"], R["weights"]
        chain, shifted, expd = sem("r_chain"), sem("r_shifted"), sem("r_expd")
        block = own.enter_context(nc.Block())

        def by_row(x):
            return x.unsqueeze(2).to_broadcast([P, NT, E])

        @block.vector
        def _(dve):
            steps = Chain(dve, chain)
            steps.add(nc.vector.tensor_reduce(top[:, 0], logits[:], AX.X, ALU.max))
            steps.settle()
            nc.vector.tensor_tensor(weights[:], logits[:], by_row(top[:, 0]), ALU.subtract).then_inc(shifted, 1)
            dve.wait_ge(expd, 1)
            steps.add(nc.vector.tensor_reduce(top[:, 1], weights[:], AX.X, ALU.add))
            steps.settle()
            steps.add(nc.vector.reciprocal(top[:, 2], top[:, 1]))
            steps.settle()
            nc.vector.tensor_tensor(weights[:], weights[:], by_row(top[:, 2]), ALU.mult)

        @block.scalar
        def _(act):
            act.wait_ge(shifted, 1)
            nc.scalar.activation(weights[:], weights[:], ACT.Exp).then_inc(expd, 1)


GROUP = 4


def whole(tiles):
    return -(-tiles // GROUP) * GROUP


PER_LOAD = 4


def load_first(sp, R, tag, w1_d, loaded):
    sp.dma_start(R[tag + "w1"][:], w1_d.rearrange("e p f -> p e f")).then_inc(loaded, 16)


def load_second(sp, R, tag, w2_d, loaded):
    E, C = w2_d.shape[0], w2_d.shape[1] // P
    starts = range(0, E, PER_LOAD)
    for lo in starts:
        hi = min(lo + PER_LOAD, E)
        sp.dma_start(R[tag + "w2"][:, lo * C:hi * C],
                     w2_d[lo:hi].rearrange("e (c p) d -> p (e c) d", p=P)).then_inc(loaded, 16)
    return len(starts)


def expert_tiles(nc, R, tag, TILES, E, table_in, table_out, gated):
    W1, W2 = R[tag + "w1"], R[tag + "w2"]
    N1 = W1.shape[2]
    C1 = N1 // P
    CF = W2.shape[1] // E
    owner = R[tag + "owner"]
    GROUPS = TILES // GROUP
    with ExitStack() as own:
        def sb(name, shape, dt=F32):
            return own.enter_context(nc.sbuf_tensor(tag + name, shape, dt))

        def sem(name):
            return nc.alloc_semaphore(tag + name)

        xs = sb("xs", [P, 3, GROUP, D])
        xT = sb("xT", [P, 2, GROUP * P])
        w1 = sb("w1t", [P, GROUP, N1])
        w2 = sb("w2t", [P, 3, GROUP, CF, D])
        b1 = None if gated else sb("b1t", [P, 3, GROUP, CF])
        hid = sb("hid", [P, 2, GROUP, CF, P])
        sil = sb("sil", [P, GROUP, CF, P]) if gated else None
        y = sb("y", [P, 3, GROUP, D])
        p_x = own.enter_context(nc.psum_tensor(tag + "p_x", [P, GROUP * P], F32))
        p_h = [own.enter_context(nc.psum_tensor(tag + f"p_h{n}", [P, 4, P], F32)) for n in range(GROUP)]
        p_y = [own.enter_context(nc.psum_tensor(tag + f"p_y{n}", [P, GROUP, D], F32)) for n in range(2)]
        group_in = [sem(f"group_in{n}") for n in range(3)]
        group_out = [sem(f"group_out{n}") for n in range(3)]
        x_turned, x_kept, w1_kept, w2_kept, h_done, sil_done, hid_done, y_done, y_kept = (
            sem(n) for n in ("x_turned", "x_kept", "w1_kept", "w2_kept", "h_done", "sil_done", "hid_done", "y_done", "y_kept"))
        t_in = table_in.rearrange("(j p) d -> p j d", p=P)
        t_out = table_out.rearrange("(j p) d -> p j d", p=P)
        block = own.enter_context(nc.Block())

        def all_groups(eng, group, lo=0, hi=GROUPS):
            loops = hi // 6
            for g in range(lo, 6):
                group(g, g, 0, True)
            if loops > 1:
                with eng.Fori(1, loops) as i:
                    for u in range(6):
                        group(i * 6 + u, u, i, False)
            for g in range(loops * 6, hi):
                group(g, g % 6, g // 6, False)

        @block.sync
        def _(sp):
            def load(g, u, i, first):
                if not (first and u < 3):
                    sp.wait_ge(x_turned, g - 2)
                sp.dma_start(xs[:, u % 3], t_in[:, bass.ds(g * GROUP, GROUP), :]).then_inc(group_in[u % 3], 16)

            def store(g, u, i, first):
                sp.wait_ge(y_kept, g + 1)
                sp.dma_start(t_out[:, bass.ds(g * GROUP, GROUP), :], y[:, u % 3]).then_inc(group_out[u % 3], 16)

            def both(g, u, i, first):
                load(g, u, i, first)
                if not (first and u < 4):
                    store(g - 4, u - 4, i, first)

            all_groups(sp, both)
            for g in range(GROUPS - 4, GROUPS):
                store(g, g % 3, 0, False)
            for n in range(3):
                sp.wait_ge(group_out[n], 16 * len(range(n, GROUPS, 3)))

        @block.tensor
        def _(pe):
            def turn(g, u, i, first):
                pe.wait_ge(group_in[u % 3], i * 32 + (32 if u >= 3 else 16))
                if not (first and u == 0):
                    pe.wait_ge(x_kept, g)
                for n in range(GROUP):
                    last = nc.tensor.transpose(p_x[:, n * P:(n + 1) * P], xs[:, u % 3, n], R["ident"][:])
                last.then_inc(x_turned, 1)

            def hidden(g, u, n, first):
                if n == 0:
                    pe.wait_ge(x_kept, g + 1)
                pe.wait_ge(w1_kept, g * GROUP + n + 1)
                if not (first and u == 0):
                    pe.wait_ge(hid_done, g * GROUP + n - GROUP + 1)
                for c in range(C1):
                    last = nc.tensor.matmul(p_h[n][:, c], w1[:, n, c * P:(c + 1) * P], xT[:, u % 2, n * P:(n + 1) * P],
                                            start=True, stop=True)
                last.then_inc(h_done, 1)

            def product(g, u, n, first):
                pe.wait_ge(hid_done, g * GROUP + n + 1)
                pe.wait_ge(w2_kept, (g * GROUP + n + 1) * (1 if gated else 2))
                if n == 0 and not (first and u < 2):
                    pe.wait_ge(y_kept, g - 1)
                for c in range(CF):
                    last = nc.tensor.matmul(p_y[u % 2][:, n], hid[:, u % 2, n, c], w2[:, u % 3, n, c],
                                            start=c == 0, stop=c == CF - 1)
                if n == GROUP - 1:
                    last.then_inc(y_done, 1)

            def group(g, u, i, first, more=True):
                if more:
                    turn(g + 1, (u + 1) % 6, i + (1 if u == 5 else 0), False)
                before = not (first and u == 0)
                for n in range(GROUP):
                    hidden(g, u, n, first)
                    if before:
                        product(g - 1, (u - 1) % 6, n, first and u > 0)

            turn(0, 0, 0, True)
            all_groups(pe, group, hi=GROUPS - 1)
            group(GROUPS - 1, (GROUPS - 1) % 6, (GROUPS - 1) // 6, False, more=False)
            for n in range(GROUP):
                product(GROUPS - 1, (GROUPS - 1) % 6, n, False)

        @block.scalar
        def _(act):
            def keep_x(g, u, first):
                act.wait_ge(x_turned, g + 1)
                if not (first and u < 2):
                    act.wait_ge(h_done, (g - 1) * GROUP)
                nc.scalar.activation(xT[:, u % 2], p_x[:], ACT.Copy).then_inc(x_kept, 1)

            def keep_y(g, u, i, first):
                act.wait_ge(y_done, g + 1)
                if not (first and u < 3):
                    act.wait_ge(group_out[u % 3], i * 32 + (16 if u >= 3 else 0))
                nc.scalar.activation(y[:, u % 3], p_y[u % 2][:], ACT.Copy).then_inc(y_kept, 1)

            def group(g, u, i, first):
                if not (isinstance(g, int) and g == GROUPS - 1):
                    keep_x(g + 1, (u + 1) % 6, first and u < 5)
                if not (first and u < 2):
                    keep_y(g - 2, (u - 2) % 6, i - (1 if u < 2 else 0), first)
                for n in range(GROUP):
                    act.wait_ge(h_done, g * GROUP + n + 1)
                    if gated:
                        if not (first and u == 0):
                            act.wait_ge(hid_done, g * GROUP + n - GROUP + 1)
                        nc.scalar.activation(sil[:, n], p_h[n][:, 0:CF], ACT.Silu).then_inc(sil_done, 1)
                    else:
                        act.wait_ge(w2_kept, (g * GROUP + n) * 2 + 1)
                        if n == 0 and not (first and u < 2):
                            act.wait_ge(y_done, g - 1)
                        for c in range(CF):
                            last = nc.scalar.activation(hid[:, u % 2, n, c], p_h[n][:, c], ACT.Gelu,
                                                        bias=b1[:, u % 3, n, c:c + 1])
                        last.then_inc(hid_done, 1)

            keep_x(0, 0, True)
            all_groups(act, group)
            g = GROUPS
            keep_y(g - 2, (g - 2) % 6, (g - 2) // 6, False)
            keep_y(g - 1, (g - 1) % 6, (g - 1) // 6, False)

        @block.vector
        def _(dve):
            def copy_weights(g, u, n, e, first):
                if not (first and u == 0):
                    dve.wait_ge(h_done, g * GROUP + n - GROUP + 1)
                nc.vector.tensor_copy(w1[:, n], W1[:, bass.ds(e, 1), :]).then_inc(w1_kept, 1)
                if n == 0 and not (first and u < 3):
                    dve.wait_ge(y_done, g - 2)
                if not gated:
                    nc.vector.tensor_copy(b1[:, u % 3, n], R["b1T"][:, bass.ds(e * CF, CF)]).then_inc(w2_kept, 1)
                nc.vector.tensor_copy(w2[:, u % 3, n], W2[:, bass.ds(e * CF, CF), :]).then_inc(w2_kept, 1)

            def hide(g, u, n, first):
                dve.wait_ge(sil_done, g * GROUP + n + 1)
                if n == 0 and not (first and u < 2):
                    dve.wait_ge(y_done, g - 1)
                nc.vector.tensor_tensor(hid[:, u % 2, n], sil[:, n], p_h[n][:, CF:C1], ALU.mult).then_inc(hid_done, 1)

            def group(g, u, i, first):
                _, e = nc.values_load_multi_w_load_instructions(
                    owner[0:1, bass.ds(g * GROUP, GROUP)], engines=[dve.engine], min_val=0, max_val=E - 1)
                for n in range(GROUP):
                    if gated and not (first and u == 0):
                        hide(g - 1, (u - 1) % 6, n, first and u > 0)
                    copy_weights(g, u, n, e[n], first)

            all_groups(dve, group)
            if gated:
                for n in range(GROUP):
                    hide(GROUPS - 1, (GROUPS - 1) % 6, n, False)


def expert_biases(nc, ctx, A, R, E):
    CF, CS = A["rb1"].shape[1] // P, A["sb1"].shape[1] // P
    with ExitStack() as own:
        rows = own.enter_context(nc.sbuf_tensor("b_rows", [E * CF + CS, P], F32))
        p_b = own.enter_context(nc.psum_tensor("p_b", [P, E * CF + CS], F32))
        b_in, b_turned, w_in = (nc.alloc_semaphore(n) for n in ("b_in", "b_turned", "sw_in"))
        g_set = nc.alloc_semaphore("g_set")
        block = own.enter_context(nc.Block())

        @block.sync
        def _(sp):
            sp.dma_start(rows[0:E * CF], A["rb1"].rearrange("e (c p) -> (e c) p", p=P)).then_inc(b_in, 16)
            sp.dma_start(rows[E * CF:], A["sb1"].rearrange("o (c p) -> (o c) p", p=P)).then_inc(b_in, 16)
            sp.dma_start(R["b2"][0:E], A["rb2"]).then_inc(w_in, 16)
            sp.dma_start(R["b2"][E:E + 1], A["sb2"]).then_inc(w_in, 16)
            sp.dma_start(R["sw1"][:], A["sW1"].rearrange("o p f -> (o p) f")).then_inc(w_in, 16)
            sp.dma_start(R["sw2"][:], A["sW2"].rearrange("o (c p) d -> (o p) c d", p=P)).then_inc(w_in, 16)
            sp.wait_ge(w_in, 64)

        @block.tensor
        def _(pe):
            pe.wait_ge(b_in, 32)
            n = E * CF + CS
            nc.tensor.transpose(p_b[:], rows[:], R["ident"][0:n, 0:n]).then_inc(b_turned, 1)

        @block.vector
        def _(dve):
            nc.vector.memset(R["gates"][:, :, E], 1.0).then_inc(g_set, 1)
            nc.vector.tensor_tensor(R["gates"][:, :, 0:E], R["achosen"][:], R["weights"][:], ALU.mult).then_inc(g_set, 1)
            dve.wait_ge(b_turned, 1)
            nc.vector.tensor_copy(R["b1T"][:], p_b[:])


def shared_expert(nc, ctx, A, R, E):
    CS = R["sw2"].shape[1]
    S0 = R["b1T"].shape[1] - CS
    with ExitStack() as own:
        def sb(name, shape, dt=F32):
            return own.enter_context(nc.sbuf_tensor("s_" + name, shape, dt))

        def sem(name):
            return nc.alloc_semaphore("s_" + name)

        hs = sb("hs", [P, 2, CS, L])
        gs = sb("gs", [P, T, E + 1])
        gT = sb("gT", [E + 1, L])
        p_h = own.enter_context(nc.psum_tensor("s_p_h", [P, 4, L], F32))
        p_g = own.enter_context(nc.psum_tensor("s_p_g", [E + 1, L], F32))
        p_o = own.enter_context(nc.psum_tensor("s_p_o", [P, 2, T, D], F32))
        h_done, hs_done, gs_done, g_turned, g_kept, o_done, o_added = (
            sem(n) for n in ("h_done", "hs_done", "gs_done", "g_turned", "g_kept", "o_done", "o_added"))
        loaded = sem("loaded")
        block = own.enter_context(nc.Block())

        @block.sync
        def _(sp):
            loads = load_second(sp, R, "a", A["rW2"], loaded)
            sp.wait_ge(loaded, 16 * loads)

        @block.tensor
        def _(pe):
            def hidden(b, first):
                for c in range(CS):
                    if not first:
                        pe.wait_ge(hs_done, b * CS + c + 1 - CS)
                    nc.tensor.matmul(p_h[:, c], R["sw1"][:, c * P:(c + 1) * P], R["xnT"][:, bass.ds(b * L, L)],
                                     start=True, stop=True).then_inc(h_done, 1)
                pe.wait_ge(gs_done, b + 1)
                for t in range(T):
                    last = nc.tensor.transpose(p_g[:, t * P:(t + 1) * P], gs[:, t], R["ident"][:])
                last.then_inc(g_turned, 1)

            def output(b, u, first):
                pe.wait_ge(hs_done, b * CS + CS)
                pe.wait_ge(g_kept, b + 1)
                if not first:
                    pe.wait_ge(o_added, b - 1)
                for t in range(T):
                    tok = slice(t * P, (t + 1) * P)
                    for c in range(CS):
                        nc.tensor.matmul(p_o[:, u, t], hs[:, u, c, tok], R["sw2"][:, c], start=c == 0, stop=False)
                    last = nc.tensor.matmul(p_o[:, u, t], gT[:, tok], R["b2"][:], start=False, stop=True)
                last.then_inc(o_done, 1)

            for u in range(2):
                hidden(u, u == 0)
                output(u, u, True)
            with pe.Fori(1, B // 2) as i:
                for u in range(2):
                    hidden(i * 2 + u, False)
                    output(i * 2 + u, u, False)

        @block.scalar
        def _(act):
            def batch(b, u, first):
                for c in range(CS):
                    act.wait_ge(h_done, b * CS + c + 1)
                    if c == 0 and not first:
                        act.wait_ge(o_done, b - 1)
                    nc.scalar.activation(hs[:, u, c], p_h[:, c], ACT.Gelu, bias=R["b1T"][:, S0 + c:S0 + c + 1]).then_inc(hs_done, 1)

            for u in range(2):
                batch(u, u, True)
            with act.Fori(1, B // 2) as i:
                for u in range(2):
                    batch(i * 2 + u, u, False)

        @block.vector
        def _(dve):
            def gates(b, first):
                if not first:
                    dve.wait_ge(g_turned, b)
                nc.vector.tensor_copy(gs[:], R["gates"][:, bass.ds(b * T, T), :]).then_inc(gs_done, 1)

            def batch(b, u, first, more=True):
                dve.wait_ge(g_turned, b + 1)
                if not first:
                    dve.wait_ge(o_done, b)
                nc.vector.tensor_copy(gT[:], p_g[:]).then_inc(g_kept, 1)
                if more:
                    gates(b + 1, False)
                dve.wait_ge(o_done, b + 1)
                rows = R["acc"][:, bass.ds(b * T, T), :]
                nc.vector.tensor_tensor(rows, rows, p_o[:, u], ALU.add).then_inc(o_added, 1)

            gates(0, True)
            batch(0, 0, True)
            batch(1, 1, False)
            with dve.Fori(1, B // 2 - 1) as i:
                for u in range(2):
                    batch(i * 2 + u, u, False)
            batch(B - 2, 0, False)
            batch(B - 1, 1, False, more=False)


def norm_chain(nc, dve, pool_wait, steps, src, xc, sq, stat, out, out_sem, rstd):
    def by_token(x):
        return x.unsqueeze(2).to_broadcast([P, T, D])

    steps.add(nc.vector.tensor_reduce(stat[:, 1], src, AX.X, ALU.add))
    steps.settle()
    steps.add(nc.vector.tensor_scalar(stat[:, 0], stat[:, 1], 1.0 / D, None, ALU.mult))
    steps.settle()
    steps.add(nc.vector.tensor_tensor(xc, src, by_token(stat[:, 0]), ALU.subtract))
    steps.settle()
    steps.add(nc.vector.tensor_tensor(sq, xc, xc, ALU.mult))
    steps.settle()
    steps.add(nc.vector.tensor_reduce(stat[:, 2], sq, AX.X, ALU.add))
    steps.settle()
    nc.vector.tensor_scalar(stat[:, 1], stat[:, 2], 1.0 / D, LN_EPS, ALU.mult, ALU.add).then_inc(pool_wait, 1)
    rstd()
    nc.vector.tensor_tensor(out, xc, by_token(stat[:, 3]), ALU.mult).then_inc(out_sem, 1)


TAPS = 4
DI = 256
NC = DI // P
NS = 16
DR = 128


def norm_and_mix(nc, ctx, A, R):
    E = A["w_router"].shape[0]
    with ExitStack() as own:
        def sb(name, shape, dt=F32):
            return own.enter_context(nc.sbuf_tensor("m_" + name, shape, dt))

        def sem(name):
            return nc.alloc_semaphore("m_" + name)

        inw = sb("inw", [P, 2 * DI])
        taps = sb("taps", [P, DI, TAPS])
        wtap = sb("wtap", [P, TAPS, DI])
        convb = sb("convb", [P, NC])
        rrows = sb("rrows", [E, D])
        rT = sb("rT", [P, E])
        nw = sb("nw", [P, 2, D])
        minus_half = sb("minus_half", [P, T])
        xc = sb("xc", [P, T, D])
        sq = sb("sq", [P, T, D])
        stat = sb("stat", [P, 2, 4, T])
        xs = sb("xs", [P, 2, T, D])
        xn_t = sb("xn_t", [P, 2, T, D])
        hn = sb("hn", [P, T, D])
        h_t = sb("h_t", [P, 2, T, D])
        xT_t = sb("xT_t", [P, 2, L])
        hT_t = sb("hT_t", [P, 2, TAPS - 1 + L])
        K = R["aslot"].shape[1]
        got = R["bw1"][:].rearrange("p e f -> p (e f)")[:, 0:2 * T * K * D].rearrange("p (u r d) -> p u r d", u=2, d=D)
        arrived, taken = [sem(f"arrived{u}") for u in range(2)], sem("taken")
        p_T = own.enter_context(nc.psum_tensor("m_p_T", [P, 2, L], F32))
        p_g = own.enter_context(nc.psum_tensor("m_p_g", [P, T, E], F32))
        p_c = own.enter_context(nc.psum_tensor("m_p_c", [P, 4, L], F32))
        w_in, r_turned, r_kept, wtap_set, set_up = sem("w_in"), sem("r_turned"), sem("r_kept"), sem("wtap_set"), sem("set_up")
        x_kept, chain, var_done, rstd_done, xn_done, hn_done, h_ready, added = (
            sem("x_kept"), sem("chain"), sem("var_done"), sem("rstd_done"), sem("xn_done"), sem("hn_done"), sem("h_ready"), sem("added"))
        x_turned, xT_kept, h_turned, hT_kept, g_done, g_kept, c_done, c_kept, copied = (
            sem("x_turned"), sem("xT_kept"), sem("h_turned"), sem("hT_kept"), sem("g_done"), sem("g_kept"), sem("c_done"), sem("c_kept"), sem("copied"))
        block = own.enter_context(nc.Block())
        LOADS = 16 * (6 + NC)

        @block.sync
        def _(sp):
            sp.dma_start(inw[:], A["in_proj_w"]).then_inc(w_in, 16)
            sp.dma_start(taps[:], A["conv_w"].partition_broadcast(P)).then_inc(w_in, 16)
            for c in range(NC):
                sp.dma_start(convb[:, c:c + 1], A["conv_b"][c * P:(c + 1) * P].unsqueeze(1)).then_inc(w_in, 16)
            sp.dma_start(rrows[:], A["w_router"]).then_inc(w_in, 16)
            sp.dma_start(nw[:, 0], A["norm_w"].partition_broadcast(P)).then_inc(w_in, 16)
            sp.dma_start(nw[:, 1], A["norm_b"].partition_broadcast(P)).then_inc(w_in, 16)
            sp.dma_start(R["A_log"][:], A["A_log"].rearrange("(c p) n -> p c n", p=P)).then_inc(w_in, 16)
            sp.wait_ge(w_in, LOADS)

        @block.gpsimd
        def _(pool):
            nc.gpsimd.memset(minus_half[:], -0.5).then_inc(set_up, 1)
            nc.gpsimd.memset(hT_t[:, :, 0:TAPS - 1], 0.0).then_inc(set_up, 1)
            pool.wait_ge(set_up, 2)
            for b in range(2):
                gather_rows(nc, R, "a", R["aslot"], b, got[:, b], arrived[b])
            for b in range(B):
                u, rows = b % 2, slice(b * T, (b + 1) * T)
                pool.wait_ge(var_done, b * 2 + 1)
                nc.gpsimd.tensor_tensor(stat[:, 0, 3], stat[:, 0, 1], minus_half[:], ALU.pow).then_inc(rstd_done, 1)
                pool.wait_ge(xn_done, b + 1)
                nc.gpsimd.tensor_copy(R["xn"][:, rows, :], xn_t[:, u]).then_inc(copied, 1)
                pool.wait_ge(var_done, b * 2 + 2)
                nc.gpsimd.tensor_tensor(stat[:, 1, 3], stat[:, 1, 1], minus_half[:], ALU.pow).then_inc(rstd_done, 1)
                nc.gpsimd.tensor_tensor(R["acc"][:, rows, :], xs[:, u], xn_t[:, u], ALU.add).then_inc(copied, 1)
                pool.wait_ge(xT_kept, b + 1)
                nc.gpsimd.tensor_copy(R["xnT"][:, b * L:(b + 1) * L], xT_t[:, u]).then_inc(copied, 1)
                if b + 2 < B:
                    pool.wait_ge(taken, b + 1)
                    gather_rows(nc, R, "a", R["aslot"], b + 2, got[:, u], arrived[u])

        @block.vector
        def _(dve):
            dve.wait_ge(w_in, LOADS)
            for k in range(TAPS):
                nc.vector.tensor_tensor(wtap[:, k], inw[:, 0:DI], taps[:, :, k], ALU.mult).then_inc(wtap_set, 1)
            dve.wait_ge(r_turned, 1)
            nc.vector.tensor_copy(rT[:], p_g[:].rearrange("p t e -> p (t e)")[:, 0:E]).then_inc(r_kept, 1)
            STEPS = 11 + (K - 1) * T

            def batch(i, u, first):
                b = i * 2 + u
                steps = Chain(dve, chain, b * STEPS)

                def rstd(n):
                    return lambda: dve.wait_ge(rstd_done, b * 2 + n)

                if not first:
                    dve.wait_ge(copied, b * 3 - 3)
                dve.wait_ge(arrived[u], i * (16 * K * T) + 16 * K * T)
                for k in range(K):
                    if k:
                        steps.settle()
                    for t in range(T):
                        last = nc.vector.scalar_tensor_tensor(
                            out=xs[:, u, t], in0=got[:, u, t * K + k], scalar=R["agate"][:, k, bass.ds(b * T + t, 1)],
                            in1=R["acc"][:, bass.ds(b * T + t, 1), :] if k == 0 else xs[:, u, t], op0=ALU.mult, op1=ALU.add)
                        if k < K - 1:
                            steps.add(last)
                last.then_inc(taken, 1)
                dve.wait_ge(taken, b + 1)
                norm_chain(nc, dve, var_done, steps, xs[:, u], xc[:], sq[:], stat[:, 0], xn_t[:, u], xn_done, rstd(1))
                dve.wait_ge(xn_done, b + 1)
                norm_chain(nc, dve, var_done, steps, xn_t[:, u], xc[:], sq[:], stat[:, 1], hn[:], hn_done, rstd(2))
                dve.wait_ge(hn_done, b + 1)
                steps.add(nc.vector.tensor_tensor(hn[:], hn[:], nw[:, 0].unsqueeze(1).to_broadcast([P, T, D]), ALU.mult))
                steps.settle()
                nc.vector.tensor_tensor(h_t[:, u], hn[:], nw[:, 1].unsqueeze(1).to_broadcast([P, T, D]), ALU.add).then_inc(h_ready, 1)
                dve.wait_ge(g_done, b + 1)
                nc.vector.tensor_copy(R["logits2"][:, bass.ds(b * T, T), :], p_g[:]).then_inc(g_kept, 1)
                assert steps.n == STEPS, steps.n

            for u in range(2):
                batch(0, u, True)
            with dve.Fori(1, B // 2) as i:
                for u in range(2):
                    batch(i, u, False)

        @block.tensor
        def _(pe):
            pe.wait_ge(w_in, LOADS)
            nc.tensor.transpose(p_g[:].rearrange("p t e -> p (t e)")[:, 0:E], rrows[:], R["ident"][0:E, 0:E]).then_inc(r_turned, 1)
            pe.wait_ge(r_kept, 1)
            pe.wait_ge(wtap_set, TAPS)
            pe.wait_ge(set_up, 2)

            def batch(b, u, first):
                pe.wait_ge(xn_done, b + 1)
                if not first:
                    pe.wait_ge(xT_kept, b)
                for t in range(T):
                    last = nc.tensor.transpose(p_T[:, 0, t * P:(t + 1) * P], xn_t[:, u, t], R["ident"][:])
                last.then_inc(x_turned, 1)
                pe.wait_ge(h_ready, b + 1)
                if not first:
                    pe.wait_ge(hT_kept, b)
                for t in range(T):
                    last = nc.tensor.transpose(p_T[:, 1, t * P:(t + 1) * P], h_t[:, u, t], R["ident"][:])
                last.then_inc(h_turned, 1)
                pe.wait_ge(xT_kept, b + 1)
                if not first:
                    pe.wait_ge(g_kept, b)
                for t in range(T):
                    last = nc.tensor.matmul(p_g[:, t], xT_t[:, u, t * P:(t + 1) * P], rT[:], start=True, stop=True)
                last.then_inc(g_done, 1)
                pe.wait_ge(hT_kept, b + 1)
                for c in range(4):
                    if not first:
                        pe.wait_ge(c_kept, b * 4 + c - 3)
                    if c < NC:
                        for k in range(TAPS):
                            last = nc.tensor.matmul(p_c[:, c], wtap[:, k, c * P:(c + 1) * P], hT_t[:, u, k:k + L],
                                                    start=k == 0, stop=k == TAPS - 1)
                    else:
                        last = nc.tensor.matmul(p_c[:, c], inw[:, c * P:(c + 1) * P], hT_t[:, u, TAPS - 1:],
                                                start=True, stop=True)
                    last.then_inc(c_done, 1)

            batch(0, 0, True)
            batch(1, 1, False)
            with pe.Fori(1, B // 2) as i:
                for u in range(2):
                    batch(i * 2 + u, u, False)

        @block.scalar
        def _(act):
            act.wait_ge(w_in, LOADS)

            def batch(b, u, first):
                act.wait_ge(x_turned, b + 1)
                if not first:
                    act.wait_ge(copied, b * 3 - 3)
                nc.scalar.activation(xT_t[:, u], p_T[:, 0], ACT.Copy).then_inc(xT_kept, 1)
                act.wait_ge(h_turned, b + 1)
                if not first:
                    act.wait_ge(c_done, b * 4 - 4)
                nc.scalar.activation(hT_t[:, u, TAPS - 1:], p_T[:, 1], ACT.Copy).then_inc(hT_kept, 1)
                for c in range(4):
                    act.wait_ge(c_done, b * 4 + c + 1)
                    if c < NC:
                        nc.scalar.activation(R["u"][:, c, bass.ds(b * L, L)], p_c[:, c], ACT.Silu, bias=convb[:, c:c + 1]).then_inc(c_kept, 1)
                    else:
                        nc.scalar.activation(R["g"][:, c - NC, bass.ds(b * L, L)], p_c[:, c], ACT.Silu).then_inc(c_kept, 1)

            for u in range(2):
                batch(u, u, True)
            with act.Fori(1, B // 2) as i:
                for u in range(2):
                    batch(i * 2 + u, u, False)


def step_sizes(nc, ctx, A, R):
    with ExitStack() as own:
        def sb(name, shape, dt=F32):
            return own.enter_context(nc.sbuf_tensor("d_" + name, shape, dt))

        def sem(name):
            return nc.alloc_semaphore("d_" + name)

        BC = 2 * NS
        xpw = sb("xpw", [P, NC, DR + BC])
        bcw = sb("bcw", [P, NC, 3, BC])
        dtw = sb("dtw", [P, DI])
        dtb = sb("dtb", [P, NC])
        dr = sb("dr", [P, L])
        first = sb("first", [3 * BC, L], BF16)
        rest = sb("rest", [3 * BC, L])
        z_abs = sb("z_abs", [P, NC, L])
        z_exp = sb("z_exp", [P, NC, L])
        z_pos = sb("z_pos", [P, NC, L])
        z_ln = sb("z_ln", [P, NC, L])
        p_dr = own.enter_context(nc.psum_tensor("d_p_dr", [P, L], F32))
        p_bc = own.enter_context(nc.psum_tensor("d_p_bc", [3 * BC, L], F32))
        p_z = own.enter_context(nc.psum_tensor("d_p_z", [P, NC, L], F32))
        w_in, bcw_set, a_exp, dr_done, dr_kept, bc_done, z_done, z_read, z_chain, ln_done, d_done = (
            sem(n) for n in ("w_in", "bcw_set", "a_exp", "dr_done", "dr_kept", "bc_done", "z_done", "z_read", "z_chain", "ln_done", "d_done"))
        split = sem("split")
        got = sb("got", [P, 2, T, D])
        arrived, taken = [sem(f"arrived{u}") for u in range(2)], sem("taken")
        block = own.enter_context(nc.Block())
        LOADS = 16 * (2 + NC)

        @block.sync
        def _(sp):
            sp.dma_start(xpw[:], A["x_proj_w"].rearrange("(c p) n -> p c n", p=P)).then_inc(w_in, 16)
            sp.dma_start(dtw[:], A["dt_proj_w"]).then_inc(w_in, 16)
            for c in range(NC):
                sp.dma_start(dtb[:, c:c + 1], A["dt_proj_b"][c * P:(c + 1) * P].unsqueeze(1)).then_inc(w_in, 16)

        @block.gpsimd
        def _(pool):
            pool.wait_ge(w_in, LOADS)
            nc.gpsimd.tensor_copy(bcw[:], xpw[:, :, DR:].unsqueeze(2).to_broadcast([P, NC, 3, BC])).then_inc(bcw_set, 1)
            for b in range(2):
                gather_rows(nc, R, "b", R["bslot"], b, got[:, b], arrived[b])
            for b in range(B):
                pool.wait_ge(ln_done, b + 1)
                nc.gpsimd.tensor_tensor(R["delta"][:, :, b * L:(b + 1) * L], z_pos[:], z_ln[:], ALU.add).then_inc(d_done, 1)
                if b + 2 < B:
                    pool.wait_ge(taken, b + 1)
                    gather_rows(nc, R, "b", R["bslot"], b + 2, got[:, b % 2], arrived[b % 2])

        @block.tensor
        def _(pe):
            pe.wait_ge(w_in, LOADS)
            pe.wait_ge(bcw_set, 1)

            def batch(b, is_first):
                tok = bass.ds(b * L, L)
                if not is_first:
                    pe.wait_ge(dr_kept, b)
                for c in range(NC):
                    last = nc.tensor.matmul(p_dr[:], xpw[:, c, 0:DR], R["u"][:, c, tok], start=c == 0, stop=c == NC - 1)
                last.then_inc(dr_done, 1)
                if not is_first:
                    pe.wait_ge(split, b * 4)
                for c in range(NC):
                    last = nc.tensor.matmul(p_bc[:], bcw[:, c].rearrange("p r n -> p (r n)"), R["u"][:, c, tok],
                                            start=c == 0, stop=c == NC - 1)
                last.then_inc(bc_done, 1)
                pe.wait_ge(dr_kept, b + 1)
                if not is_first:
                    pe.wait_ge(z_read, b * 2)
                for c in range(NC):
                    last = nc.tensor.matmul(p_z[:, c], dtw[:, c * P:(c + 1) * P], dr[:], start=True, stop=True)
                last.then_inc(z_done, 1)

            batch(0, True)
            with pe.Fori(1, B) as b:
                batch(b, False)

        @block.scalar
        def _(act):
            for r in range(3):
                part = slice(r * BC, (r + 1) * BC)
                nc.scalar.activation(R["pick"][part], R["ident"][part, part].unsqueeze(2).to_broadcast([BC, BC, P]), ACT.Copy)
            act.wait_ge(w_in, LOADS)
            nc.scalar.activation(R["A_neg"][:], R["A_log"][:], ACT.Exp).then_inc(a_exp, 1)

            def batch(b, is_first):
                act.wait_ge(z_done, b + 1)
                if not is_first:
                    act.wait_ge(d_done, b)
                for c in range(NC):
                    last = nc.scalar.activation(z_abs[:, c], p_z[:, c], ACT.Abs, bias=dtb[:, c:c + 1])
                last.then_inc(z_read, 1)
                for c in range(NC):
                    last = nc.scalar.activation(z_pos[:, c], p_z[:, c], ACT.Relu, bias=dtb[:, c:c + 1])
                last.then_inc(z_read, 1)
                act.wait_ge(z_read, b * 2 + 2)
                nc.scalar.activation(z_exp[:], z_abs[:], ACT.Exp, scale=-1.0).then_inc(z_chain, 1)
                act.wait_ge(z_chain, b + 1)
                nc.scalar.activation(z_ln[:], z_exp[:], ACT.Ln, bias=1.0).then_inc(ln_done, 1)

            batch(0, True)
            with act.Fori(1, B) as b:
                batch(b, False)

        @block.vector
        def _(dve):
            dve.wait_ge(a_exp, 1)
            nc.vector.tensor_scalar(R["A_neg"][:], R["A_neg"][:], -1.0, None, ALU.mult)

            def batch(b, is_first):
                tok = bass.ds(b * L, L)
                dve.wait_ge(dr_done, b + 1)
                if not is_first:
                    dve.wait_ge(z_done, b)
                nc.vector.tensor_copy(dr[:], p_dr[:]).then_inc(dr_kept, 1)
                dve.wait_ge(bc_done, b + 1)
                nc.vector.tensor_copy(first[:], p_bc[:]).then_inc(split, 1)
                dve.wait_ge(split, b * 4 + 1)
                nc.vector.tensor_tensor(rest[:], p_bc[:], first[:], ALU.subtract).then_inc(split, 1)
                nc.vector.tensor_copy(R["bc"][0:BC, tok], first[0:BC])
                dve.wait_ge(split, b * 4 + 2)
                nc.vector.tensor_copy(first[BC:2 * BC], rest[BC:2 * BC])
                nc.vector.tensor_copy(first[2 * BC:], rest[2 * BC:]).then_inc(split, 1)
                dve.wait_ge(split, b * 4 + 3)
                nc.vector.tensor_copy(R["bc"][BC:2 * BC, tok], first[BC:2 * BC])
                nc.vector.tensor_tensor(R["bc"][2 * BC:, tok], rest[2 * BC:], first[2 * BC:], ALU.subtract).then_inc(split, 1)

            def add_experts(i, u):
                dve.wait_ge(arrived[u], i * (16 * T) + 16 * T)
                rows = R["acc"][:, bass.ds((i * 2 + u) * T, T), :]
                nc.vector.tensor_tensor(rows, rows, got[:, u], ALU.add).then_inc(taken, 1)

            batch(0, True)
            add_experts(0, 0)
            batch(1, False)
            add_experts(0, 1)
            with dve.Fori(1, B // 2) as i:
                for u in range(2):
                    batch(i * 2 + u, False)
                    add_experts(i, u)


def state_space(nc, ctx, A, R):
    with ExitStack() as own:
        def sb(name, shape, dt=F32):
            return own.enter_context(nc.sbuf_tensor("y_" + name, shape, dt))

        def sem(name):
            return nc.alloc_semaphore("y_" + name)

        BC = 2 * NS
        pick = R["pick"]
        opw = sb("opw", [P, NC, D])
        dpar = sb("dpar", [P, NC])
        dl = sb("dl", [P, 2, NC, L])
        du = sb("du", [P, 2, NC, L])
        bs = sb("bs", [P, 2, L])
        da = sb("da", [P, 2, NC, L])
        dbu = sb("dbu", [P, 2, NC, L])
        h = sb("h", [P, 2, NC, L])
        hc = sb("hc", [P, 2, NC, L])
        yz = sb("yz", [P, 2, NC, L])
        p_b = own.enter_context(nc.psum_tensor("y_p_b", [P, 2, L], F32))
        p_c = own.enter_context(nc.psum_tensor("y_p_c", [P, 2, L], F32))
        p_y = own.enter_context(nc.psum_tensor("y_p_y", [P, NC, L], F32))
        p_o = own.enter_context(nc.psum_tensor("y_p_o", [P, T, D], F32))
        (w_in, du_done, b_done, c_done, b_kept, da_done, dbu_done, dbu_dve, h_done, hc_done, y_sum, yu, yz_done, o_done, o_added) = (
            sem(n) for n in ("w_in", "du_done", "b_done", "c_done", "b_kept", "da_done", "dbu_done", "dbu_dve", "h_done",
                             "hc_done", "y_sum", "yu", "yz_done", "o_done", "o_added"))
        dl_done = sem("dl_done")
        block = own.enter_context(nc.Block())
        LOADS = 16 * (1 + NC)

        def on_pool(n, c):
            return (n, c) != (NS - 1, 1)

        N_POOL = sum(on_pool(n, c) for n in range(NS) for c in range(NC))
        N_DVE = NS * NC - N_POOL

        def pool_count(n, c):
            return sum(on_pool(m, d) for m in range(NS) for d in range(NC) if (m, d) <= (n, c))

        def pool_before(n):
            return pool_count(n, NC - 1) if n >= 0 else pool_count(NS + n, NC - 1) - N_POOL

        def dve_count(n, c):
            return n * NC + c + 1 - pool_count(n, c)

        @block.sync
        def _(sp):
            sp.dma_start(opw[:], A["out_proj_w"].rearrange("(c p) d -> p c d", p=P)).then_inc(w_in, 16)
            for c in range(NC):
                sp.dma_start(dpar[:, c:c + 1], A["D_param"][c * P:(c + 1) * P].unsqueeze(1)).then_inc(w_in, 16)

        @block.gpsimd
        def _(pool):
            def batch(b, u, first):
                pool.wait_ge(du_done, b + 1)
                for n in range(NS):
                    pool.wait_ge(b_kept, b * NS + n + 1)
                    for c in range(NC):
                        if on_pool(n, c):
                            if not (first and n < 2):
                                pool.wait_ge(h_done, b * NS * NC + (n - 2) * NC + c + 1)
                            nc.gpsimd.tensor_tensor(dbu[:, n % 2, c], du[:, u, c], bs[:, n % 2], ALU.mult).then_inc(dbu_done, 1)

            batch(0, 0, True)
            batch(1, 1, False)
            with pool.Fori(1, B // 2) as i:
                for u in range(2):
                    batch(i * 2 + u, u, False)

        @block.tensor
        def _(pe):
            pe.wait_ge(w_in, LOADS)

            def spread_b(b, n, first):
                if not (first and n < 2):
                    pe.wait_ge(b_kept, b * NS + n - 1)
                    if n == 1:
                        pe.wait_ge(dbu_dve, b * N_DVE)
                nc.tensor.matmul(p_b[:, n % 2], pick[:, n], R["bc"][:, bass.ds(b * L, L)], start=True, stop=True).then_inc(b_done, 1)

            def spread_c(b, n, first):
                if not (first and n < 2):
                    pe.wait_ge(hc_done, (b * NS + n - 1) * NC)
                nc.tensor.matmul(p_c[:, n % 2], pick[:, NS + n], R["bc"][:, bass.ds(b * L, L)], start=True, stop=True).then_inc(c_done, 1)

            def gather(b, n, first):
                for c in range(NC):
                    pe.wait_ge(hc_done, (b * NS + n) * NC + c + 1)
                    if n == 0 and not first:
                        pe.wait_ge(yu, (b - 1) * NC + c + 1)
                    nc.tensor.matmul(p_y[:, c], R["ident"][:], hc[:, n % 2, c], start=n == 0, stop=n == NS - 1).then_inc(y_sum, 1)

            def project(b, u, first):
                pe.wait_ge(yz_done, b * NC + NC)
                if not first:
                    pe.wait_ge(o_added, b)
                for t in range(T):
                    for c in range(NC):
                        last = nc.tensor.matmul(p_o[:, t], yz[:, u, c, t * P:(t + 1) * P], opw[:, c], start=c == 0, stop=c == NC - 1)
                last.then_inc(o_done, 1)

            def batch(b, u, first, before=True, after=True):
                for n in range(NS):
                    if n + 1 < NS:
                        spread_b(b, n + 1, first)
                    elif after:
                        spread_b(b + 1, 0, False)
                    spread_c(b, n, first)
                    if n >= 2:
                        gather(b, n - 2, first)
                    elif before:
                        gather(b - 1, NS - 2 + n, False)
                    if n == 5 and before:
                        project(b - 1, 1 - u, isinstance(b, int) and b == 1)

            spread_b(0, 0, True)
            batch(0, 0, True, before=False)
            batch(1, 1, False)
            with pe.Fori(1, B // 2 - 1) as i:
                for u in range(2):
                    batch(i * 2 + u, u, False)
            batch(B - 2, 0, False)
            batch(B - 1, 1, False, after=False)
            gather(B - 1, NS - 2, False)
            gather(B - 1, NS - 1, False)
            project(B - 1, 1, False)

        @block.scalar
        def _(act):
            def step(b, u):
                nc.scalar.activation(dl[:, u], R["delta"][:, :, bass.ds(b * L, L)], ACT.Copy).then_inc(dl_done, 1)

            def batch(b, u, first, after=True):
                for n in range(NS):
                    act.wait_ge(b_done, b * NS + n + 1)
                    if not (first and n < 2):
                        act.wait_ge(dbu_done, b * N_POOL + pool_before(n - 2))
                    nc.scalar.activation(bs[:, n % 2], p_b[:, n % 2], ACT.Copy).then_inc(b_kept, 1)
                    if n == 0:
                        act.wait_ge(dl_done, b + 1)
                    for c in range(NC):
                        if not (first and n < 2):
                            act.wait_ge(h_done, b * NS * NC + (n - 2) * NC + c + 1)
                        nc.scalar.activation(da[:, n % 2, c], dl[:, u, c], ACT.Exp,
                                             scale=R["A_neg"][:, c, n:n + 1]).then_inc(da_done, 1)
                    if n == 8 and after:
                        if not first:
                            act.wait_ge(da_done, b * NS * NC)
                        step(b + 1, 1 - u)

            step(0, 0)
            batch(0, 0, True)
            batch(1, 1, False)
            with act.Fori(1, B // 2 - 1) as i:
                for u in range(2):
                    batch(i * 2 + u, u, False)
            batch(B - 2, 0, False)
            batch(B - 1, 1, False, after=False)

        @block.vector
        def _(dve):
            dve.wait_ge(w_in, LOADS)

            def step_times_u(b, u, first):
                tok = bass.ds(b * L, L)
                if not first:
                    dve.wait_ge(dbu_done, (b - 1) * N_POOL)
                nc.vector.tensor_tensor(du[:, u], R["delta"][:, :, tok], R["u"][:, :, tok], ALU.mult).then_inc(du_done, 1)

            def scan(b, u, n, first):
                for c in range(NC):
                    at = (b * NS + n) * NC + c
                    if on_pool(n, c):
                        dve.wait_ge(dbu_done, b * N_POOL + pool_count(n, c))
                    else:
                        dve.wait_ge(b_done, b * NS + n + 1)
                        dve.wait_ge(du_done, b + 1)
                        nc.vector.tensor_tensor(dbu[:, n % 2, c], du[:, u, c], p_b[:, n % 2], ALU.mult).then_inc(dbu_dve, 1)
                        dve.wait_ge(dbu_dve, b * N_DVE + dve_count(n, c))
                    if not (first and n < 2):
                        dve.wait_ge(hc_done, at - 2 * NC + 1)
                    dve.wait_ge(da_done, at + 1)
                    nc.vector.tensor_tensor_scan(h[:, n % 2, c], da[:, n % 2, c], dbu[:, n % 2, c], 0.0,
                                                 ALU.mult, ALU.add).then_inc(h_done, 1)

            def times_c(b, n, first):
                for c in range(NC):
                    at = (b * NS + n) * NC + c
                    dve.wait_ge(c_done, b * NS + n + 1)
                    dve.wait_ge(h_done, at + 1)
                    if not (first and n < 2):
                        dve.wait_ge(y_sum, at - 2 * NC + 1)
                    nc.vector.tensor_tensor(hc[:, n % 2, c], h[:, n % 2, c], p_c[:, n % 2], ALU.mult).then_inc(hc_done, 1)

            def gate(b, u):
                tok = bass.ds(b * L, L)
                for c in range(NC):
                    dve.wait_ge(y_sum, (b * NS + NS - 1) * NC + c + 1)
                    nc.vector.scalar_tensor_tensor(out=yz[:, u, c], in0=R["u"][:, c, tok], scalar=dpar[:, c:c + 1],
                                                   in1=p_y[:, c], op0=ALU.mult, op1=ALU.add).then_inc(yu, 1)
                for c in range(NC):
                    dve.wait_ge(yu, b * NC + c + 1)
                    nc.vector.tensor_tensor(yz[:, u, c], yz[:, u, c], R["g"][:, c, tok], ALU.mult).then_inc(yz_done, 1)

            def add_out(b):
                rows = R["acc"][:, bass.ds(b * T, T), :]
                dve.wait_ge(o_done, b + 1)
                nc.vector.tensor_tensor(rows, rows, p_o[:], ALU.add).then_inc(o_added, 1)

            def batch(b, u, first, before=True, after=True):
                for n in range(NS):
                    if n == 2 and before:
                        gate(b - 1, 1 - u)
                    scan(b, u, n, first)
                    if n > 0:
                        times_c(b, n - 1, first)
                    elif before:
                        times_c(b - 1, NS - 1, False)
                    if n == 8 and before:
                        add_out(b - 1)
                    if n == 10 and after:
                        step_times_u(b + 1, 1 - u, first)

            step_times_u(0, 0, True)
            batch(0, 0, True, before=False)
            batch(1, 1, False)
            with dve.Fori(1, B // 2 - 1) as i:
                for u in range(2):
                    batch(i * 2 + u, u, False)
            batch(B - 2, 0, False)
            batch(B - 1, 1, False, after=False)
            times_c(B - 1, NS - 1, False)
            gate(B - 1, 1)
            add_out(B - 1)


def shared_gated(nc, ctx, A, R):
    F = A["w_gate"].shape[0]
    CF = F // P
    with ExitStack() as own:
        def sb(name, shape, dt=F32):
            return own.enter_context(nc.sbuf_tensor("v_" + name, shape, dt))

        def sem(name):
            return nc.alloc_semaphore("v_" + name)

        score = sb("score", [P, NT])
        raw = sb("raw", [P, 3, CF, P])
        wT = sb("wT", [P, 3, CF, P])
        sil = sb("sil", [P, CF, L])
        hid = sb("hid", [P, 2, CF, L])
        p_w = own.enter_context(nc.psum_tensor("v_p_w", [P, 2, CF, P], F32))
        p_h = own.enter_context(nc.psum_tensor("v_p_h", [P, 2, CF, L], F32))
        p_o = own.enter_context(nc.psum_tensor("v_p_o", [P, 2, T, D], F32))
        w_in, w_turned, w_kept, gate_done, up_done, sil_done, hid_done, o_done, o_added = (
            sem(n) for n in ("w_in", "w_turned", "w_kept", "gate_done", "up_done", "sil_done", "hid_done", "o_done", "o_added"))
        scored, scaled, scattered, loaded = sem("scored"), sem("scaled"), sem("scattered"), sem("bloaded")
        block = own.enter_context(nc.Block())

        @block.gpsimd
        def _(pool):
            pool.wait_ge(scaled, 1)
            scatter_rows(nc, R, "b", R["bslot"], range(NT), scattered)
            pool.wait_ge(scattered, 16 * NT)

        @block.sync
        def _(sp):
            sp.dma_start(raw[:, 0], A["w_gate"].rearrange("(c p) d -> p c d", p=P)).then_inc(w_in, 16)
            sp.dma_start(raw[:, 1], A["w_up"].rearrange("(c p) d -> p c d", p=P)).then_inc(w_in, 16)
            sp.dma_start(raw[:, 2], A["w_down"].rearrange("d (c p) -> d c p", p=P)).then_inc(w_in, 16)
            load_first(sp, R, "b", A["gate_up"], loaded)
            loads = 1 + load_second(sp, R, "b", A["down"], loaded)
            sp.wait_ge(loaded, 16 * loads)

        @block.tensor
        def _(pe):
            pe.wait_ge(w_in, 48)
            for m in range(3):
                if m > 0:
                    pe.wait_ge(w_kept, m)
                for c in range(CF):
                    last = nc.tensor.transpose(p_w[:, 0, c], raw[:, m, c], R["ident"][:])
                last.then_inc(w_turned, 1)
            pe.wait_ge(w_kept, 3)

            def hidden(b, first):
                tok = bass.ds(b * L, L)
                for m, done in ((0, gate_done), (1, up_done)):
                    if not first:
                        pe.wait_ge(hid_done, b)
                    for c in range(CF):
                        last = nc.tensor.matmul(p_h[:, m, c], wT[:, m, c], R["xnT"][:, tok], start=True, stop=True)
                    last.then_inc(done, 1)

            def output(b, u, first):
                pe.wait_ge(hid_done, b + 1)
                if not first:
                    pe.wait_ge(o_added, b - 1)
                for t in range(T):
                    for c in range(CF):
                        last = nc.tensor.matmul(p_o[:, u, t], hid[:, u, c, t * P:(t + 1) * P], wT[:, 2, c],
                                                start=c == 0, stop=c == CF - 1)
                last.then_inc(o_done, 1)

            for u in range(2):
                hidden(u, u == 0)
                output(u, u, True)
            with pe.Fori(1, B // 2) as i:
                for u in range(2):
                    hidden(i * 2 + u, False)
                    output(i * 2 + u, u, False)

        @block.scalar
        def _(act):
            nc.scalar.activation(score[:], R["bgate"][:, 0], ACT.Sigmoid).then_inc(scored, 1)

            def batch(b, first):
                act.wait_ge(gate_done, b + 1)
                if not first:
                    act.wait_ge(hid_done, b)
                nc.scalar.activation(sil[:], p_h[:, 0], ACT.Silu).then_inc(sil_done, 1)

            batch(0, True)
            with act.Fori(1, B) as b:
                batch(b, False)

        @block.vector
        def _(dve):
            dve.wait_ge(scored, 1)
            nc.vector.tensor_tensor(R["xn"][:], R["xn"][:], score[:].unsqueeze(2).to_broadcast([P, NT, D]),
                                    ALU.mult).then_inc(scaled, 1)
            for m in range(3):
                dve.wait_ge(w_turned, m + 1)
                nc.vector.tensor_copy(wT[:, m], p_w[:, 0]).then_inc(w_kept, 1)

            def batch(b, u, first):
                dve.wait_ge(up_done, b + 1)
                dve.wait_ge(sil_done, b + 1)
                if not first:
                    dve.wait_ge(o_done, b - 1)
                nc.vector.tensor_tensor(hid[:, u], sil[:], p_h[:, 1], ALU.mult).then_inc(hid_done, 1)
                dve.wait_ge(o_done, b + 1)
                rows = R["acc"][:, bass.ds(b * T, T), :]
                nc.vector.tensor_tensor(rows, rows, p_o[:, u], ALU.add).then_inc(o_added, 1)

            for u in range(2):
                batch(u, u, True)
            with dve.Fori(1, B // 2) as i:
                for u in range(2):
                    batch(i * 2 + u, u, False)


def store_acc(nc, ctx, R, out):
    with ExitStack() as own:
        stored = nc.alloc_semaphore("stored")
        block = own.enter_context(nc.Block())

        @block.sync
        def _(sp):
            sp.dma_start(out.rearrange("b (t p) d -> p (b t) d", p=P), R["acc"][:]).then_inc(stored, 16)
            sp.wait_ge(stored, 16)


@contextmanager
def signals_of_a_part(nc):
    before = nc.snapshot_sems()
    yield
    nc.clear_and_free_semaphores(nc.allocated_since(before))
    nc.all_engine_barrier()


def two_layers(nc, A, out):
    E0, K0, E1 = A["gW"].shape[1], 3, A["w_router"].shape[0]
    tiles0, tiles1 = whole(most_tiles(K0 * B * L, E0)), whole(most_tiles(B * L, E1))
    CF0, CS = A["rb1"].shape[1] // P, A["sb1"].shape[1] // P

    def dram(name, shape, dt=F32):
        return nc.dram_tensor(name, shape, dt).ap()

    with ExitStack() as ctx:
        R = {}

        def keep(scope, name, shape, dt=F32, tag="sb"):
            R[name] = scope.enter_context(nc.sbuf_tensor(name + "_" + tag, shape, dt))

        keep(ctx, "ident", [P, P])
        keep(ctx, "identb", [P, P], BF16)
        keep(ctx, "acc", [P, NT, D])
        for tag, E, K, tiles in (("a", E0, K0, tiles0), ("b", E1, 1, tiles1)):
            keep(ctx, tag + "gate", [P, K, NT])
            keep(ctx, tag + "slot", [P, K, NT], I32)
            keep(ctx, tag + "chosen", [P, NT, E])
            keep(ctx, tag + "owner", [P, tiles], I32)
            R[tag + "table"] = dram(tag + "_table", [tiles * P, D])
            R[tag + "answers"] = dram(tag + "_answers", [tiles * P, D])
        R["q_dram"], R["k_dram"] = dram("q_parts", [B, 3, P, L], BF16), dram("k_parts", [B, 3, P, L], BF16)
        R["at_dram"], R["nm_dram"] = dram("heads_out", [2, L * D]), dram("max_rows", [2, 3 * HH, L], BF16)

        R["cleared"] = nc.alloc_semaphore("cleared")
        with ExitStack() as first, signals_of_a_part(nc):
            keep(first, "xn", [P, NT, D])
            keep(first, "xnT", [P, B * L])
            keep(first, "logits", [P, NT, E0])
            keep(first, "weights", [P, NT, E0])
            keep(first, "aw1", [P, E0, CF0 * P])
            with ExitStack() as heads:
                keep(heads, "v", [P, NT, D])
                keep(heads, "qs", [P, 2, H, L], BF16)
                keep(heads, "ks", [P, 2, H, L], BF16)
                norm_and_project(nc, ctx, A, R)
                softmax_weights(nc, ctx, R, E0)
                route(nc, ctx, R, "a", R["weights"][:], E0, K0, tiles0)
                attention(nc, ctx, A, R)
            keep(first, "aw2", [P, E0 * CF0, D])
            keep(first, "gates", [P, NT, E0 + 1])
            keep(first, "b1T", [P, E0 * CF0 + CS])
            keep(first, "b2", [E0 + 1, D])
            keep(first, "sw1", [P, CS * P])
            keep(first, "sw2", [P, CS, D])
            expert_biases(nc, ctx, A, R, E0)
            shared_expert(nc, ctx, A, R, E0)
            expert_tiles(nc, R, "a", tiles0, E0, R["atable"], R["aanswers"], False)
        with ExitStack() as states:
            keep(states, "u", [P, NC, B * L])
            keep(states, "g", [P, NC, B * L])
            keep(states, "A_log", [P, NC, NS])
            keep(states, "A_neg", [P, NC, NS])
            with ExitStack() as experts:
                keep(experts, "bw1", [P, E1, A["gate_up"].shape[2]])
                keep(experts, "bw2", [P, E1 * A["down"].shape[1] // P, D])
                with ExitStack() as rows:
                    keep(rows, "xn", [P, NT, D], tag="second")
                    keep(rows, "xnT", [P, B * L], tag="second")
                    keep(rows, "logits2", [P, NT, E1])
                    norm_and_mix(nc, ctx, A, R)
                    route(nc, ctx, R, "b", R["logits2"][:], E1, 1, tiles1)
                    shared_gated(nc, ctx, A, R)
                expert_tiles(nc, R, "b", tiles1, E1, R["btable"], R["banswers"], True)
            keep(states, "delta", [P, NC, B * L])
            keep(states, "bc", [3 * 2 * NS, B * L], BF16)
            keep(states, "pick", [3 * 2 * NS, 2 * NS, P], BF16)
            step_sizes(nc, ctx, A, R)
            state_space(nc, ctx, A, R)
        store_acc(nc, ctx, R, out)


_INS = {
    "x": "L0_attn_x", "Wqkv": "L0_attn_W_qkv", "bqkv": "L0_attn_b_qkv",
    "sW1": "L0_ffn_sW1", "sb1": "L0_ffn_sb1", "sW2": "L0_ffn_sW2", "sb2": "L0_ffn_sb2",
    "rW1": "L0_ffn_rW1", "rb1": "L0_ffn_rb1", "rW2": "L0_ffn_rW2", "rb2": "L0_ffn_rb2",
    "gW": "L0_ffn_gW", "gb": "L0_ffn_gb",
    "norm_w": "L1_attn_norm_w", "norm_b": "L1_attn_norm_b", "in_proj_w": "L1_attn_in_proj_w",
    "conv_w": "L1_attn_conv_w", "conv_b": "L1_attn_conv_b", "x_proj_w": "L1_attn_x_proj_w",
    "dt_proj_w": "L1_attn_dt_proj_w", "dt_proj_b": "L1_attn_dt_proj_b", "A_log": "L1_attn_A_log",
    "D_param": "L1_attn_D_param", "out_proj_w": "L1_attn_out_proj_w",
    "w_router": "L1_ffn_w_router", "gate_up": "L1_ffn_gate_up_proj", "down": "L1_ffn_down_proj",
    "w_gate": "L1_ffn_w_gate", "w_up": "L1_ffn_w_up", "w_down": "L1_ffn_w_down",
}


def kernel(**inputs):
    import numpy as _np
    import concourse.bacc as _bacc
    from concourse import mybir as _mybir
    from concourse.bass_utils import run_bass_kernel_spmd as _run

    nc = _bacc.Bacc("TRN2", target_bir_lowering=False, num_devices=1)
    arrays, args = {}, {}
    for short, name in _INS.items():
        a = _np.ascontiguousarray(inputs[name])
        arrays[f"in_{name}"] = a
        args[short] = nc.dram_tensor(f"in_{name}", a.shape, _mybir.dt.from_np(a.dtype), kind="ExternalInput").ap()
    out = nc.dram_tensor("out_x", [B, L, D], F32, kind="ExternalOutput").ap()
    two_layers(nc, args, out)
    r = _run(nc, [arrays], core_ids=[0])
    return r.results[0]["out_x"]
```

```python
import concourse.bass as bass
from concourse import mybir
from contextlib import ExitStack, contextmanager

F32 = mybir.dt.float32
BF16 = mybir.dt.bfloat16
I32 = mybir.dt.int32
ALU = mybir.AluOpType
ACT = mybir.ActivationFunctionType
AX = mybir.AxisListType

P = 128
B, L, D = 8, 512, 128
T = L // P
NT = B * T
H, HD = 16, 8
LN_EPS = 1e-5

Q_ROWS = [0, 0, 0, 1, 1, 2]
K_ROWS = [0, 1, 2, 0, 1, 0]
SR = 96
MR = SR + 3
HH = H // 2
VW = 32


class Chain:

    def __init__(self, eng, sem, base=0):
        self.eng, self.sem, self.base, self.n = eng, sem, base, 0

    def add(self, ins):
        ins.then_inc(self.sem, 1)
        self.n += 1

    def settle(self):
        self.eng.wait_ge(self.sem, self.base + self.n)


def scatter_rows(nc, R, tag, slot, tiles, sent):
    for t in tiles:
        for k in range(slot.shape[1]):
            nc.gpsimd.indirect_dma_start(
                out=R[tag + "table"], out_offset=bass.IndirectOffsetOnAxis(ap=slot[:, k, t:t + 1], axis=0),
                in_=R["xn"][:, t], in_offset=None).then_inc(sent, 16)


def gather_rows(nc, R, tag, slot, b, got, arrived, which):
    K = slot.shape[1]
    for r in which:
        t, k = divmod(r, K)
        nc.gpsimd.indirect_dma_start(
            out=got[:, r], out_offset=None, in_=R[tag + "answers"],
            in_offset=bass.IndirectOffsetOnAxis(ap=slot[:, k, b * T + t:b * T + t + 1], axis=0)).then_inc(arrived, 16)


ROW_RUNS = [(0, 3), (3, 5), (5, 6)]


HALF_STACKS = 2 * len(ROW_RUNS) * 16


def load_stacks(sp, R, b, u, hf):
    hs, cols = slice(hf * HH, (hf + 1) * HH), slice(hf * HH * L, (hf + 1) * HH * L)
    for name, rows in (("q", Q_ROWS), ("k", K_ROWS)):
        src, dst = R[name + "_dram"].rearrange("b c (p h) t -> b c p (h t)", p=HD), R[name + "s"]
        for lo, hi in ROW_RUNS:
            c = rows[lo]
            if rows[hi - 1] == c:
                part = src[bass.ds(b, 1), c, :, cols].to_broadcast([hi - lo, HD, HH * L])
            else:
                part = src[bass.ds(b, 1), c:c + hi - lo, :, cols].rearrange("o c p t -> (o c) p t")
            sp.dma_start(dst[HD * lo:HD * hi, u, hs].rearrange("p h t -> p (h t)"), part).then_inc(R["stacked"][u][hf], 16)


def norm_and_project(nc, A, R):
    with ExitStack() as own:
        def sb(name, shape, dt):
            return own.enter_context(nc.sbuf_tensor(name, shape, dt))

        def ps(name, shape, dt=F32):
            return own.enter_context(nc.psum_tensor(name, shape, dt))

        def sem(name):
            return nc.alloc_semaphore(name)

        E = A["gW"].shape[1]
        x_t = sb("x_t", [P, 2, T, D], F32)
        xc_t = sb("xc_t", [P, 2, T, D], F32)
        xn_t = sb("xn_t", [P, 2, T, D], F32)
        xT_t = sb("xT_t", [P, 2, L], F32)
        stat = sb("stat", [P, 2, 4, T], F32)
        minus_half = sb("minus_half", [P, T], F32)
        qk_f, qk_r = (R[w][:].rearrange("p e f -> p (e f)")[:, 0:4 * L].rearrange("p (u n t) -> p u n t", u=2, n=2)
                      for w in ("aw1", "aw2"))
        sq_t = R["aw1"][:].rearrange("p e f -> p (e f)")[:, 4 * L:6 * L].rearrange("p (u t d) -> p u t d", u=2, t=T)
        qk_p = sb("qk_p", [P, 2, 2, 3, L], BF16)
        wqkv = R["aw2"][:].rearrange("p e f -> p (e f)")[:, 4 * L:4 * L + 3 * D]
        wqk = R["aw1"][:].rearrange("p e f -> p (e f)")[:, 6 * L:6 * L + 2 * D].rearrange("p (n d) -> p n d", n=2)
        gw = sb("gw", [P, E], F32)
        bqk = sb("bqk", [P, 2], F32)
        bv = sb("bv", [P, D], F32)
        gb = sb("gb", [P, E], F32)
        p_T = ps("p_T", [P, L])
        p_q = ps("p_q", [P, L])
        p_k = ps("p_k", [P, L])
        p_v = ps("p_v", [P, T, D])
        p_g = ps("p_g", [P, T, E])

        ident_set = sem("ident_set")
        weights_in, vectors_in = sem("weights_in"), sem("vectors_in")
        VECTORS = 16 * (2 + 2 * HD)
        x_in = [sem(f"x_in{u}") for u in range(2)]
        xc_done, sq_done, xn_done, a_dve = sem("xc_done"), sem("sq_done"), sem("xn_done"), sem("a_dve")
        T_done, T_kept, q_done, k_done, vg_done = sem("T_done"), sem("T_kept"), sem("q_done"), sem("k_done"), sem("vg_done")
        part1, rest1, part2, part3 = sem("part1"), sem("rest1"), sem("part2"), sem("part3")
        stacks_zero = sem("stacks_zero")
        half_set, w_turned = sem("half_set"), sem("w_turned")
        a_act, rstd_done = sem("a_act"), sem("rstd_done")
        summed, vg_kept = sem("summed"), sem("vg_kept")
        xn_out, xT_out = [sem(f"xn_out{u}") for u in range(2)], [sem(f"xT_out{u}") for u in range(2)]
        qk_out = [sem(f"qk_out{u}") for u in range(2)]

        x_d = A["x"].rearrange("b (t p) d -> b p t d", p=P)
        block = own.enter_context(nc.Block())

        @block.sync
        def _(sp):
            def load_x(b, u, first):
                if not first:
                    sp.wait_ge(summed, b - 1)
                sp.dma_start(x_t[:, u], x_d[bass.ds(b, 1)].rearrange("o p t d -> (o p) t d")).then_inc(x_in[u], 16)

            def copy_xn(b, u):
                sp.wait_ge(xn_done, b + 1)
                sp.dma_start(R["xn"][:, bass.ds(b * T, T), :], xn_t[:, u]).then_inc(xn_out[u], 16)
                sp.wait_ge(T_kept, b + 1)
                sp.dma_start(R["xnT"][:, bass.ds(b * L, L)], xT_t[:, u]).then_inc(xT_out[u], 16)

            def store_qk(b, u):
                sp.wait_ge(part3, b + 1)
                for n, dst in ((0, R["q_dram"]), (1, R["k_dram"])):
                    sp.dma_start(dst[bass.ds(b, 1)].rearrange("o c p t -> (o p) c t"), qk_p[:, u, n]).then_inc(qk_out[u], 16)

            load_x(0, 0, True)
            load_x(1, 1, True)
            sp.dma_start(wqkv, A["Wqkv"]).then_inc(weights_in, 16)
            sp.dma_start(gw[:], A["gW"]).then_inc(weights_in, 16)
            for n in range(2):
                for c in range(HD):
                    sp.dma_start(bqk[H * c:H * (c + 1), n:n + 1],
                                 A["bqkv"][n * D:(n + 1) * D].rearrange("(h c) -> c h", c=HD)[c].unsqueeze(1),
                                 allow_slow_non_contiguous=True).then_inc(vectors_in, 16)
            sp.dma_start(bv[:], A["bqkv"][2 * D:3 * D].partition_broadcast(P)).then_inc(vectors_in, 16)
            sp.dma_start(gb[:], A["gb"].partition_broadcast(P)).then_inc(vectors_in, 16)
            load_shared_expert(sp, A, R, A["rW1"].shape[0])
            copy_xn(0, 0)
            load_x(2, 0, False)
            copy_xn(1, 1)
            load_x(3, 1, False)
            store_qk(0, 0)
            with sp.Fori(1, B // 2 - 1) as i:
                for u in range(2):
                    copy_xn(i * 2 + u, u)
                    load_x(i * 2 + u + 2, u, False)
                    store_qk(i * 2 + u - 1, 1 - u)
            for b in (B - 2, B - 1):
                copy_xn(b, b % 2)
                store_qk(b - 1, 1 - b % 2)
            store_qk(B - 1, 1)
            for u in range(2):
                sp.wait_ge(qk_out[u], 32 * (B // 2))
            sp.wait_ge(stacks_zero, 2)
            for u in range(2):
                sp.wait_ge(xn_out[u], 16 * (B // 2))
                sp.wait_ge(xT_out[u], 16 * (B // 2))

        @block.gpsimd
        def _(pool):
            ident = R["ident"]
            nc.gpsimd.memset(minus_half[:], -0.5).then_inc(half_set, 1)
            nc.gpsimd.memset(R["b2"][:], 0.0).then_inc(R["b2_zero"], 1)
            pool.wait_ge(half_set, 1)
            nc.gpsimd.memset(ident[:], 0.0).then_inc(ident_set, 1)
            pool.wait_ge(ident_set, 1)
            nc.gpsimd.affine_select(out=ident[:], in_=ident[:], compare_op=ALU.not_equal, fill=1.0, base=0,
                                    pattern=[[-1, P]], channel_multiplier=1).then_inc(ident_set, 1)
            pool.wait_ge(weights_in, 32)
            for n in range(2):
                nc.gpsimd.tensor_copy(wqk[:, n].rearrange("k (c h) -> k c h", c=HD),
                                      wqkv[:, n * D:(n + 1) * D].rearrange("k (h c) -> k c h", c=HD)).then_inc(w_turned, 1)
            nc.gpsimd.memset(R["ks"][:].bitcast(F32), 0.0).then_inc(stacks_zero, 1)
            with pool.Fori(0, B // 2) as i:
                for u in range(2):
                    b = i * 2 + u
                    rows = bass.ds(b * T, T)
                    pool.wait_ge(a_dve, b * 4 + 4)
                    nc.gpsimd.tensor_tensor(stat[:, u, 3], stat[:, u, 1], minus_half[:], ALU.pow).then_inc(rstd_done, 1)
                    pool.wait_ge(xn_done, b + 1)
                    nc.gpsimd.tensor_tensor(R["acc"][:, rows, :], x_t[:, u], xn_t[:, u], ALU.add).then_inc(summed, 1)

        @block.vector
        def _(dve):
            nc.vector.memset(R["qs"][:].bitcast(F32), 0.0).then_inc(stacks_zero, 1)
            STEPS = 4

            def norm(b, u, i, first):
                steps = Chain(dve, a_dve, b * STEPS)
                dve.wait_ge(x_in[u], i * 16 + 16)
                steps.add(nc.vector.tensor_reduce(stat[:, u, 1], x_t[:, u], AX.X, ALU.add))
                steps.settle()
                steps.add(nc.vector.tensor_scalar(stat[:, u, 0], stat[:, u, 1], 1.0 / D, None, ALU.mult))
                steps.settle()
                nc.vector.tensor_tensor(xc_t[:, u], x_t[:, u], stat[:, u, 0].unsqueeze(2).to_broadcast([P, T, D]),
                                        ALU.subtract).then_inc(xc_done, 1)
                dve.wait_ge(sq_done, b + 1)
                steps.add(nc.vector.tensor_reduce(stat[:, u, 2], sq_t[:, u], AX.X, ALU.add))
                steps.settle()
                steps.add(nc.vector.tensor_scalar(stat[:, u, 1], stat[:, u, 2], 1.0 / D, LN_EPS, ALU.mult, ALU.add))
                steps.settle()
                dve.wait_ge(rstd_done, b + 1)
                if not first:
                    dve.wait_ge(xn_out[u], i * 16)
                    dve.wait_ge(summed, b - 1)
                    dve.wait_ge(T_done, b - 1)
                nc.vector.tensor_tensor(xn_t[:, u], xc_t[:, u], stat[:, u, 3].unsqueeze(2).to_broadcast([P, T, D]),
                                        ALU.mult).then_inc(xn_done, 1)
                assert steps.n == STEPS

            def project(b, u):
                dve.wait_ge(vg_done, b + 1)
                nc.vector.tensor_tensor(R["v"][:, bass.ds(b * T, T), :], p_v[:],
                                        bv[:].unsqueeze(1).to_broadcast([P, T, D]), ALU.add).then_inc(vg_kept, 1)
                dve.wait_ge(part1, b + 1)
                nc.vector.tensor_tensor(qk_r[:, u], qk_f[:, u], qk_p[:, u, :, 0], ALU.subtract).then_inc(rest1, 1)
                nc.vector.tensor_tensor(R["logits"][:, bass.ds(b * T, T), :], p_g[:],
                                        gb[:].unsqueeze(1).to_broadcast([P, T, E]), ALU.add).then_inc(vg_kept, 1)

            def third_part(b, u):
                dve.wait_ge(part2, b + 1)
                nc.vector.tensor_tensor(qk_p[:, u, :, 2], qk_r[:, u], qk_p[:, u, :, 1], ALU.subtract).then_inc(part3, 1)

            norm(0, 0, 0, True)
            norm(1, 1, 0, True)
            dve.wait_ge(vectors_in, VECTORS)
            project(0, 0)
            norm(2, 0, 1, False)
            project(1, 1)
            third_part(0, 0)
            norm(3, 1, 1, False)
            project(2, 0)
            third_part(1, 1)
            with dve.Fori(2, B // 2) as i:
                for u in range(2):
                    norm(i * 2 + u, u, i, False)
                    project(i * 2 + u - 1, 1 - u)
                    third_part(i * 2 + u - 2, u)
            project(B - 1, 1)
            third_part(B - 2, 0)
            third_part(B - 1, 1)

        @block.scalar
        def _(act):
            def square(b, u):
                act.wait_ge(xc_done, b + 1)
                nc.scalar.activation(sq_t[:, u], xc_t[:, u], ACT.Square).then_inc(sq_done, 1)

            def second_part(b, u):
                act.wait_ge(rest1, b + 1)
                nc.scalar.activation(qk_p[:, u, :, 1], qk_r[:, u], ACT.Copy).then_inc(part2, 1)

            def batch(b, u, i, first, more=True):
                act.wait_ge(T_done, b + 1)
                if not first:
                    act.wait_ge(xT_out[u], i * 16)
                    act.wait_ge(vg_done, b - 1)
                nc.scalar.activation(xT_t[:, u], p_T[:], ACT.Copy).then_inc(T_kept, 1)
                if not (first and u == 0):
                    second_part(b - 1, 1 - u)
                if more:
                    square(b + 1, 1 - u)
                act.wait_ge(q_done, b + 1)
                if not first:
                    act.wait_ge(part3, b - 1)
                nc.scalar.activation(qk_f[:, u, 0], p_q[:], ACT.Identity, bias=bqk[:, 0:1]).then_inc(a_act, 1)
                act.wait_ge(k_done, b + 1)
                nc.scalar.activation(qk_f[:, u, 1], p_k[:], ACT.Identity, bias=bqk[:, 1:2]).then_inc(a_act, 1)
                act.wait_ge(a_act, b * 2 + 2)
                if not first:
                    act.wait_ge(qk_out[u], i * 32)
                nc.scalar.activation(qk_p[:, u, :, 0], qk_f[:, u], ACT.Copy).then_inc(part1, 1)

            square(0, 0)
            act.wait_ge(vectors_in, VECTORS)
            for u in range(2):
                batch(u, u, 0, True)
            with act.Fori(1, B // 2 - 1) as i:
                for u in range(2):
                    batch(i * 2 + u, u, i, False)
            batch(B - 2, 0, B // 2 - 1, False)
            batch(B - 1, 1, B // 2 - 1, False, more=False)
            second_part(B - 1, 1)

        @block.tensor
        def _(pe):
            pe.wait_ge(ident_set, 2)
            pe.wait_ge(weights_in, 32)
            pe.wait_ge(w_turned, 2)

            def batch(b, u, first):
                pe.wait_ge(xn_done, b + 1)
                for t in range(T):
                    last = nc.tensor.transpose(p_T[:, t * P:(t + 1) * P], xn_t[:, u, t], R["ident"][:])
                last.then_inc(T_done, 1)
                pe.wait_ge(T_kept, b + 1)
                if not first:
                    pe.wait_ge(a_act, b * 2)
                nc.tensor.matmul(p_q[:], wqk[:, 0], xT_t[:, u], start=True, stop=True).then_inc(q_done, 1)
                nc.tensor.matmul(p_k[:], wqk[:, 1], xT_t[:, u], start=True, stop=True).then_inc(k_done, 1)
                if not first:
                    pe.wait_ge(vg_kept, b * 2)
                for t in range(T):
                    nc.tensor.matmul(p_v[:, t], xT_t[:, u, t * P:(t + 1) * P], wqkv[:, 2 * D:3 * D], start=True, stop=True)
                for t in range(T):
                    last = nc.tensor.matmul(p_g[:, t], xT_t[:, u, t * P:(t + 1) * P], gw[:], start=True, stop=True)
                last.then_inc(vg_done, 1)

            batch(0, 0, True)
            batch(1, 1, False)
            with pe.Fori(1, B // 2) as i:
                for u in range(2):
                    batch(i * 2 + u, u, False)


def attention(nc, A, R):
    with ExitStack() as own:
        def sb(name, shape, dt):
            return own.enter_context(nc.sbuf_tensor(name, shape, dt))

        def ps(name, shape, dt=F32):
            return own.enter_context(nc.psum_tensor(name, shape, dt))

        def sem(name):
            return nc.alloc_semaphore(name)

        qs, ks = R["qs"], R["ks"]
        ones = sb("ones", [3, L], BF16)
        zeros = sb("zeros", [P, D], F32)
        va = sb("va", [P, 2, T, H, VW], F32)
        pr = sb("pr", [P, 2, 4, L], F32)
        os_t = sb("os_t", [P, L], F32)
        rden = sb("rden", [P, T, 4], F32)
        at = sb("at", [P, 2, H, T, HD], F32)
        att = sb("att", [P, 2, T, D], F32)
        nres = sb("nres", [P, T, HH], F32)
        nmp = sb("nmp", [P, T, 3, HH], BF16)
        nmT = sb("nmT", [3 * HH, L], BF16)
        p_st = ps("p_st", [P, 2, 2, L])
        p_s = ps("p_s", [P, 2, L])
        p_o = ps("p_o", [P, L])
        p_m = ps("p_m", [P, L])
        p_to = p_m[:].rearrange("p (t g c) -> p t g c", t=T, g=4)
        p_nm = p_m[0:3 * HH, 0:L // 2].bitcast(BF16)

        stacked = R["stacked"]
        ones_set, ones_in, va_zero, va_set = sem("ones_set"), sem("ones_in"), sem("va_zero"), sem("va_set")
        s_done, max_done, nmax = R["s_done"], R["max_done"], R["nmax"]
        st_done, exp_done, pv_done = sem("st_done"), sem("exp_done"), sem("pv_done")
        o_kept, to_done, at_done, added = sem("o_kept"), sem("to_done"), sem("at_done"), sem("added")
        at_out, at_in = sem("at_out"), sem("at_in")
        b_dve_r = sem("b_dve_r")
        b_dve, parts_done, nmT_done, nmT_kept, nm_out = (
            sem("b_dve"), sem("parts_done"), sem("nmT_done"), sem("nmT_kept"), sem("nm_out"))
        nm_in = [sem(f"nm_in{h}") for h in range(2)]
        identb_set, scattered, loaded = sem("identb_set"), sem("scattered"), sem("aloaded")
        zeros_set, cleared = sem("zeros_set"), sem("cleared")

        UNITS = 4 * T
        SCORES = H * T
        block = own.enter_context(nc.Block())

        @block.sync
        def _(sp):
            def place_max(u, h, n):
                sp.wait_ge(nmT_kept, n)
                sp.dma_start(R["nm_dram"][h], nmT[:]).then_inc(nm_out, 16)
                sp.wait_ge(nm_out, n * 16)
                sp.dma_start(qs[SR:MR, u, h * HH:(h + 1) * HH],
                             R["nm_dram"][h].rearrange("(c j) t -> c j t", c=3)).then_inc(nm_in[h], 16)

            sp.wait_ge(ones_set, 1)
            for u in range(2):
                sp.dma_start(ks[SR:MR, u], ones[:].unsqueeze(1).to_broadcast([3, H, L])).then_inc(ones_in, 16)
            for h in range(2):
                place_max(0, h, 1 + h)
            sp.wait_ge(zeros_set, 1)
            for table in (R["atable"], R["btable"]):
                n = table.shape[0] // P
                sp.dma_start(table.rearrange("(p a) d -> p a d", p=P),
                             zeros[:].unsqueeze(1).to_broadcast([P, n, D])).then_inc(cleared, 16)
            load_first(sp, R, "a", A["rW1"], loaded)
            weight_loads = 1 + load_second(sp, R, "a", A["rW2"], loaded)

            def reshape_out(b, u, first):
                if not first:
                    sp.wait_ge(added, b - 1)
                sp.wait_ge(at_done, b * 4 + 4)
                sp.dma_start(R["at_dram"][u].rearrange("(h p c) -> p h c", h=H, p=P),
                             at[:, u].rearrange("p h t c -> p h (t c)")).then_inc(at_out, 16)
                sp.wait_ge(at_out, b * 16 + 16)
                sp.dma_start(att[:, u], R["at_dram"][u].rearrange("(t p d) -> p t d", t=T, p=P)).then_inc(at_in, 16)

            def batch(b, u, first=False, maxima=True, stacks=True):
                for hf in range(2):
                    if stacks:
                        sp.wait_ge(pv_done, b * UNITS + (hf + 1) * (UNITS // 2))
                        load_stacks(sp, R, b + 2, u, hf)
                    if maxima:
                        place_max(1 - u, hf, b * 2 + 3 + hf)
                reshape_out(b, u, first)

            for u in range(2):
                batch(u, u, first=True)
            with sp.Fori(1, B // 2 - 1) as i:
                for u in range(2):
                    batch(i * 2 + u, u)
            batch(B - 2, 0, stacks=False)
            batch(B - 1, 1, maxima=False, stacks=False)
            sp.wait_ge(loaded, 16 * weight_loads)

        @block.gpsimd
        def _(pool):
            nc.gpsimd.memset(ones[:], 1.0).then_inc(ones_set, 1)
            nc.gpsimd.memset(zeros[:], 0.0).then_inc(zeros_set, 1)
            nc.gpsimd.tensor_copy(R["identb"][:], R["ident"][:]).then_inc(identb_set, 1)
            nc.gpsimd.memset(va[:], 0.0).then_inc(va_zero, 1)
            pool.wait_ge(va_zero, 1)
            nc.gpsimd.memset(va[:, :, :, :, HD], 1.0).then_inc(va_zero, 1)

            def place_v(b, u):
                nc.gpsimd.tensor_copy(va[:, u, :, :, 0:HD],
                                      R["v"][:, bass.ds(b * T, T), :].rearrange("p t (h c) -> p t h c", c=HD)).then_inc(va_set, 1)

            def batch(b, u, more):
                rows = bass.ds(b * T, T)
                pool.wait_ge(at_in, b * 16 + 16)
                nc.gpsimd.tensor_tensor(R["acc"][:, rows, :], R["acc"][:, rows, :], att[:, u], ALU.add).then_inc(added, 1)
                if more:
                    place_v(b + 2, u)

            pool.wait_ge(va_zero, 2)
            place_v(0, 0)
            place_v(1, 1)
            pool.wait_ge(cleared, 32)
            cuts = [0, NT // 2, 3 * NT // 4, NT]
            scatter_rows(nc, R, "a", R["aslot"], range(cuts[0], cuts[1]), scattered)
            for u in range(2):
                batch(u, u, True)
                scatter_rows(nc, R, "a", R["aslot"], range(cuts[u + 1], cuts[u + 2]), scattered)
            with pool.Fori(1, B // 2 - 1) as i:
                for u in range(2):
                    batch(i * 2 + u, u, True)
            for u in range(2):
                batch(B - 2 + u, u, False)
            pool.wait_ge(scattered, 16 * R["aslot"].shape[1] * NT)

        @block.tensor
        def _(pe):
            def max_scores(b, u, n):
                h, t = n // T, n % T
                pe.wait_ge(max_done, b * SCORES + n - 1)
                q, k = qs[0:SR, u, h], ks[0:SR, u, h]
                nc.tensor.matmul(p_s[:, n % 2], q[:, t::T], k, start=True, stop=True).then_inc(s_done, 1)

            def turn_max(b, hf, turned):
                pe.wait_ge(parts_done, b * 2 + hf + 1)
                if turned is not None:
                    pe.wait_ge(at_done, turned)
                elif hf:
                    pe.wait_ge(nmT_kept, 1)
                for t in range(T):
                    last = nc.tensor.transpose(p_nm[:, t * P:(t + 1) * P], nmp[:, t].rearrange("p c h -> p (c h)"),
                                               R["identb"][:])
                last.then_inc(nmT_done, 1)

            def scores(b, u, w, n, first):
                g, t, x, y = w // T, w % T, n // 2, n % 2
                if y == 0 and not (first and w == 0):
                    pe.wait_ge(exp_done, b * (2 * UNITS) + 2 * w + x - 1)
                h = 4 * g + n
                q, k = qs[:, u, h], ks[:, u, h]
                last = nc.tensor.matmul(p_st[:, x, y], k[:, t * P:(t + 1) * P], q, start=True, stop=True)
                if y == 1:
                    last.then_inc(st_done, 1)

            def products(b, u, w, first):
                g, t = w // T, w % T
                if t == 0 and not (first and g == 0):
                    pe.wait_ge(o_kept, b * 4 + g)
                pe.wait_ge(exp_done, b * (2 * UNITS) + 2 * w + 2)
                for y in range(4):
                    last = nc.tensor.matmul(p_o[VW * y:VW * (y + 1)], va[:, u, t, 4 * g + y], pr[:, w % 2, y],
                                            start=t == 0, stop=t == T - 1, tile_position=(0, VW * y))
                last.then_inc(pv_done, 1)

            def turn_out(b, g, more):
                pe.wait_ge(o_kept, b * 4 + g + 1)
                if g == 0:
                    pe.wait_ge(nmT_kept, b * 2 + 2)
                if g > 1 and more:
                    pe.wait_ge(nmT_kept, b * 2 + g + 1)
                if not (g == 0 and isinstance(b, int) and b == 0):
                    pe.wait_ge(at_done, b * 4 + g)
                for t in range(T):
                    last = nc.tensor.transpose(p_m[:, t * P:(t + 1) * P], os_t[:, t::T], R["ident"][:])
                last.then_inc(to_done, 1)

            def batch(b, u, i, first, more):
                for w in range(UNITS):
                    if w == 0:
                        pe.wait_ge(nm_in[0], b * 16 + 16)
                        pe.wait_ge(va_set, b + 1)
                        if more:
                            pe.wait_ge(stacked[1 - u][0], (i + u) * HALF_STACKS + HALF_STACKS)
                    if w == UNITS // 2:
                        if more:
                            pe.wait_ge(stacked[1 - u][1], (i + u) * HALF_STACKS + HALF_STACKS)
                        pe.wait_ge(nm_in[1], b * 16 + 16)
                    for n in range(4):
                        scores(b, u, w, n, first)
                        if more and n > 0:
                            max_scores(b + 1, 1 - u, 4 * w + n - 1)
                    if w > 0:
                        products(b, u, w - 1, first)
                    elif not first:
                        products(b - 1, 1 - u, UNITS - 1, False)
                    if w == 1:
                        turn_max(b, 1, None if first else b * 4 - 1)
                    if w == 2 and not first:
                        turn_out(b - 1, 3, True)
                    if w % T == 1 and w > T:
                        turn_out(b, w // T - 1, more)
                    if more:
                        max_scores(b + 1, 1 - u, 4 * w + 3)
                        if w == UNITS // 2 + 3:
                            turn_max(b + 1, 0, b * 4 + 2)

            pe.wait_ge(identb_set, 1)
            turn_max(0, 0, None)
            pe.wait_ge(ones_in, 32)
            batch(0, 0, 0, True, True)
            batch(1, 1, 0, False, True)
            with pe.Fori(1, B // 2 - 1) as i:
                for u in range(2):
                    batch(i * 2 + u, u, i, False, True)
            batch(B - 2, 0, B // 2 - 1, False, True)
            batch(B - 1, 1, B // 2 - 1, False, False)
            products(B - 1, 1, UNITS - 1, False)
            turn_out(B - 1, 3, False)

        @block.scalar
        def _(act):
            def keep_max(b, hf, first=False):
                act.wait_ge(nmT_done, b * 2 + hf + 1)
                if not (first and hf == 0):
                    act.wait_ge(nm_out, (b * 2 + hf) * 16)
                nc.scalar.activation(nmT[:].rearrange("m (q t) -> m t q", t=T),
                                     p_nm.rearrange("m (t q) -> m t q", t=T), ACT.Copy).then_inc(nmT_kept, 1)

            def keep_out(b, g, first=False):
                act.wait_ge(pv_done, b * UNITS + (g + 1) * T)
                if not first:
                    act.wait_ge(to_done, b * 4 + g)
                nc.scalar.activation(os_t[:], p_o[:], ACT.Copy).then_inc(o_kept, 1)

            def batch(b, first, more=True):
                for w in range(UNITS):
                    for x in range(2):
                        act.wait_ge(st_done, b * (2 * UNITS) + 2 * w + x + 1)
                        if x == 0 and not (first and w < 2):
                            act.wait_ge(pv_done, b * UNITS + w - 1)
                        nc.scalar.activation(pr[:, w % 2, 2 * x:2 * x + 2], p_st[:, x], ACT.Exp).then_inc(exp_done, 1)
                    if w == 0 and not first:
                        keep_out(b - 1, 3)
                    elif w % T == 0 and w > 0:
                        keep_out(b, w // T - 1, first and w == T)
                    if w == 1:
                        keep_max(b, 1)
                    if w == UNITS // 2 + 4 and more:
                        keep_max(b + 1, 0)

            keep_max(0, 0, first=True)
            batch(0, True)
            with act.Fori(1, B - 1) as b:
                batch(b, False)
            batch(B - 1, False, more=False)
            keep_out(B - 1, 3)

        @block.vector
        def _(dve):

            def maxima(b, n):
                h, t = n // T, n % T
                dve.wait_ge(s_done, b * SCORES + n + 1)
                nc.vector.tensor_reduce(nmax[:, t, h:h + 1], p_s[:, n % 2], AX.X, ALU.max,
                                        negate=True).then_inc(max_done, 1)

            def split_max(b, hf, steps):
                m, rest = nmax[:, :, hf * HH:(hf + 1) * HH], nres[:]
                part = [nmp[:, :, c] for c in range(3)]
                dve.wait_ge(max_done, b * SCORES + (hf + 1) * (SCORES // 2))
                steps.add(nc.vector.tensor_copy(part[0], m))
                steps.settle()
                steps.add(nc.vector.tensor_tensor(rest, m, part[0], ALU.subtract))
                steps.settle()
                steps.add(nc.vector.tensor_copy(part[1], rest))
                steps.settle()
                nc.vector.tensor_tensor(part[2], rest, part[1], ALU.subtract).then_inc(parts_done, 1)

            def normalize(b, u, g, first):
                dve.wait_ge(to_done, b * 4 + g + 1)
                if g == 0 and not first:
                    dve.wait_ge(at_out, b * 16 - 16)
                nc.vector.reciprocal(rden[:], p_to[:, :, :, HD]).then_inc(b_dve_r, 1)
                dve.wait_ge(b_dve_r, b * 4 + g + 1)
                nc.vector.tensor_tensor(at[:, u, 4 * g:4 * g + 4], p_to[:, :, :, 0:HD].rearrange("p t g c -> p g t c"),
                                        rden[:].rearrange("p t g -> p g t").unsqueeze(3).to_broadcast([P, 4, T, HD]),
                                        ALU.mult).then_inc(at_done, 1)

            def batch(b, u, before, first, more):
                steps = Chain(dve, b_dve, b * 6 + 3)
                for w in range(UNITS):
                    if more:
                        for n in range(3):
                            maxima(b + 1, 4 * w + n)
                    if w == 0:
                        dve.wait_ge(nmT_done, b * 2 + 1)
                        split_max(b, 1, steps)
                    if more:
                        maxima(b + 1, 4 * w + 3)
                        if w == UNITS // 2:
                            dve.wait_ge(nmT_done, b * 2 + 2)
                            split_max(b + 1, 0, steps)
                    if w == 2 and before:
                        normalize(b - 1, 1 - u, 3, False)
                    if w % T == 1 and w > T:
                        normalize(b, u, w // T - 1, first)
                if more:
                    assert steps.n == 6

            steps = Chain(dve, b_dve)
            split_max(0, 0, steps)
            batch(0, 0, False, True, True)
            batch(1, 1, True, True, True)
            with dve.Fori(1, B // 2 - 1) as i:
                for u in range(2):
                    batch(i * 2 + u, u, True, False, True)
            batch(B - 2, 0, True, False, True)
            batch(B - 1, 1, True, False, False)
            normalize(B - 1, 1, 3, False)


def most_tiles(rows, experts):
    return rows // P - 1 + experts


def route(nc, R, tag, w, E, K, TILES, logits=None, shared=None, gated=None):
    gate, slot, chosen, owner = R[tag + "gate"], R[tag + "slot"], R[tag + "chosen"], R[tag + "owner"]
    with ExitStack() as own:
        def sb(name, shape, dt=F32):
            return own.enter_context(nc.sbuf_tensor(tag + name, shape, dt))

        def sem(name):
            return nc.alloc_semaphore(tag + name)

        e_no = sb("e_no", [P, NT, E])
        t_rows = sb("t_rows", [P, E, NT])
        if gated is not None:
            tile_no = sb("tile_no", [P, TILES, E])[:]
        else:
            tile_no = R["aw2"][:].rearrange("p e f -> p (e f)")[:, 4 * L:4 * L + TILES * E].rearrange("p (j e) -> p j e", e=E)
        below = sb("below", [P, P], BF16)
        ones = sb("ones", [P, P], BF16)
        left = sb("left", [P, NT, E]) if K > 1 else None
        is_max = sb("is_max", [P, NT, E])
        key = sb("key", [P, NT, E])
        first_key = sb("first_key", [P, NT])
        pick = sb("pick", [P, K, NT, E])
        picked = sb("picked", [P, E, NT], BF16)
        total = sb("total", [P, E, NT])
        reset = sb("reset", [P, E, NT])
        run = sb("run", [P, E, NT])
        over = t_rows
        tiles = sb("tiles", [P, E])
        cum = sb("cum", [P, E])
        base = sb("base", [P, E])
        place = total
        prod = key
        slot_f = sb("slot_f", [P, K, NT])
        owner_f = sb("owner_f", [P, TILES])
        p_rank = own.enter_context(nc.psum_tensor(tag + "p_rank", [P, E, NT], F32))
        p_total = own.enter_context(nc.psum_tensor(tag + "p_total", [P, E, NT], F32))
        tables, chain, picked_set, counted = sem("tables"), sem("chain"), sem("picked_set"), sem("counted")
        shifted, expd = sem("shifted"), sem("expd")
        top = sb("top", [P, 3, NT])
        block = own.enter_context(nc.Block())

        @block.sync
        def _(sp):
            if logits is not None:
                for u in range(2):
                    for hf in range(2):
                        load_stacks(sp, R, u, u, hf)
            if gated is not None:
                gated.load_weights(sp)

        @block.scalar
        def _(act):
            if gated is not None:
                gated.act(act, chain)
            if logits is not None:
                act.wait_ge(shifted, 1)
                nc.scalar.activation(w, w, ACT.Exp).then_inc(expd, 1)
                shared.act(act)

        @block.gpsimd
        def _(pool):
            exact = dict(allow_small_or_imprecise_dtypes=True)
            nc.gpsimd.iota(e_no[:], [[0, NT], [1, E]], base=0, channel_multiplier=0, **exact).then_inc(tables, 1)
            nc.gpsimd.memset(ones[:], 1.0).then_inc(tables, 1)
            nc.gpsimd.memset(reset[:], 1.0).then_inc(tables, 1)
            pool.wait_ge(tables, 3)
            nc.gpsimd.memset(reset[:, :, 0], 0.0).then_inc(tables, 1)
            nc.gpsimd.affine_select(out=below[:], in_=ones[:], compare_op=ALU.is_gt, fill=0.0, base=0,
                                    pattern=[[1, P]], channel_multiplier=-1).then_inc(tables, 1)
            nc.gpsimd.iota(t_rows[:], [[0, E], [P, NT]], base=0, channel_multiplier=0, **exact).then_inc(tables, 1)
            nc.gpsimd.iota(tile_no, [[1, TILES], [0, E]], base=0, channel_multiplier=0, **exact).then_inc(tables, 1)
            if shared is not None:
                shared.pool(pool)
            if gated is not None:
                gated.scatter(pool)

        @block.tensor
        def _(pe):
            def count():
                pe.wait_ge(tables, 7)
                pe.wait_ge(picked_set, 1)
                nc.tensor.matmul(p_rank[:], below[:], picked[:], start=True, stop=True)
                nc.tensor.matmul(p_total[:], ones[:], picked[:], start=True, stop=True).then_inc(counted, 1)

            if gated is not None:
                gated.turn_weights(pe)
                gated.hidden(pe, 0, True)
                gated.hidden(pe, 1, False)
                gated.output(pe, 0, 0, True)
                count()
                gated.hidden(pe, 2, False)
                gated.output(pe, 1, 1, True)
                with pe.Fori(1, B // 2 - 1) as i:
                    for u in range(2):
                        gated.hidden(pe, i * 2 + u + 1, False)
                        gated.output(pe, i * 2 + u, u, False)
                gated.hidden(pe, B - 1, False)
                gated.output(pe, B - 2, 0, False)
                gated.output(pe, B - 1, 1, False)
            else:
                shared.turn_biases(pe)
                done = 0
                for b in range(B):
                    more = {2: EARLY_SCORES // 3, 3: EARLY_SCORES - EARLY_SCORES // 3, 6: 18, 7: 18}.get(b, 0)
                    shared.products(pe, b, b % 2, b == 0, scores=(done, done + more))
                    done += more
                    if b == 3:
                        count()
                shared.first_scores(pe, done, H * T)
                shared.biases(pe)

        @block.vector
        def _(dve):
            steps = Chain(dve, chain)

            def step(ins):
                steps.add(ins)
                steps.settle()

            def by_row(x):
                return x.unsqueeze(2).to_broadcast([P, NT, E])

            tt, stt = nc.vector.tensor_tensor, nc.vector.scalar_tensor_tensor
            if gated is not None:
                gated.keep_weights(dve)
            if logits is not None:
                step(nc.vector.tensor_reduce(top[:, 0], logits, AX.X, ALU.max))
                tt(w, logits, by_row(top[:, 0]), ALU.subtract).then_inc(shifted, 1)
                dve.wait_ge(expd, 1)
                step(nc.vector.tensor_reduce(top[:, 1], w, AX.X, ALU.add))
                step(nc.vector.reciprocal(top[:, 2], top[:, 1]))
                step(tt(w, w, by_row(top[:, 2]), ALU.mult))
            dve.wait_ge(tables, 7)
            values = w
            for k in range(K):
                step(nc.vector.tensor_reduce(gate[:, k], values, AX.X, ALU.max))
                step(tt(is_max[:], values, by_row(gate[:, k]), ALU.is_equal))
                step(stt(out=key[:], in0=is_max[:], scalar=-2.0 * E, in1=e_no[:], op0=ALU.mult, op1=ALU.add))
                step(nc.vector.tensor_reduce(first_key[:], key[:], AX.X, ALU.min))
                step(tt(pick[:, k], key[:], by_row(first_key[:]), ALU.is_equal))
                if k < K - 1:
                    step(stt(out=left[:], in0=pick[:, k], scalar=-4.0, in1=values, op0=ALU.mult, op1=ALU.add))
                    values = left[:]
                step(nc.vector.tensor_copy(chosen[:], pick[:, 0]) if k == 0 else
                     tt(chosen[:], chosen[:], pick[:, k], ALU.add))
                if gated is not None:
                    gated.hide(dve, 0, 0, True)
            nc.vector.tensor_copy(picked[:], chosen[:].rearrange("p t e -> p e t")).then_inc(picked_set, 1)
            if shared is not None:
                shared.first_maxima(dve, 0, EARLY_SCORES)
            else:
                gated.hide(dve, 1, 1, True)
                gated.add_out(dve, 0, 0)
            dve.wait_ge(counted, 1)
            step(nc.vector.tensor_copy(total[:], p_total[:]))
            step(nc.vector.tensor_tensor_scan(run[:].rearrange("p e t -> p (e t)"), reset[:].rearrange("p e t -> p (e t)"),
                                              total[:].rearrange("p e t -> p (e t)"), 0.0, ALU.mult, ALU.add))
            step(tt(over[:], run[:, :, NT - 1:NT].to_broadcast([P, E, NT]), t_rows[:], ALU.is_gt))
            step(nc.vector.tensor_reduce(tiles[:], over[:], AX.X, ALU.add))
            step(nc.vector.tensor_tensor_scan(cum[:], ones[:, 0:E], tiles[:], 0.0, ALU.mult, ALU.add))
            step(tt(base[:], cum[:], tiles[:], ALU.subtract))
            step(tt(place[:], run[:], total[:], ALU.subtract))
            step(tt(place[:], place[:], p_rank[:], ALU.add))
            step(stt(out=place[:], in0=base[:].unsqueeze(2).to_broadcast([P, E, NT]), scalar=float(P), in1=place[:],
                     op0=ALU.mult, op1=ALU.add))
            for k in range(K):
                step(tt(prod[:], pick[:, k], place[:].rearrange("p e t -> p t e"), ALU.mult))
                step(nc.vector.tensor_reduce(slot_f[:, k], prod[:], AX.X, ALU.add))
            step(nc.vector.tensor_copy(slot[:], slot_f[:]))
            if gated is not None:
                gated.scale(dve)
                gated.hide(dve, 2, 0, False)
                gated.add_out(dve, 1, 1)
                gated.hide(dve, 3, 1, False)
                gated.add_out(dve, 2, 0)
            step(tt(tile_no, tile_no, cum[:].unsqueeze(1).to_broadcast([P, TILES, E]), ALU.is_ge))
            step(nc.vector.tensor_reduce(owner_f[:], tile_no, AX.X, ALU.add))
            step(nc.vector.tensor_scalar(owner[:], owner_f[:], float(E - 1), None, ALU.min))
            if shared is not None:
                shared.first_maxima(dve, EARLY_SCORES, H * T)
                shared.gates(dve)
            else:
                gated.later_batches(dve)


GROUP = 4


def whole(tiles):
    return -(-tiles // GROUP) * GROUP


PER_LOAD = 4


def load_first(sp, R, tag, w1_d, loaded):
    sp.dma_start(R[tag + "w1"][:], w1_d.rearrange("e p f -> p e f")).then_inc(loaded, 16)


def load_second(sp, R, tag, w2_d, loaded):
    E, C = w2_d.shape[0], w2_d.shape[1] // P
    starts = range(0, E, PER_LOAD)
    for lo in starts:
        hi = min(lo + PER_LOAD, E)
        sp.dma_start(R[tag + "w2"][:, lo * C:hi * C],
                     w2_d[lo:hi].rearrange("e (c p) d -> p (e c) d", p=P)).then_inc(loaded, 16)
    return len(starts)


def expert_tiles(nc, R, tag, TILES, E, table_in, table_out, gated):
    W1, W2 = R[tag + "w1"], R[tag + "w2"]
    N1 = W1.shape[2]
    C1 = N1 // P
    CF = W2.shape[1] // E
    owner = R[tag + "owner"]
    GROUPS = TILES // GROUP
    with ExitStack() as own:
        def sb(name, shape, dt=F32):
            return own.enter_context(nc.sbuf_tensor(tag + name, shape, dt))

        def sem(name):
            return nc.alloc_semaphore(tag + name)

        xs = sb("xs", [P, 3, GROUP, D])
        xT = sb("xT", [P, 2, GROUP * P])
        w1 = sb("w1t", [P, GROUP, N1])
        w2 = sb("w2t", [P, 3, GROUP, CF, D])
        b1 = None if gated else sb("b1t", [P, 3, GROUP, CF])
        hid = sb("hid", [P, 2, GROUP, CF, P])
        sil = sb("sil", [P, GROUP, CF, P]) if gated else None
        y = sb("y", [P, 3, GROUP, D])
        p_x = own.enter_context(nc.psum_tensor(tag + "p_x", [P, GROUP * P], F32))
        p_h = [own.enter_context(nc.psum_tensor(tag + f"p_h{n}", [P, 4, P], F32)) for n in range(GROUP)]
        p_y = [own.enter_context(nc.psum_tensor(tag + f"p_y{n}", [P, GROUP, D], F32)) for n in range(2)]
        group_in = [sem(f"group_in{n}") for n in range(3)]
        group_out = [sem(f"group_out{n}") for n in range(3)]
        x_turned, x_kept, w1_kept, w2_kept, h_done, sil_done, hid_done, y_done, y_kept = (
            sem(n) for n in ("x_turned", "x_kept", "w1_kept", "w2_kept", "h_done", "sil_done", "hid_done", "y_done", "y_kept"))
        t_in = table_in.rearrange("(j p) d -> p j d", p=P)
        t_out = table_out.rearrange("(j p) d -> p j d", p=P)
        block = own.enter_context(nc.Block())

        def all_groups(eng, group, lo=0, hi=GROUPS):
            loops = hi // 6
            for g in range(lo, 6):
                group(g, g, 0, True)
            if loops > 1:
                with eng.Fori(1, loops) as i:
                    for u in range(6):
                        group(i * 6 + u, u, i, False)
            for g in range(loops * 6, hi):
                group(g, g % 6, g // 6, False)

        @block.sync
        def _(sp):
            def load(g, u, i, first):
                if not (first and u < 3):
                    sp.wait_ge(x_turned, g - 2)
                sp.dma_start(xs[:, u % 3], t_in[:, bass.ds(g * GROUP, GROUP), :]).then_inc(group_in[u % 3], 16)

            def store(g, u, i, first):
                sp.wait_ge(y_kept, g + 1)
                sp.dma_start(t_out[:, bass.ds(g * GROUP, GROUP), :], y[:, u % 3]).then_inc(group_out[u % 3], 16)

            def both(g, u, i, first):
                load(g, u, i, first)
                if not (first and u < 4):
                    store(g - 4, u - 4, i, first)

            all_groups(sp, both)
            for g in range(GROUPS - 4, GROUPS):
                store(g, g % 3, 0, False)
            for n in range(3):
                sp.wait_ge(group_out[n], 16 * len(range(n, GROUPS, 3)))

        @block.tensor
        def _(pe):
            def turn(g, u, i, first):
                pe.wait_ge(group_in[u % 3], i * 32 + (32 if u >= 3 else 16))
                if not (first and u == 0):
                    pe.wait_ge(x_kept, g)
                for n in range(GROUP):
                    last = nc.tensor.transpose(p_x[:, n * P:(n + 1) * P], xs[:, u % 3, n], R["ident"][:])
                last.then_inc(x_turned, 1)

            def hidden(g, u, n, first):
                if n == 0:
                    pe.wait_ge(x_kept, g + 1)
                pe.wait_ge(w1_kept, g * GROUP + n + 1)
                if not (first and u == 0):
                    pe.wait_ge(hid_done, g * GROUP + n - GROUP + 1)
                for c in range(C1):
                    last = nc.tensor.matmul(p_h[n][:, c], w1[:, n, c * P:(c + 1) * P], xT[:, u % 2, n * P:(n + 1) * P],
                                            start=True, stop=True)
                last.then_inc(h_done, 1)

            def product(g, u, n, first):
                pe.wait_ge(hid_done, g * GROUP + n + 1)
                pe.wait_ge(w2_kept, (g * GROUP + n + 1) * (1 if gated else 2))
                if n == 0 and not (first and u < 2):
                    pe.wait_ge(y_kept, g - 1)
                for c in range(CF):
                    last = nc.tensor.matmul(p_y[u % 2][:, n], hid[:, u % 2, n, c], w2[:, u % 3, n, c],
                                            start=c == 0, stop=c == CF - 1)
                if n == GROUP - 1:
                    last.then_inc(y_done, 1)

            def group(g, u, i, first, more=True):
                if more:
                    turn(g + 1, (u + 1) % 6, i + (1 if u == 5 else 0), False)
                before = not (first and u == 0)
                for n in range(GROUP):
                    hidden(g, u, n, first)
                    if before:
                        product(g - 1, (u - 1) % 6, n, first and u > 0)

            turn(0, 0, 0, True)
            all_groups(pe, group, hi=GROUPS - 1)
            group(GROUPS - 1, (GROUPS - 1) % 6, (GROUPS - 1) // 6, False, more=False)
            for n in range(GROUP):
                product(GROUPS - 1, (GROUPS - 1) % 6, n, False)

        @block.scalar
        def _(act):
            def keep_x(g, u, first):
                act.wait_ge(x_turned, g + 1)
                if not (first and u < 2):
                    act.wait_ge(h_done, (g - 1) * GROUP)
                nc.scalar.activation(xT[:, u % 2], p_x[:], ACT.Copy).then_inc(x_kept, 1)

            def keep_y(g, u, i, first):
                act.wait_ge(y_done, g + 1)
                if not (first and u < 3):
                    act.wait_ge(group_out[u % 3], i * 32 + (16 if u >= 3 else 0))
                nc.scalar.activation(y[:, u % 3], p_y[u % 2][:], ACT.Copy).then_inc(y_kept, 1)

            def group(g, u, i, first):
                if not (isinstance(g, int) and g == GROUPS - 1):
                    keep_x(g + 1, (u + 1) % 6, first and u < 5)
                if not (first and u < 2):
                    keep_y(g - 2, (u - 2) % 6, i - (1 if u < 2 else 0), first)
                for n in range(GROUP):
                    act.wait_ge(h_done, g * GROUP + n + 1)
                    if gated:
                        if not (first and u == 0):
                            act.wait_ge(hid_done, g * GROUP + n - GROUP + 1)
                        nc.scalar.activation(sil[:, n], p_h[n][:, 0:CF], ACT.Silu).then_inc(sil_done, 1)
                    else:
                        act.wait_ge(w2_kept, (g * GROUP + n) * 2 + 1)
                        if n == 0 and not (first and u < 2):
                            act.wait_ge(y_done, g - 1)
                        for c in range(CF):
                            last = nc.scalar.activation(hid[:, u % 2, n, c], p_h[n][:, c], ACT.Gelu,
                                                        bias=b1[:, u % 3, n, c:c + 1])
                        last.then_inc(hid_done, 1)

            keep_x(0, 0, True)
            all_groups(act, group)
            g = GROUPS
            keep_y(g - 2, (g - 2) % 6, (g - 2) // 6, False)
            keep_y(g - 1, (g - 1) % 6, (g - 1) // 6, False)

        @block.vector
        def _(dve):
            def copy_weights(g, u, n, e, first):
                if not (first and u == 0):
                    dve.wait_ge(h_done, g * GROUP + n - GROUP + 1)
                nc.vector.tensor_copy(w1[:, n], W1[:, bass.ds(e, 1), :]).then_inc(w1_kept, 1)
                if n == 0 and not (first and u < 3):
                    dve.wait_ge(y_done, g - 2)
                if not gated:
                    nc.vector.tensor_copy(b1[:, u % 3, n], R["b1T"][:, bass.ds(e * CF, CF)]).then_inc(w2_kept, 1)
                nc.vector.tensor_copy(w2[:, u % 3, n], W2[:, bass.ds(e * CF, CF), :]).then_inc(w2_kept, 1)

            def hide(g, u, n, first):
                dve.wait_ge(sil_done, g * GROUP + n + 1)
                if n == 0 and not (first and u < 2):
                    dve.wait_ge(y_done, g - 1)
                nc.vector.tensor_tensor(hid[:, u % 2, n], sil[:, n], p_h[n][:, CF:C1], ALU.mult).then_inc(hid_done, 1)

            def group(g, u, i, first):
                _, e = nc.values_load_multi_w_load_instructions(
                    owner[0:1, bass.ds(g * GROUP, GROUP)], engines=[dve.engine], min_val=0, max_val=E - 1)
                for n in range(GROUP):
                    if gated and not (first and u == 0):
                        hide(g - 1, (u - 1) % 6, n, first and u > 0)
                    copy_weights(g, u, n, e[n], first)

            all_groups(dve, group)
            if gated:
                for n in range(GROUP):
                    hide(GROUPS - 1, (GROUPS - 1) % 6, n, False)


def load_shared_expert(sp, A, R, E):
    E2 = R["b1rows"].shape[0] - A["sb1"].shape[1] // P
    sp.dma_start(R["b1rows"][0:E2], A["rb1"].rearrange("e (c p) -> (e c) p", p=P)).then_inc(R["biases_in"], 16)
    sp.dma_start(R["b1rows"][E2:], A["sb1"].rearrange("o (c p) -> (o c) p", p=P)).then_inc(R["biases_in"], 16)
    sp.wait_ge(R["b2_zero"], 1)
    for q in range(T):
        lo = q * QUARTER
        sp.dma_start(R["b2"][lo:lo + E, q], A["rb2"]).then_inc(R["biases_in"], 16)
        sp.dma_start(R["b2"][lo + E:lo + E + 1, q], A["sb2"]).then_inc(R["biases_in"], 16)
    sp.dma_start(R["sw1"][:], A["sW1"].rearrange("o p f -> (o p) f")).then_inc(R["biases_in"], 16)
    sp.dma_start(R["sw2"][:], A["sW2"].rearrange("o (c p) d -> (o p) c d", p=P)).then_inc(R["biases_in"], 16)


EARLY_SCORES = 24
QUARTER = 32


class SharedExpert:

    def __init__(self, nc, own, A, R, E):
        def sb(name, shape, dt=F32):
            return own.enter_context(nc.sbuf_tensor("s_" + name, shape, dt))

        def ps(name, shape):
            return own.enter_context(nc.psum_tensor("s_" + name, shape, F32))

        self.nc, self.R, self.E, self.CS = nc, R, E, R["sw2"].shape[1]
        place1, place2 = (R[w][:].rearrange("p e f -> p (e f)") for w in ("aw1", "aw2"))
        self.hs_most = place1[:, 0:(2 * self.CS - 1) * L].rearrange("p (c t) -> p c t", t=L)
        self.hs_last = sb("hs_last", [P, L])
        self.kept = place2[:, 0:2 * L].rearrange("p (u t d) -> p u t d", u=2, t=T)
        self.gT = place2[:, 2 * L:4 * L].rearrange("p (b t) -> p b t", t=P)
        self.p_h = ps("p_h", [P, 2, L])
        self.p_s = ps("p_s", [P, 2, L])
        self.p_o = ps("p_o", [P, T, D])
        self.p_g = ps("p_g", [P, L])
        (self.b_turned, self.b_kept, self.h_done, self.hs_done, self.o_done, self.o_kept, self.o_added,
         self.gates_set, self.g_turned, self.g_kept, self.g_out, self.g_added) = (
            nc.alloc_semaphore("s_" + n) for n in ("b_turned", "b_kept", "h_done", "hs_done", "o_done", "o_kept", "o_added",
                                                   "gates_set", "g_turned", "g_kept", "g_out", "g_added"))

    def hs(self, u, c):
        n = u * self.CS + c
        return self.hs_most[:, n] if n < 2 * self.CS - 1 else self.hs_last[:]

    def turn_biases(self, pe):
        n = self.R["b1rows"].shape[0]
        pe.wait_ge(self.R["biases_in"], 16 * (4 + 2 * T))
        self.nc.tensor.transpose(self.p_g[:, 0:n], self.R["b1rows"][:], self.R["ident"][0:n, 0:n]).then_inc(self.b_turned, 1)

    def first_scores(self, pe, lo, hi):
        for n in range(lo, hi):
            if n >= 2:
                pe.wait_ge(self.R["max_done"], n - 1)
            q, k = (self.R[x][0:SR, 0, n // T] for x in ("qs", "ks"))
            if n % T == 0:
                pe.wait_ge(self.R["stacked"][0][n // T // HH], HALF_STACKS)
            self.nc.tensor.matmul(self.p_s[:, n % 2], q[:, n % T::T], k, start=True, stop=True).then_inc(self.R["s_done"], 1)

    def first_maxima(self, dve, lo, hi):
        for n in range(lo, hi):
            h, t = n // T, n % T
            dve.wait_ge(self.R["s_done"], n + 1)
            self.nc.vector.tensor_reduce(self.R["nmax"][:, t, h:h + 1], self.p_s[:, n % 2], AX.X, ALU.max,
                                         negate=True).then_inc(self.R["max_done"], 1)

    def products(self, pe, b, u, first, scores):
        nc, R, CS = self.nc, self.R, self.CS
        lo, hi = scores
        runs = [lo + (hi - lo) * n // (CS + T) for n in range(CS + T + 1)]
        for c in range(CS):
            if not (first and c < 2):
                pe.wait_ge(self.hs_done, b * CS + c - 1)
            nc.tensor.matmul(self.p_h[:, c % 2], R["sw1"][:, c * P:(c + 1) * P], R["xnT"][:, bass.ds(b * L, L)],
                             start=True, stop=True).then_inc(self.h_done, 1)
            self.first_scores(pe, runs[c], runs[c + 1])
        pe.wait_ge(self.hs_done, b * CS + CS)
        if not first:
            pe.wait_ge(self.o_kept, b)
        for t in range(T):
            for c in range(CS):
                last = nc.tensor.matmul(self.p_o[:, t], self.hs(u, c)[:, t * P:(t + 1) * P], R["sw2"][:, c],
                                        start=c == 0, stop=c == CS - 1)
            if t == T - 1:
                last.then_inc(self.o_done, 1)
            self.first_scores(pe, runs[CS + t], runs[CS + t + 1])

    def biases(self, pe):
        nc, R = self.nc, self.R
        pe.wait_ge(self.gates_set, 3)
        pe.wait_ge(self.hs_done, B * self.CS)
        for b in range(B):
            last = nc.tensor.transpose(self.p_h[:, b // T, (b % T) * P:(b % T + 1) * P],
                                       R["gates"][:, b * T:(b + 1) * T].rearrange("p t e -> p (t e)"), R["ident"][:])
            if b % T == T - 1:
                last.then_inc(self.g_turned, 1)
        for b in range(B):
            if b % T == 0:
                pe.wait_ge(self.g_kept, b // T + 1)
            if b >= 2:
                pe.wait_ge(self.g_added, b - 1)
            elif b == 0:
                pe.wait_ge(self.o_kept, B)
            nc.tensor.matmul(self.biased(b), self.gT[:, b], R["b2"][:].rearrange("p t d -> p (t d)"),
                             start=True, stop=True).then_inc(self.g_out, 1)

    def biased(self, b):
        return self.p_g[:] if b % 2 else self.p_o[:].rearrange("p t d -> p (t d)")

    def act(self, act):
        nc, R, CS = self.nc, self.R, self.CS
        S0 = R["b1T"].shape[1] - CS

        def keep_out(b, u, first):
            act.wait_ge(self.o_done, b + 1)
            if not first:
                act.wait_ge(self.o_added, b - 1)
            nc.scalar.activation(self.kept[:, u], self.p_o[:], ACT.Copy).then_inc(self.o_kept, 1)

        act.wait_ge(self.b_turned, 1)
        nc.scalar.activation(R["b1T"][:], self.p_g[:, 0:R["b1rows"].shape[0]], ACT.Copy).then_inc(self.b_kept, 1)
        act.wait_ge(self.b_kept, 1)

        def batch(b, u, first):
            for c in range(CS):
                act.wait_ge(self.h_done, b * CS + c + 1)
                if c == 0 and not first:
                    act.wait_ge(self.o_done, b - 1)
                nc.scalar.activation(self.hs(u, c), self.p_h[:, c % 2], ACT.Gelu,
                                     bias=R["b1T"][:, S0 + c:S0 + c + 1]).then_inc(self.hs_done, 1)
            keep_out(b, u, first)

        for u in range(2):
            batch(u, u, True)
        with act.Fori(1, B // 2) as i:
            for u in range(2):
                batch(i * 2 + u, u, False)

    def pool(self, pool):
        nc, R = self.nc, self.R
        nc.gpsimd.memset(R["gates"][:], 0.0).then_inc(self.gates_set, 1)
        with pool.Fori(0, B // 2) as i:
            for u in range(2):
                b = i * 2 + u
                rows = R["acc"][:, bass.ds(b * T, T), :]
                pool.wait_ge(self.o_kept, b + 1)
                nc.gpsimd.tensor_tensor(rows, rows, self.kept[:, u], ALU.add).then_inc(self.o_added, 1)

    def gates(self, dve):
        nc, R, E = self.nc, self.R, self.E
        dve.wait_ge(self.gates_set, 1)
        nc.vector.memset(R["gates"][:, :, E], 1.0).then_inc(self.gates_set, 1)
        nc.vector.tensor_tensor(R["gates"][:, :, 0:E], R["achosen"][:], R["weights"][:], ALU.mult).then_inc(self.gates_set, 1)
        dve.wait_ge(self.b_kept, 1)
        dve.wait_ge(self.o_added, B)
        for n in range(B // T):
            dve.wait_ge(self.g_turned, n + 1)
            nc.vector.tensor_copy(self.gT[:, n * T:(n + 1) * T].rearrange("p b t -> p (b t)"), self.p_h[:, n]).then_inc(self.g_kept, 1)
        for b in range(B):
            dve.wait_ge(self.g_out, b + 1)
            rows = R["acc"][:, b * T:(b + 1) * T].rearrange("p t d -> p (t d)")
            nc.vector.tensor_tensor(rows, rows, self.biased(b), ALU.add).then_inc(self.g_added, 1)


def norm_chain(nc, pool_wait, steps, src, xc, sq, stat, out, out_sem, rstd):
    def by_token(x):
        return x.unsqueeze(2).to_broadcast([P, T, D])

    steps.add(nc.vector.tensor_reduce(stat[:, 1], src, AX.X, ALU.add))
    steps.settle()
    steps.add(nc.vector.tensor_scalar(stat[:, 0], stat[:, 1], 1.0 / D, None, ALU.mult))
    steps.settle()
    steps.add(nc.vector.tensor_tensor(xc, src, by_token(stat[:, 0]), ALU.subtract))
    steps.settle()
    steps.add(nc.vector.tensor_tensor(sq, xc, xc, ALU.mult))
    steps.settle()
    steps.add(nc.vector.tensor_reduce(stat[:, 2], sq, AX.X, ALU.add))
    steps.settle()
    nc.vector.tensor_scalar(stat[:, 1], stat[:, 2], 1.0 / D, LN_EPS, ALU.mult, ALU.add).then_inc(pool_wait, 1)
    rstd()
    nc.vector.tensor_tensor(out, xc, by_token(stat[:, 3]), ALU.mult).then_inc(out_sem, 1)


TAPS = 4
DI = 256
NC = DI // P
NS = 16
DR = 128


def norm_and_mix(nc, A, R):
    E = A["w_router"].shape[0]
    with ExitStack() as own:
        def sb(name, shape, dt=F32):
            return own.enter_context(nc.sbuf_tensor("m_" + name, shape, dt))

        def sem(name):
            return nc.alloc_semaphore("m_" + name)

        inw = sb("inw", [P, 2 * DI])
        taps = sb("taps", [P, DI, TAPS])
        wtap = sb("wtap", [P, TAPS, DI])
        convb = sb("convb", [P, NC])
        rrows = sb("rrows", [E, D])
        rT = sb("rT", [P, E])
        nw = sb("nw", [P, 2, D])
        minus_half = sb("minus_half", [P, T])
        xc = sb("xc", [P, T, D])
        sq = sb("sq", [P, T, D])
        stat = sb("stat", [P, 2, 4, T])
        xs = sb("xs", [P, 2, T, D])
        xn_t = sb("xn_t", [P, 2, T, D])
        hn = sb("hn", [P, T, D])
        h_t = sb("h_t", [P, 2, T, D])
        xT_t = sb("xT_t", [P, 2, L])
        hT_t = sb("hT_t", [P, 2, TAPS - 1 + L])
        K = R["aslot"].shape[1]
        got = R["bw1"][:].rearrange("p e f -> p (e f)")[:, 0:2 * T * K * D].rearrange("p (u r d) -> p u r d", u=2, d=D)
        arrived, taken = [sem(f"arrived{u}") for u in range(2)], sem("taken")
        xn_out, xT_out = [sem(f"xn_out{u}") for u in range(2)], [sem(f"xT_out{u}") for u in range(2)]
        p_T = own.enter_context(nc.psum_tensor("m_p_T", [P, 2, L], F32))
        p_g = own.enter_context(nc.psum_tensor("m_p_g", [P, T, E], F32))
        p_c = own.enter_context(nc.psum_tensor("m_p_c", [P, 4, L], F32))
        w_in, r_turned, r_kept, wtap_set, set_up = sem("w_in"), sem("r_turned"), sem("r_kept"), sem("wtap_set"), sem("set_up")
        chain, var_done, rstd_done, xn_done, hn_done, h_ready = (
            sem("chain"), sem("var_done"), sem("rstd_done"), sem("xn_done"), sem("hn_done"), sem("h_ready"))
        x_turned, xT_kept, h_turned, hT_kept, g_done, g_kept, c_done, c_kept, summed = (
            sem("x_turned"), sem("xT_kept"), sem("h_turned"), sem("hT_kept"), sem("g_done"), sem("g_kept"), sem("c_done"), sem("c_kept"), sem("summed"))
        block = own.enter_context(nc.Block())
        LOADS = 16 * (6 + NC)

        @block.sync
        def _(sp):
            sp.dma_start(inw[:], A["in_proj_w"]).then_inc(w_in, 16)
            sp.dma_start(taps[:], A["conv_w"].partition_broadcast(P)).then_inc(w_in, 16)
            for c in range(NC):
                sp.dma_start(convb[:, c:c + 1], A["conv_b"][c * P:(c + 1) * P].unsqueeze(1)).then_inc(w_in, 16)
            sp.dma_start(rrows[:], A["w_router"]).then_inc(w_in, 16)
            sp.dma_start(nw[:, 0], A["norm_w"].partition_broadcast(P)).then_inc(w_in, 16)
            sp.dma_start(nw[:, 1], A["norm_b"].partition_broadcast(P)).then_inc(w_in, 16)
            sp.dma_start(R["A_log"][:], A["A_log"].rearrange("(c p) n -> p c n", p=P)).then_inc(w_in, 16)

            def copy_xn(b, u):
                sp.wait_ge(xn_done, b + 1)
                sp.dma_start(R["xn"][:, bass.ds(b * T, T), :], xn_t[:, u]).then_inc(xn_out[u], 16)
                sp.wait_ge(xT_kept, b + 1)
                sp.dma_start(R["xnT"][:, bass.ds(b * L, L)], xT_t[:, u]).then_inc(xT_out[u], 16)

            with sp.Fori(0, B // 2) as i:
                for u in range(2):
                    copy_xn(i * 2 + u, u)
            load_shared_gated(sp, A, R, R["shared_in"])
            for u in range(2):
                sp.wait_ge(xn_out[u], 16 * (B // 2))
                sp.wait_ge(xT_out[u], 16 * (B // 2))

        @block.gpsimd
        def _(pool):
            nc.gpsimd.memset(minus_half[:], -0.5).then_inc(set_up, 1)
            nc.gpsimd.memset(hT_t[:, :, 0:TAPS - 1], 0.0).then_inc(set_up, 1)
            pool.wait_ge(set_up, 2)
            for b in range(2):
                gather_rows(nc, R, "a", R["aslot"], b, got[:, b], arrived[b], range(T * K))
            for b in range(B):
                u = b % 2

                def gather(lo, hi):
                    if b + 2 < B:
                        gather_rows(nc, R, "a", R["aslot"], b + 2, got[:, u], arrived[u], range(lo, hi))

                pool.wait_ge(taken, b + 1)
                gather(0, 3)
                pool.wait_ge(var_done, b * 2 + 1)
                nc.gpsimd.tensor_tensor(stat[:, 0, 3], stat[:, 0, 1], minus_half[:], ALU.pow).then_inc(rstd_done, 1)
                gather(3, 7)
                pool.wait_ge(var_done, b * 2 + 2)
                nc.gpsimd.tensor_tensor(stat[:, 1, 3], stat[:, 1, 1], minus_half[:], ALU.pow).then_inc(rstd_done, 1)
                gather(7, T * K)

        @block.vector
        def _(dve):
            dve.wait_ge(w_in, LOADS)
            for k in range(TAPS):
                nc.vector.tensor_tensor(wtap[:, k], inw[:, 0:DI], taps[:, :, k], ALU.mult).then_inc(wtap_set, 1)
            dve.wait_ge(r_turned, 1)
            nc.vector.tensor_copy(rT[:], p_g[:].rearrange("p t e -> p (t e)")[:, 0:E]).then_inc(r_kept, 1)
            STEPS = 11 + (K - 1) * T

            def add_experts(b, u, i, k, steps, first=False):
                if k == 0:
                    dve.wait_ge(arrived[u], i * (16 * K * T) + 16 * K * T)
                    if not first:
                        dve.wait_ge(summed, b - 1)
                for t in range(T):
                    last = nc.vector.scalar_tensor_tensor(
                        out=xs[:, u, t], in0=got[:, u, t * K + k], scalar=R["agate"][:, k, bass.ds(b * T + t, 1)],
                        in1=R["acc"][:, bass.ds(b * T + t, 1), :] if k == 0 else xs[:, u, t], op0=ALU.mult, op1=ALU.add)
                    if k < K - 1:
                        steps.add(last)
                if k == K - 1:
                    last.then_inc(taken, 1)

            def keep_logits(b):
                dve.wait_ge(g_done, b + 1)
                nc.vector.tensor_copy(R["logits2"][:, bass.ds(b * T, T), :], p_g[:]).then_inc(g_kept, 1)

            def batch(i, u, first, more=True):
                b = i * 2 + u
                steps = Chain(dve, chain, b * STEPS + (K - 1) * T)
                following = (b + 1, 1 - u, i + u)

                def rstd(n):
                    def between():
                        if more:
                            add_experts(*following, n - 1, steps, first and u == 0)
                        dve.wait_ge(rstd_done, b * 2 + n)
                    return between

                dve.wait_ge(taken, b + 1)
                if not first:
                    dve.wait_ge(xn_out[u], i * 16)
                norm_chain(nc, var_done, steps, xs[:, u], xc[:], sq[:], stat[:, 0], xn_t[:, u], xn_done, rstd(1))
                if not (first and u == 0):
                    keep_logits(b - 1)
                dve.wait_ge(xn_done, b + 1)
                nc.vector.tensor_tensor(R["acc"][:, bass.ds(b * T, T), :], xs[:, u], xn_t[:, u], ALU.add).then_inc(summed, 1)
                norm_chain(nc, var_done, steps, xn_t[:, u], xc[:], sq[:], stat[:, 1], hn[:], hn_done, rstd(2))
                dve.wait_ge(hn_done, b + 1)
                steps.add(nc.vector.tensor_tensor(hn[:], hn[:], nw[:, 0].unsqueeze(1).to_broadcast([P, T, D]), ALU.mult))
                steps.settle()
                nc.vector.tensor_tensor(h_t[:, u], hn[:], nw[:, 1].unsqueeze(1).to_broadcast([P, T, D]), ALU.add).then_inc(h_ready, 1)
                if more:
                    add_experts(*following, K - 1, steps)
                    assert steps.n == STEPS, steps.n

            steps = Chain(dve, chain)
            for k in range(K):
                add_experts(0, 0, 0, k, steps, True)
                if k < K - 1:
                    steps.settle()
            for u in range(2):
                batch(0, u, True)
            with dve.Fori(1, B // 2 - 1) as i:
                for u in range(2):
                    batch(i, u, False)
            batch(B // 2 - 1, 0, False)
            batch(B // 2 - 1, 1, False, more=False)
            keep_logits(B - 1)

        @block.tensor
        def _(pe):
            pe.wait_ge(w_in, LOADS)
            nc.tensor.transpose(p_g[:].rearrange("p t e -> p (t e)")[:, 0:E], rrows[:], R["ident"][0:E, 0:E]).then_inc(r_turned, 1)
            pe.wait_ge(r_kept, 1)
            pe.wait_ge(wtap_set, TAPS)
            pe.wait_ge(set_up, 2)

            def batch(b, u, first):
                pe.wait_ge(xn_done, b + 1)
                if not first:
                    pe.wait_ge(xT_kept, b)
                for t in range(T):
                    last = nc.tensor.transpose(p_T[:, 0, t * P:(t + 1) * P], xn_t[:, u, t], R["ident"][:])
                last.then_inc(x_turned, 1)
                pe.wait_ge(h_ready, b + 1)
                if not first:
                    pe.wait_ge(hT_kept, b)
                for t in range(T):
                    last = nc.tensor.transpose(p_T[:, 1, t * P:(t + 1) * P], h_t[:, u, t], R["ident"][:])
                last.then_inc(h_turned, 1)
                pe.wait_ge(xT_kept, b + 1)
                if not first:
                    pe.wait_ge(g_kept, b)
                for t in range(T):
                    last = nc.tensor.matmul(p_g[:, t], xT_t[:, u, t * P:(t + 1) * P], rT[:], start=True, stop=True)
                last.then_inc(g_done, 1)
                pe.wait_ge(hT_kept, b + 1)
                for c in range(4):
                    if not first:
                        pe.wait_ge(c_kept, b * 4 + c - 3)
                    if c < NC:
                        for k in range(TAPS):
                            last = nc.tensor.matmul(p_c[:, c], wtap[:, k, c * P:(c + 1) * P], hT_t[:, u, k:k + L],
                                                    start=k == 0, stop=k == TAPS - 1)
                    else:
                        last = nc.tensor.matmul(p_c[:, c], inw[:, c * P:(c + 1) * P], hT_t[:, u, TAPS - 1:],
                                                start=True, stop=True)
                    last.then_inc(c_done, 1)

            batch(0, 0, True)
            batch(1, 1, False)
            with pe.Fori(1, B // 2) as i:
                for u in range(2):
                    batch(i * 2 + u, u, False)

        @block.scalar
        def _(act):
            act.wait_ge(w_in, LOADS)

            def batch(b, u, i, first):
                act.wait_ge(x_turned, b + 1)
                if not first:
                    act.wait_ge(xT_out[u], i * 16)
                    act.wait_ge(g_done, b - 1)
                nc.scalar.activation(xT_t[:, u], p_T[:, 0], ACT.Copy).then_inc(xT_kept, 1)
                act.wait_ge(h_turned, b + 1)
                if not first:
                    act.wait_ge(c_done, b * 4 - 4)
                nc.scalar.activation(hT_t[:, u, TAPS - 1:], p_T[:, 1], ACT.Copy).then_inc(hT_kept, 1)
                for c in range(4):
                    act.wait_ge(c_done, b * 4 + c + 1)
                    if c < NC:
                        nc.scalar.activation(R["u"][:, c, bass.ds(b * L, L)], p_c[:, c], ACT.Silu, bias=convb[:, c:c + 1]).then_inc(c_kept, 1)
                    else:
                        nc.scalar.activation(R["g"][:, c - NC, bass.ds(b * L, L)], p_c[:, c], ACT.Silu).then_inc(c_kept, 1)

            for u in range(2):
                batch(u, u, 0, True)
            with act.Fori(1, B // 2) as i:
                for u in range(2):
                    batch(i * 2 + u, u, i, False)


def step_sizes(nc, A, R):
    with ExitStack() as own:
        def sb(name, shape, dt=F32):
            return own.enter_context(nc.sbuf_tensor("d_" + name, shape, dt))

        def sem(name):
            return nc.alloc_semaphore("d_" + name)

        BC = 2 * NS
        xpw = sb("xpw", [P, NC, DR + BC])
        bcw = sb("bcw", [P, NC, 3, BC])
        dtw = sb("dtw", [P, DI])
        dtb = sb("dtb", [P, NC])
        dr = sb("dr", [P, L])
        first = sb("first", [3 * BC, L], BF16)
        rest = sb("rest", [3 * BC, L])
        z_abs = sb("z_abs", [P, NC, L])
        z_exp = sb("z_exp", [P, NC, L])
        z_pos = sb("z_pos", [P, 2, NC, L])
        z_ln = sb("z_ln", [P, 2, NC, L])
        p_dr = own.enter_context(nc.psum_tensor("d_p_dr", [P, L], F32))
        p_bc = own.enter_context(nc.psum_tensor("d_p_bc", [3 * BC, L], F32))
        p_z = own.enter_context(nc.psum_tensor("d_p_z", [P, NC, L], F32))
        w_in, bcw_set, a_exp, dr_done, dr_kept, bc_done, z_done, z_read, z_chain, ln_done, d_done = (
            sem(n) for n in ("w_in", "bcw_set", "a_exp", "dr_done", "dr_kept", "bc_done", "z_done", "z_read", "z_chain", "ln_done", "d_done"))
        split, later_in, pos_done = sem("split"), sem("later_in"), sem("pos_done")
        got = sb("got", [P, 2, T, D])
        arrived, taken = [sem(f"arrived{u}") for u in range(2)], sem("taken")
        block = own.enter_context(nc.Block())
        LOADS = 16 * (2 + NC)

        @block.sync
        def _(sp):
            sp.dma_start(xpw[:], A["x_proj_w"].rearrange("(c p) n -> p c n", p=P)).then_inc(w_in, 16)
            sp.dma_start(dtw[:], A["dt_proj_w"]).then_inc(w_in, 16)
            for c in range(NC):
                sp.dma_start(dtb[:, c:c + 1], A["dt_proj_b"][c * P:(c + 1) * P].unsqueeze(1)).then_inc(w_in, 16)
            sp.dma_start(R["opw"][:], A["out_proj_w"].rearrange("(c p) d -> p c d", p=P)).then_inc(later_in, 16)
            for c in range(NC):
                sp.dma_start(R["dpar"][:, c:c + 1], A["D_param"][c * P:(c + 1) * P].unsqueeze(1)).then_inc(later_in, 16)
            sp.wait_ge(later_in, 16 * (1 + NC))

        @block.gpsimd
        def _(pool):
            pool.wait_ge(w_in, LOADS)
            nc.gpsimd.tensor_copy(bcw[:], xpw[:, :, DR:].unsqueeze(2).to_broadcast([P, NC, 3, BC])).then_inc(bcw_set, 1)
            for b in range(2):
                gather_rows(nc, R, "b", R["bslot"], b, got[:, b], arrived[b], range(T))
            for b in range(B):
                pool.wait_ge(ln_done, b + 1)
                pool.wait_ge(pos_done, b + 1)
                nc.gpsimd.tensor_tensor(R["delta"][:, :, b * L:(b + 1) * L], z_pos[:, b % 2], z_ln[:, b % 2], ALU.add).then_inc(d_done, 1)
                if b + 2 < B:
                    pool.wait_ge(taken, b + 1)
                    gather_rows(nc, R, "b", R["bslot"], b + 2, got[:, b % 2], arrived[b % 2], range(T))

        @block.tensor
        def _(pe):
            pe.wait_ge(w_in, LOADS)
            pe.wait_ge(bcw_set, 1)

            def batch(b, is_first):
                tok = bass.ds(b * L, L)
                if not is_first:
                    pe.wait_ge(dr_kept, b)
                for c in range(NC):
                    last = nc.tensor.matmul(p_dr[:], xpw[:, c, 0:DR], R["u"][:, c, tok], start=c == 0, stop=c == NC - 1)
                last.then_inc(dr_done, 1)
                if not is_first:
                    pe.wait_ge(split, b * 4)
                for c in range(NC):
                    last = nc.tensor.matmul(p_bc[:], bcw[:, c].rearrange("p r n -> p (r n)"), R["u"][:, c, tok],
                                            start=c == 0, stop=c == NC - 1)
                last.then_inc(bc_done, 1)
                pe.wait_ge(dr_kept, b + 1)
                if not is_first:
                    pe.wait_ge(pos_done, b)
                for c in range(NC):
                    last = nc.tensor.matmul(p_z[:, c], dtw[:, c * P:(c + 1) * P], dr[:], start=True, stop=True)
                last.then_inc(z_done, 1)

            batch(0, True)
            with pe.Fori(1, B) as b:
                batch(b, False)

        @block.scalar
        def _(act):
            def set_pick(r):
                part = slice(r * BC, (r + 1) * BC)
                nc.scalar.activation(R["pick"][part], R["ident"][part, part].unsqueeze(2).to_broadcast([BC, BC, P]), ACT.Copy)

            set_pick(0)
            act.wait_ge(w_in, LOADS)
            nc.scalar.activation(R["A_neg"][:], R["A_log"][:], ACT.Exp).then_inc(a_exp, 1)

            def batch(b, u, is_first):
                act.wait_ge(z_done, b + 1)
                for c in range(NC):
                    last = nc.scalar.activation(z_abs[:, c], p_z[:, c], ACT.Abs, bias=dtb[:, c:c + 1])
                last.then_inc(z_read, 1)
                act.wait_ge(z_read, b + 1)
                nc.scalar.activation(z_exp[:], z_abs[:], ACT.Exp, scale=-1.0).then_inc(z_chain, 1)
                act.wait_ge(z_chain, b + 1)
                if not is_first:
                    act.wait_ge(d_done, b - 1)
                nc.scalar.activation(z_ln[:, u], z_exp[:], ACT.Ln, bias=1.0).then_inc(ln_done, 1)

            batch(0, 0, True)
            set_pick(1)
            batch(1, 1, True)
            set_pick(2)
            with act.Fori(1, B // 2) as i:
                for u in range(2):
                    batch(i * 2 + u, u, False)

        @block.vector
        def _(dve):
            dve.wait_ge(a_exp, 1)
            nc.vector.tensor_scalar(R["A_neg"][:], R["A_neg"][:], -1.0, None, ALU.mult)

            def batch(b, u, is_first):
                tok = bass.ds(b * L, L)
                dve.wait_ge(dr_done, b + 1)
                if not (is_first and u == 0):
                    dve.wait_ge(z_done, b)
                nc.vector.tensor_copy(dr[:], p_dr[:]).then_inc(dr_kept, 1)
                dve.wait_ge(bc_done, b + 1)
                nc.vector.tensor_copy(first[:], p_bc[:]).then_inc(split, 1)
                dve.wait_ge(split, b * 4 + 1)
                nc.vector.tensor_tensor(rest[:], p_bc[:], first[:], ALU.subtract).then_inc(split, 1)
                nc.vector.tensor_copy(R["bc"][0:BC, tok], first[0:BC])
                dve.wait_ge(split, b * 4 + 2)
                nc.vector.tensor_copy(first[BC:2 * BC], rest[BC:2 * BC])
                nc.vector.tensor_copy(first[2 * BC:], rest[2 * BC:]).then_inc(split, 1)
                dve.wait_ge(split, b * 4 + 3)
                nc.vector.tensor_copy(R["bc"][BC:2 * BC, tok], first[BC:2 * BC])
                nc.vector.tensor_tensor(R["bc"][2 * BC:, tok], rest[2 * BC:], first[2 * BC:], ALU.subtract).then_inc(split, 1)
                dve.wait_ge(z_read, b + 1)
                if not is_first:
                    dve.wait_ge(d_done, b - 1)
                for c in range(NC):
                    last = nc.vector.tensor_scalar(z_pos[:, u, c], p_z[:, c], dtb[:, c:c + 1], 0.0, ALU.add, ALU.max)
                last.then_inc(pos_done, 1)

            def add_experts(i, u):
                dve.wait_ge(arrived[u], i * (16 * T) + 16 * T)
                rows = R["acc"][:, bass.ds((i * 2 + u) * T, T), :]
                nc.vector.tensor_tensor(rows, rows, got[:, u], ALU.add).then_inc(taken, 1)

            batch(0, 0, True)
            add_experts(0, 0)
            batch(1, 1, True)
            add_experts(0, 1)
            with dve.Fori(1, B // 2) as i:
                for u in range(2):
                    batch(i * 2 + u, u, False)
                    add_experts(i, u)


def state_space(nc, R):
    with ExitStack() as own:
        def sb(name, shape, dt=F32):
            return own.enter_context(nc.sbuf_tensor("y_" + name, shape, dt))

        def sem(name):
            return nc.alloc_semaphore("y_" + name)

        pick = R["pick"]
        opw, dpar = R["opw"], R["dpar"]
        dl = sb("dl", [P, 2, NC, L])
        du = sb("du", [P, 2, NC, L])
        bs = sb("bs", [P, 2, L])
        da = sb("da", [P, 2, NC, L])
        dbu = sb("dbu", [P, 2, NC, L])
        h = sb("h", [P, 2, NC, L])
        hc = sb("hc", [P, 2, NC, L])
        yz = sb("yz", [P, 2, NC, L])
        p_b = own.enter_context(nc.psum_tensor("y_p_b", [P, 2, L], F32))
        p_c = own.enter_context(nc.psum_tensor("y_p_c", [P, 2, L], F32))
        p_y = own.enter_context(nc.psum_tensor("y_p_y", [P, NC, L], F32))
        p_o = own.enter_context(nc.psum_tensor("y_p_o", [P, T, D], F32))
        (du_done, b_done, c_done, b_kept, da_done, dbu_done, dbu_dve, h_done, hc_done, y_sum, yu, yz_done, o_done, o_added) = (
            sem(n) for n in ("du_done", "b_done", "c_done", "b_kept", "da_done", "dbu_done", "dbu_dve", "h_done",
                             "hc_done", "y_sum", "yu", "yz_done", "o_done", "o_added"))
        dl_done = sem("dl_done")
        block = own.enter_context(nc.Block())

        def on_pool(n, c):
            return (n, c) != (NS - 1, 1)

        N_POOL = sum(on_pool(n, c) for n in range(NS) for c in range(NC))
        N_DVE = NS * NC - N_POOL

        def pool_count(n, c):
            return sum(on_pool(m, d) for m in range(NS) for d in range(NC) if (m, d) <= (n, c))

        def pool_before(n):
            return pool_count(n, NC - 1) if n >= 0 else pool_count(NS + n, NC - 1) - N_POOL

        def dve_count(n, c):
            return n * NC + c + 1 - pool_count(n, c)

        @block.gpsimd
        def _(pool):
            def batch(b, u, first):
                pool.wait_ge(du_done, b + 1)
                for n in range(NS):
                    pool.wait_ge(b_kept, b * NS + n + 1)
                    for c in range(NC):
                        if on_pool(n, c):
                            if not (first and n < 2):
                                pool.wait_ge(h_done, b * NS * NC + (n - 2) * NC + c + 1)
                            nc.gpsimd.tensor_tensor(dbu[:, n % 2, c], du[:, u, c], bs[:, n % 2], ALU.mult).then_inc(dbu_done, 1)

            batch(0, 0, True)
            batch(1, 1, False)
            with pool.Fori(1, B // 2) as i:
                for u in range(2):
                    batch(i * 2 + u, u, False)

        @block.tensor
        def _(pe):
            def spread_b(b, n, first):
                if not (first and n < 2):
                    pe.wait_ge(b_kept, b * NS + n - 1)
                    if n == 1:
                        pe.wait_ge(dbu_dve, b * N_DVE)
                nc.tensor.matmul(p_b[:, n % 2], pick[:, n], R["bc"][:, bass.ds(b * L, L)], start=True, stop=True).then_inc(b_done, 1)

            def spread_c(b, n, first):
                if not (first and n < 2):
                    pe.wait_ge(hc_done, (b * NS + n - 1) * NC)
                nc.tensor.matmul(p_c[:, n % 2], pick[:, NS + n], R["bc"][:, bass.ds(b * L, L)], start=True, stop=True).then_inc(c_done, 1)

            def gather(b, n, first):
                for c in range(NC):
                    pe.wait_ge(hc_done, (b * NS + n) * NC + c + 1)
                    if n == 0 and not first:
                        pe.wait_ge(yu, (b - 1) * NC + c + 1)
                    nc.tensor.matmul(p_y[:, c], R["ident"][:], hc[:, n % 2, c], start=n == 0, stop=n == NS - 1).then_inc(y_sum, 1)

            def project(b, u, first):
                pe.wait_ge(yz_done, b * NC + NC)
                if not first:
                    pe.wait_ge(o_added, b)
                for t in range(T):
                    for c in range(NC):
                        last = nc.tensor.matmul(p_o[:, t], yz[:, u, c, t * P:(t + 1) * P], opw[:, c], start=c == 0, stop=c == NC - 1)
                last.then_inc(o_done, 1)

            def batch(b, u, first, before=True, after=True):
                for n in range(NS):
                    if n + 1 < NS:
                        spread_b(b, n + 1, first)
                    elif after:
                        spread_b(b + 1, 0, False)
                    spread_c(b, n, first)
                    if n >= 2:
                        gather(b, n - 2, first)
                    elif before:
                        gather(b - 1, NS - 2 + n, False)
                    if n == 5 and before:
                        project(b - 1, 1 - u, isinstance(b, int) and b == 1)

            spread_b(0, 0, True)
            batch(0, 0, True, before=False)
            batch(1, 1, False)
            with pe.Fori(1, B // 2 - 1) as i:
                for u in range(2):
                    batch(i * 2 + u, u, False)
            batch(B - 2, 0, False)
            batch(B - 1, 1, False, after=False)
            gather(B - 1, NS - 2, False)
            gather(B - 1, NS - 1, False)
            project(B - 1, 1, False)

        @block.scalar
        def _(act):
            def step(b, u):
                nc.scalar.activation(dl[:, u], R["delta"][:, :, bass.ds(b * L, L)], ACT.Copy).then_inc(dl_done, 1)

            def batch(b, u, first, after=True):
                for n in range(NS):
                    act.wait_ge(b_done, b * NS + n + 1)
                    if not (first and n < 2):
                        act.wait_ge(dbu_done, b * N_POOL + pool_before(n - 2))
                    nc.scalar.activation(bs[:, n % 2], p_b[:, n % 2], ACT.Copy).then_inc(b_kept, 1)
                    if n == 0:
                        act.wait_ge(dl_done, b + 1)
                    for c in range(NC):
                        if not (first and n < 2):
                            act.wait_ge(h_done, b * NS * NC + (n - 2) * NC + c + 1)
                        nc.scalar.activation(da[:, n % 2, c], dl[:, u, c], ACT.Exp,
                                             scale=R["A_neg"][:, c, n:n + 1]).then_inc(da_done, 1)
                    if n == 8 and after:
                        if not first:
                            act.wait_ge(da_done, b * NS * NC)
                        step(b + 1, 1 - u)

            step(0, 0)
            batch(0, 0, True)
            batch(1, 1, False)
            with act.Fori(1, B // 2 - 1) as i:
                for u in range(2):
                    batch(i * 2 + u, u, False)
            batch(B - 2, 0, False)
            batch(B - 1, 1, False, after=False)

        @block.vector
        def _(dve):
            def step_times_u(b, u, first):
                tok = bass.ds(b * L, L)
                if not first:
                    dve.wait_ge(dbu_done, (b - 1) * N_POOL)
                nc.vector.tensor_tensor(du[:, u], R["delta"][:, :, tok], R["u"][:, :, tok], ALU.mult).then_inc(du_done, 1)

            def scan(b, u, n, first):
                for c in range(NC):
                    at = (b * NS + n) * NC + c
                    if on_pool(n, c):
                        dve.wait_ge(dbu_done, b * N_POOL + pool_count(n, c))
                    else:
                        dve.wait_ge(b_done, b * NS + n + 1)
                        dve.wait_ge(du_done, b + 1)
                        nc.vector.tensor_tensor(dbu[:, n % 2, c], du[:, u, c], p_b[:, n % 2], ALU.mult).then_inc(dbu_dve, 1)
                        dve.wait_ge(dbu_dve, b * N_DVE + dve_count(n, c))
                    if not (first and n < 2):
                        dve.wait_ge(hc_done, at - 2 * NC + 1)
                    dve.wait_ge(da_done, at + 1)
                    nc.vector.tensor_tensor_scan(h[:, n % 2, c], da[:, n % 2, c], dbu[:, n % 2, c], 0.0,
                                                 ALU.mult, ALU.add).then_inc(h_done, 1)

            def times_c(b, n, first):
                for c in range(NC):
                    at = (b * NS + n) * NC + c
                    dve.wait_ge(c_done, b * NS + n + 1)
                    dve.wait_ge(h_done, at + 1)
                    if not (first and n < 2):
                        dve.wait_ge(y_sum, at - 2 * NC + 1)
                    nc.vector.tensor_tensor(hc[:, n % 2, c], h[:, n % 2, c], p_c[:, n % 2], ALU.mult).then_inc(hc_done, 1)

            def gate(b, u):
                tok = bass.ds(b * L, L)
                for c in range(NC):
                    dve.wait_ge(y_sum, (b * NS + NS - 1) * NC + c + 1)
                    nc.vector.scalar_tensor_tensor(out=yz[:, u, c], in0=R["u"][:, c, tok], scalar=dpar[:, c:c + 1],
                                                   in1=p_y[:, c], op0=ALU.mult, op1=ALU.add).then_inc(yu, 1)
                for c in range(NC):
                    dve.wait_ge(yu, b * NC + c + 1)
                    nc.vector.tensor_tensor(yz[:, u, c], yz[:, u, c], R["g"][:, c, tok], ALU.mult).then_inc(yz_done, 1)

            def add_out(b):
                rows = R["acc"][:, bass.ds(b * T, T), :]
                dve.wait_ge(o_done, b + 1)
                nc.vector.tensor_tensor(rows, rows, p_o[:], ALU.add).then_inc(o_added, 1)

            def batch(b, u, first, before=True, after=True):
                for n in range(NS):
                    if n == 2 and before:
                        gate(b - 1, 1 - u)
                    scan(b, u, n, first)
                    if n > 0:
                        times_c(b, n - 1, first)
                    elif before:
                        times_c(b - 1, NS - 1, False)
                    if n == 8 and before:
                        add_out(b - 1)
                    if n == 10 and after:
                        step_times_u(b + 1, 1 - u, first)

            step_times_u(0, 0, True)
            batch(0, 0, True, before=False)
            batch(1, 1, False)
            with dve.Fori(1, B // 2 - 1) as i:
                for u in range(2):
                    batch(i * 2 + u, u, False)
            batch(B - 2, 0, False)
            batch(B - 1, 1, False, after=False)
            times_c(B - 1, NS - 1, False)
            gate(B - 1, 1)
            add_out(B - 1)


def shared_raw(A, R):
    CF = A["w_gate"].shape[0] // P
    return R["bw2"][:].rearrange("p e d -> p (e d)")[:, 0:3 * CF * P].rearrange("p (m c q) -> p m c q", m=3, c=CF)


def load_shared_gated(sp, A, R, w_in):
    raw = shared_raw(A, R)
    sp.dma_start(raw[:, 0], A["w_gate"].rearrange("(c p) d -> p c d", p=P)).then_inc(w_in, 16)
    sp.dma_start(raw[:, 1], A["w_up"].rearrange("(c p) d -> p c d", p=P)).then_inc(w_in, 16)
    sp.dma_start(raw[:, 2], A["w_down"].rearrange("d (c p) -> d c p", p=P)).then_inc(w_in, 16)


class SharedGated:

    def __init__(self, nc, own, A, R):
        def sb(name, shape):
            return own.enter_context(nc.sbuf_tensor("v_" + name, shape, F32))

        def ps(name, shape):
            return own.enter_context(nc.psum_tensor("v_" + name, shape, F32))

        self.nc, self.A, self.R, self.CF = nc, A, R, A["w_gate"].shape[0] // P
        CF = self.CF
        self.score = sb("score", [P, NT])
        self.raw = shared_raw(A, R)
        self.wT = sb("wT", [P, 3, CF, P])
        self.sil = sb("sil", [P, CF, L])
        self.hid = sb("hid", [P, 2, CF, L])
        self.p_h = ps("p_h", [P, 2, CF, L])
        self.p_o = ps("p_o", [P, 2, T, D])
        self.p_w = self.p_o[:, 0].rearrange("p t d -> p (t d)")[:, 0:CF * P].rearrange("p (c q) -> p c q", c=CF)
        (self.w_turned, self.w_kept, self.gate_done, self.up_done, self.sil_done, self.hid_done, self.o_done,
         self.o_added, self.scored, self.scaled, self.scattered, self.loaded) = (
            nc.alloc_semaphore("v_" + n) for n in ("w_turned", "w_kept", "gate_done", "up_done", "sil_done", "hid_done", "o_done",
                                                   "o_added", "scored", "scaled", "scattered", "loaded"))

    def load_weights(self, sp):
        load_first(sp, self.R, "b", self.A["gate_up"], self.loaded)
        sp.wait_ge(self.w_turned, 3)
        loads = 1 + load_second(sp, self.R, "b", self.A["down"], self.loaded)
        sp.wait_ge(self.loaded, 16 * loads)

    def scatter(self, pool):
        for n, tiles in enumerate((range(T), range(T, NT))):
            pool.wait_ge(self.scaled, n + 1)
            scatter_rows(self.nc, self.R, "b", self.R["bslot"], tiles, self.scattered)
        pool.wait_ge(self.scattered, 16 * NT)

    def turn_weights(self, pe):
        pe.wait_ge(self.R["shared_in"], 48)
        for m in range(3):
            if m > 0:
                pe.wait_ge(self.w_kept, m)
            for c in range(self.CF):
                last = self.nc.tensor.transpose(self.p_w[:, c], self.raw[:, m, c], self.R["ident"][:])
            last.then_inc(self.w_turned, 1)
        pe.wait_ge(self.w_kept, 3)

    def hidden(self, pe, b, first):
        tok = bass.ds(b * L, L)
        for m, done, read in ((0, self.gate_done, self.sil_done), (1, self.up_done, self.hid_done)):
            if not first:
                pe.wait_ge(read, b)
            for c in range(self.CF):
                last = self.nc.tensor.matmul(self.p_h[:, m, c], self.wT[:, m, c], self.R["xnT"][:, tok], start=True, stop=True)
            last.then_inc(done, 1)

    def output(self, pe, b, u, first):
        pe.wait_ge(self.hid_done, b + 1)
        if not first:
            pe.wait_ge(self.o_added, b - 1)
        for t in range(T):
            for c in range(self.CF):
                last = self.nc.tensor.matmul(self.p_o[:, u, t], self.hid[:, u, c, t * P:(t + 1) * P], self.wT[:, 2, c],
                                             start=c == 0, stop=c == self.CF - 1)
        last.then_inc(self.o_done, 1)

    def act(self, act, best):
        nc, R = self.nc, self.R

        def batch(b, first):
            act.wait_ge(self.gate_done, b + 1)
            if not first:
                act.wait_ge(self.hid_done, b)
            nc.scalar.activation(self.sil[:], self.p_h[:, 0], ACT.Silu).then_inc(self.sil_done, 1)

        batch(0, True)
        batch(1, False)
        act.wait_ge(best, 1)
        nc.scalar.activation(self.score[:], R["bgate"][:, 0], ACT.Sigmoid).then_inc(self.scored, 1)
        batch(2, False)
        with act.Fori(3, B) as b:
            batch(b, False)

    def keep_weights(self, dve):
        for m in range(3):
            dve.wait_ge(self.w_turned, m + 1)
            self.nc.vector.tensor_copy(self.wT[:, m], self.p_w).then_inc(self.w_kept, 1)

    def scale(self, dve):
        dve.wait_ge(self.scored, 1)
        for part in (slice(0, T), slice(T, NT)):
            xn, score = self.R["xn"][:, part], self.score[:, part]
            self.nc.vector.tensor_tensor(xn, xn, score.unsqueeze(2).to_broadcast(xn.shape), ALU.mult).then_inc(self.scaled, 1)

    def hide(self, dve, b, u, first):
        dve.wait_ge(self.up_done, b + 1)
        dve.wait_ge(self.sil_done, b + 1)
        if not first:
            dve.wait_ge(self.o_done, b - 1)
        self.nc.vector.tensor_tensor(self.hid[:, u], self.sil[:], self.p_h[:, 1], ALU.mult).then_inc(self.hid_done, 1)

    def add_out(self, dve, b, u):
        dve.wait_ge(self.o_done, b + 1)
        rows = self.R["acc"][:, bass.ds(b * T, T), :]
        self.nc.vector.tensor_tensor(rows, rows, self.p_o[:, u], ALU.add).then_inc(self.o_added, 1)

    def later_batches(self, dve):
        with dve.Fori(2, B // 2) as i:
            for u in range(2):
                self.hide(dve, i * 2 + u, u, False)
                self.add_out(dve, i * 2 + u - 1, 1 - u)
        self.add_out(dve, B - 1, 1)


def store_acc(nc, R, out):
    with ExitStack() as own:
        stored = nc.alloc_semaphore("stored")
        block = own.enter_context(nc.Block())

        @block.sync
        def _(sp):
            sp.dma_start(out.rearrange("b (t p) d -> p (b t) d", p=P), R["acc"][:]).then_inc(stored, 16)
            sp.wait_ge(stored, 16)


@contextmanager
def signals_of_a_part(nc):
    before = nc.snapshot_sems()
    yield
    nc.clear_and_free_semaphores(nc.allocated_since(before))
    nc.all_engine_barrier()


def two_layers(nc, A, out):
    E0, K0, E1 = A["gW"].shape[1], 3, A["w_router"].shape[0]
    tiles0, tiles1 = whole(most_tiles(K0 * B * L, E0)), whole(most_tiles(B * L, E1))
    CF0, CS = A["rb1"].shape[1] // P, A["sb1"].shape[1] // P

    def dram(name, shape, dt=F32):
        return nc.dram_tensor(name, shape, dt).ap()

    with ExitStack() as ctx:
        R = {}

        def keep(scope, name, shape, dt=F32, tag="sb"):
            R[name] = scope.enter_context(nc.sbuf_tensor(name + "_" + tag, shape, dt))

        keep(ctx, "ident", [P, P])
        keep(ctx, "identb", [P, P], BF16)
        keep(ctx, "acc", [P, NT, D])
        for tag, E, K, tiles in (("a", E0, K0, tiles0), ("b", E1, 1, tiles1)):
            keep(ctx, tag + "gate", [P, K, NT])
            keep(ctx, tag + "slot", [P, K, NT], I32)
            keep(ctx, tag + "chosen", [P, NT, E])
            keep(ctx, tag + "owner", [P, tiles], I32)
            R[tag + "table"] = dram(tag + "_table", [tiles * P, D])
            R[tag + "answers"] = dram(tag + "_answers", [tiles * P, D])
        R["q_dram"], R["k_dram"] = dram("q_parts", [B, 3, P, L], BF16), dram("k_parts", [B, 3, P, L], BF16)
        R["at_dram"], R["nm_dram"] = dram("heads_out", [2, L * D]), dram("max_rows", [2, 3 * HH, L], BF16)

        with ExitStack() as first, signals_of_a_part(nc):
            keep(first, "xn", [P, NT, D])
            keep(first, "aw1", [P, E0, CF0 * P])
            keep(first, "aw2", [P, E0 * CF0, D])
            keep(first, "b1T", [P, E0 * CF0 + CS])
            with ExitStack() as heads:
                keep(heads, "v", [P, NT, D])
                keep(heads, "qs", [P, 2, H, L], BF16)
                keep(heads, "ks", [P, 2, H, L], BF16)
                keep(heads, "nmax", [P, T, H])
                R["s_done"], R["max_done"] = nc.alloc_semaphore("s_done"), nc.alloc_semaphore("max_done")
                R["stacked"] = [[nc.alloc_semaphore(f"stacked{u}{h}") for h in range(2)] for u in range(2)]
                with ExitStack() as early:
                    keep(early, "xnT", [P, B * L])
                    keep(early, "logits", [P, NT, E0])
                    keep(early, "weights", [P, NT, E0])
                    keep(early, "gates", [P, NT, QUARTER])
                    keep(early, "b1rows", [E0 * CF0 + CS, P])
                    keep(early, "b2", [P, T, D])
                    keep(early, "sw1", [P, CS * P])
                    keep(early, "sw2", [P, CS, D])
                    R["biases_in"], R["b2_zero"] = nc.alloc_semaphore("biases_in"), nc.alloc_semaphore("b2_zero")
                    norm_and_project(nc, A, R)
                    shared = SharedExpert(nc, early, A, R, E0)
                    route(nc, R, "a", R["weights"][:], E0, K0, tiles0, logits=R["logits"][:], shared=shared)
                attention(nc, A, R)
            expert_tiles(nc, R, "a", tiles0, E0, R["atable"], R["aanswers"], False)
        with ExitStack() as states:
            R["shared_in"] = nc.alloc_semaphore("shared_in")
            keep(states, "opw", [P, NC, D])
            keep(states, "dpar", [P, NC])
            keep(states, "u", [P, NC, B * L])
            keep(states, "g", [P, NC, B * L])
            keep(states, "A_log", [P, NC, NS])
            keep(states, "A_neg", [P, NC, NS])
            with ExitStack() as experts:
                keep(experts, "bw1", [P, E1, A["gate_up"].shape[2]])
                keep(experts, "bw2", [P, E1 * A["down"].shape[1] // P, D])
                with ExitStack() as rows:
                    keep(rows, "xn", [P, NT, D], tag="second")
                    keep(rows, "xnT", [P, B * L], tag="second")
                    keep(rows, "logits2", [P, NT, E1])
                    norm_and_mix(nc, A, R)
                    route(nc, R, "b", R["logits2"][:], E1, 1, tiles1, gated=SharedGated(nc, rows, A, R))
                expert_tiles(nc, R, "b", tiles1, E1, R["btable"], R["banswers"], True)
            keep(states, "delta", [P, NC, B * L])
            keep(states, "bc", [3 * 2 * NS, B * L], BF16)
            keep(states, "pick", [3 * 2 * NS, 2 * NS, P], BF16)
            step_sizes(nc, A, R)
            state_space(nc, R)
        store_acc(nc, R, out)


_INS = {
    "x": "L0_attn_x", "Wqkv": "L0_attn_W_qkv", "bqkv": "L0_attn_b_qkv",
    "sW1": "L0_ffn_sW1", "sb1": "L0_ffn_sb1", "sW2": "L0_ffn_sW2", "sb2": "L0_ffn_sb2",
    "rW1": "L0_ffn_rW1", "rb1": "L0_ffn_rb1", "rW2": "L0_ffn_rW2", "rb2": "L0_ffn_rb2",
    "gW": "L0_ffn_gW", "gb": "L0_ffn_gb",
    "norm_w": "L1_attn_norm_w", "norm_b": "L1_attn_norm_b", "in_proj_w": "L1_attn_in_proj_w",
    "conv_w": "L1_attn_conv_w", "conv_b": "L1_attn_conv_b", "x_proj_w": "L1_attn_x_proj_w",
    "dt_proj_w": "L1_attn_dt_proj_w", "dt_proj_b": "L1_attn_dt_proj_b", "A_log": "L1_attn_A_log",
    "D_param": "L1_attn_D_param", "out_proj_w": "L1_attn_out_proj_w",
    "w_router": "L1_ffn_w_router", "gate_up": "L1_ffn_gate_up_proj", "down": "L1_ffn_down_proj",
    "w_gate": "L1_ffn_w_gate", "w_up": "L1_ffn_w_up", "w_down": "L1_ffn_w_down",
}


def kernel(**inputs):
    import numpy as _np
    import concourse.bacc as _bacc
    from concourse import mybir as _mybir
    from concourse.bass_utils import run_bass_kernel_spmd as _run

    nc = _bacc.Bacc("TRN2", target_bir_lowering=False, num_devices=1)
    arrays, args = {}, {}
    for short, name in _INS.items():
        a = _np.ascontiguousarray(inputs[name])
        arrays[f"in_{name}"] = a
        args[short] = nc.dram_tensor(f"in_{name}", a.shape, _mybir.dt.from_np(a.dtype), kind="ExternalInput").ap()
    out = nc.dram_tensor("out_x", [B, L, D], F32, kind="ExternalOutput").ap()
    two_layers(nc, args, out)
    r = _run(nc, [arrays], core_ids=[0])
    return r.results[0]["out_x"]
```
